# Optimizing a Trainium2 kernel written in Bass

```python
import numpy as np
import jax
import jax.numpy as jnp

def _softmax(x, axis=-1):
    return jax.nn.softmax(x, axis=axis)

def _gelu(x):
    return jax.nn.gelu(x, approximate=True)

def _silu(x):
    return jax.nn.silu(x)

def _sigmoid(x):
    return jax.nn.sigmoid(x)

def _layernorm(x, axis=-1, eps=1e-05):
    m = jnp.mean(x, axis=axis, keepdims=True)
    v = jnp.var(x, axis=axis, keepdims=True)
    return (x - m) / jnp.sqrt(v + eps)

def _scatter_add(tgt, idx, src, axis=0):
    return tgt.at[idx].add(src)

def _segment_sum(src, seg, n):
    return jax.ops.segment_sum(src, seg, n)
kernel_name = 'mk_decoder_preln_d1_seqx_r4_8a4c88'

def setup_inputs(seed: int=0):
    np.random.seed(seed)
    _w = jnp.asarray

    def _rec_inputs():
        import jax
        import jax.numpy as jnp
        _rk = jax.random.key(seed)
        x = -0.0001661 + 0.9999 * jax.random.normal(jax.random.fold_in(_rk, 1), (4, 1024, 256), jnp.float32)
        _lenS = 1024 - jax.random.randint(jax.random.fold_in(_rk, 7), (4,), 0, max(1, 1024 // 4) + 1, jnp.int32)
        _lenS2 = 154 - jax.random.randint(jax.random.fold_in(_rk, 8), (4,), 0, max(1, 154 // 4) + 1, jnp.int32)
        _ctx_1024P = jax.random.normal(jax.random.fold_in(_rk, 11), (4, 16, 256), jnp.float32)
        _ctx_1024c = jax.random.dirichlet(jax.random.fold_in(_rk, 511), 0.3 * jnp.ones((16,), jnp.float32), (4, 154))
        _ctx_1024t = jnp.einsum('bsk,bkd->bsd', _ctx_1024c, _ctx_1024P)
        _ctx_1024t = _ctx_1024t * jax.lax.rsqrt(jnp.mean(jnp.square(_ctx_1024t)) + 1e-12) * 0.953939
        ctx_1024 = -0.000119273 + 0.999915 * (_ctx_1024t + 0.3 * jax.random.normal(jax.random.fold_in(_rk, 611), (4, 154, 256), jnp.float32))
        return (x, ctx_1024)
    x, ctx_1024 = _rec_inputs()

    def _L0_attn_setup():
        import jax, jax.numpy as jnp
        import numpy as np
        D_MODEL = 256
        D_STATE = 16
        D_CONV = 4
        EXPAND = 2
        D_INNER = EXPAND * D_MODEL
        BATCH = 2
        SEQLEN = 512

        def _silu(x):
            return x * jax.nn.sigmoid(x)

        def _causal_depthwise_conv(x, w, b):
            K = w.shape[1]
            L = x.shape[1]
            xp = jnp.pad(x, ((0, 0), (K - 1, 0), (0, 0)))
            out = b
            for k in range(K):
                out = out + xp[:, k:k + L, :] * w[:, k]
            return out

        def _selective_scan(u, dt, A, Bm, Cm, D):

            def step(h, xs):
                u_t, dt_t, b_t, c_t = xs
                dA = jnp.exp(dt_t[:, :, None] * A[None])
                h = dA * h + (dt_t * u_t)[:, :, None] * b_t[:, None, :]
                y = jnp.einsum('bds,bs->bd', h, c_t) + D * u_t
                return (h, y)
            h0 = jnp.zeros((u.shape[0],) + A.shape, u.dtype)
            xs = (u.swapaxes(0, 1), dt.swapaxes(0, 1), Bm.swapaxes(0, 1), Cm.swapaxes(0, 1))
            _, ys = jax.lax.scan(step, h0, xs)
            return ys.swapaxes(0, 1)
        key = jax.random.key(seed)
        ks = jax.random.split(key, 8)
        s = 0.02
        return {'x': jax.random.normal(ks[0], (BATCH, SEQLEN, D_MODEL), jnp.float32), 'W_in': jax.random.normal(ks[1], (D_MODEL, 2 * D_INNER), jnp.float32) * s, 'conv_w': jax.random.normal(ks[2], (D_INNER, D_CONV), jnp.float32) * s, 'conv_b': jnp.zeros((D_INNER,), jnp.float32), 'W_x': jax.random.normal(ks[3], (D_INNER, 2 * D_STATE), jnp.float32) * s, 'W_dt': jax.random.normal(ks[4], (D_INNER, D_INNER), jnp.float32) * s, 'b_dt': jnp.zeros((D_INNER,), jnp.float32), 'A_log': jnp.log(jnp.tile(jnp.arange(1, D_STATE + 1, dtype=jnp.float32), (D_INNER, 1))), 'D': jnp.ones((D_INNER,), jnp.float32), 'W_out': jax.random.normal(ks[5], (D_INNER, D_MODEL), jnp.float32) * s}
    _L0_attn_all = _L0_attn_setup()
    _L0_attn_in = {k: v for k, v in _L0_attn_all.items() if k in ('W_in', 'conv_w', 'conv_b', 'W_x', 'W_dt', 'b_dt', 'A_log', 'D', 'W_out')}
    del _L0_attn_all

    def _L0_xattn_setup():
        import jax, jax.numpy as jnp
        import numpy as np
        B, LQ, LK = (8, 512, 512)
        HIST_DIM, COMB_DIM, FUSION_DIM = (256, 256, 256)

        def _linear_params(key, in_dim, out_dim):
            k1, k2 = jax.random.split(key)
            bound = 1.0 / np.sqrt(in_dim)
            W = jax.random.uniform(k1, (out_dim, in_dim), jnp.float32, -bound, bound)
            b = jax.random.uniform(k2, (out_dim,), jnp.float32, -bound, bound)
            return (W, b)

        def _lin(x, W, b):
            return jnp.einsum('bld,fd->blf', x, W) + b
        key = jax.random.key(seed)
        ks = jax.random.split(key, 8)
        hW, hb = _linear_params(ks[0], HIST_DIM, FUSION_DIM)
        cW, cb = _linear_params(ks[1], COMB_DIM, FUSION_DIM)
        qW, qb = _linear_params(ks[2], FUSION_DIM, FUSION_DIM)
        kW, kb = _linear_params(ks[3], FUSION_DIM, FUSION_DIM)
        vW, vb = _linear_params(ks[4], FUSION_DIM, FUSION_DIM)
        oW, ob = _linear_params(ks[5], FUSION_DIM, FUSION_DIM)
        return {'history_features': jax.random.normal(ks[6], (B, LQ, HIST_DIM), jnp.float32), 'combined_features': jax.random.normal(ks[7], (B, LK, COMB_DIM), jnp.float32), 'hW': hW, 'hb': hb, 'cW': cW, 'cb': cb, 'qW': qW, 'qb': qb, 'kW': kW, 'kb': kb, 'vW': vW, 'vb': vb, 'oW': oW, 'ob': ob}
    _L0_xattn_all = _L0_xattn_setup()
    _L0_xattn_in = {k: v for k, v in _L0_xattn_all.items() if k in ('hW', 'hb', 'cW', 'cb', 'qW', 'qb', 'kW', 'kb', 'vW', 'vb', 'oW', 'ob')}
    del _L0_xattn_all

    def _L0_ffn_setup():
        import jax, jax.numpy as jnp
        import numpy as np
        B, S, H, I, E, K = (4, 512, 256, 256, 8, 2)
        LIMIT = 7.0
        ALPHA = 1.702
        EPS = 1e-05
        key = jax.random.key(seed)
        ks = jax.random.split(key, 5)
        x = jax.random.normal(ks[0], (B, S, H), dtype=jnp.float32)
        norm_weight = jnp.ones((H,), dtype=jnp.float32)
        gate_weight = (jax.random.normal(ks[1], (E, H), dtype=jnp.float32) / np.sqrt(H)).astype(jnp.bfloat16)
        gate_bias = jnp.zeros((E,), dtype=jnp.bfloat16)
        mlp1_weight = (jax.random.normal(ks[2], (E, 2 * I, H), dtype=jnp.float32) / np.sqrt(H)).astype(jnp.bfloat16)
        mlp1_bias = jnp.zeros((E, 2 * I), dtype=jnp.bfloat16)
        mlp2_weight = (jax.random.normal(ks[3], (E, H, I), dtype=jnp.float32) / np.sqrt(I)).astype(jnp.bfloat16)
        mlp2_bias = jnp.zeros((E, H), dtype=jnp.bfloat16)
        return {'x': x, 'norm_weight': norm_weight, 'gate_weight': gate_weight, 'gate_bias': gate_bias, 'mlp1_weight': mlp1_weight, 'mlp1_bias': mlp1_bias, 'mlp2_weight': mlp2_weight, 'mlp2_bias': mlp2_bias}
    _L0_ffn_all = _L0_ffn_setup()
    _L0_ffn_in = {k: v for k, v in _L0_ffn_all.items() if k in ('norm_weight', 'gate_weight', 'gate_bias', 'mlp1_weight', 'mlp1_bias', 'mlp2_weight', 'mlp2_bias')}
    del _L0_ffn_all
    return {'x': x, 'ctx_1024': ctx_1024, 'L0_attn_W_in': _L0_attn_in['W_in'], 'L0_attn_conv_w': _L0_attn_in['conv_w'], 'L0_attn_conv_b': _L0_attn_in['conv_b'], 'L0_attn_W_x': _L0_attn_in['W_x'], 'L0_attn_W_dt': _L0_attn_in['W_dt'], 'L0_attn_b_dt': _L0_attn_in['b_dt'], 'L0_attn_A_log': _L0_attn_in['A_log'], 'L0_attn_D': _L0_attn_in['D'], 'L0_attn_W_out': _L0_attn_in['W_out'], 'L0_xattn_hW': _L0_xattn_in['hW'], 'L0_xattn_hb': _L0_xattn_in['hb'], 'L0_xattn_cW': _L0_xattn_in['cW'], 'L0_xattn_cb': _L0_xattn_in['cb'], 'L0_xattn_qW': _L0_xattn_in['qW'], 'L0_xattn_qb': _L0_xattn_in['qb'], 'L0_xattn_kW': _L0_xattn_in['kW'], 'L0_xattn_kb': _L0_xattn_in['kb'], 'L0_xattn_vW': _L0_xattn_in['vW'], 'L0_xattn_vb': _L0_xattn_in['vb'], 'L0_xattn_oW': _L0_xattn_in['oW'], 'L0_xattn_ob': _L0_xattn_in['ob'], 'L0_ffn_norm_weight': _L0_ffn_in['norm_weight'], 'L0_ffn_gate_weight': _L0_ffn_in['gate_weight'], 'L0_ffn_gate_bias': _L0_ffn_in['gate_bias'], 'L0_ffn_mlp1_weight': _L0_ffn_in['mlp1_weight'], 'L0_ffn_mlp1_bias': _L0_ffn_in['mlp1_bias'], 'L0_ffn_mlp2_weight': _L0_ffn_in['mlp2_weight'], 'L0_ffn_mlp2_bias': _L0_ffn_in['mlp2_bias']}

def reference(x, ctx_1024, L0_attn_W_in, L0_attn_conv_w, L0_attn_conv_b, L0_attn_W_x, L0_attn_W_dt, L0_attn_b_dt, L0_attn_A_log, L0_attn_D, L0_attn_W_out, L0_xattn_hW, L0_xattn_hb, L0_xattn_cW, L0_xattn_cb, L0_xattn_qW, L0_xattn_qb, L0_xattn_kW, L0_xattn_kb, L0_xattn_vW, L0_xattn_vb, L0_xattn_oW, L0_xattn_ob, L0_ffn_norm_weight, L0_ffn_gate_weight, L0_ffn_gate_bias, L0_ffn_mlp1_weight, L0_ffn_mlp1_bias, L0_ffn_mlp2_weight, L0_ffn_mlp2_bias):
    import jax
    import jax.numpy as jnp

    def _L0_attn_ref(x, W_in, conv_w, conv_b, W_x, W_dt, b_dt, A_log, D, W_out):
        import jax, jax.numpy as jnp
        import numpy as np
        D_MODEL = 256
        D_STATE = 16
        D_CONV = 4
        EXPAND = 2
        D_INNER = EXPAND * D_MODEL
        BATCH = 2
        SEQLEN = 512

        def _silu(x):
            return x * jax.nn.sigmoid(x)

        def _causal_depthwise_conv(x, w, b):
            K = w.shape[1]
            L = x.shape[1]
            xp = jnp.pad(x, ((0, 0), (K - 1, 0), (0, 0)))
            out = b
            for k in range(K):
                out = out + xp[:, k:k + L, :] * w[:, k]
            return out

        def _selective_scan(u, dt, A, Bm, Cm, D):

            def step(h, xs):
                u_t, dt_t, b_t, c_t = xs
                dA = jnp.exp(dt_t[:, :, None] * A[None])
                h = dA * h + (dt_t * u_t)[:, :, None] * b_t[:, None, :]
                y = jnp.einsum('bds,bs->bd', h, c_t) + D * u_t
                return (h, y)
            h0 = jnp.zeros((u.shape[0],) + A.shape, u.dtype)
            xs = (u.swapaxes(0, 1), dt.swapaxes(0, 1), Bm.swapaxes(0, 1), Cm.swapaxes(0, 1))
            _, ys = jax.lax.scan(step, h0, xs)
            return ys.swapaxes(0, 1)
        xz = x @ W_in
        xp, z = jnp.split(xz, 2, axis=-1)
        xc = _silu(_causal_depthwise_conv(xp, conv_w, conv_b))
        Bm, Cm = jnp.split(xc @ W_x, 2, axis=-1)
        dt = jax.nn.softplus(xc @ W_dt + b_dt)
        A = -jnp.exp(A_log)
        y = _selective_scan(xc, dt, A, Bm, Cm, D)
        y = y * _silu(z)
        return y @ W_out

    def _L0_xattn_ref(history_features, combined_features, hW, hb, cW, cb, qW, qb, kW, kb, vW, vb, oW, ob):
        import jax, jax.numpy as jnp
        import numpy as np
        B, LQ, LK = (8, 512, 512)
        HIST_DIM, COMB_DIM, FUSION_DIM = (256, 256, 256)

        def _linear_params(key, in_dim, out_dim):
            k1, k2 = jax.random.split(key)
            bound = 1.0 / np.sqrt(in_dim)
            W = jax.random.uniform(k1, (out_dim, in_dim), jnp.float32, -bound, bound)
            b = jax.random.uniform(k2, (out_dim,), jnp.float32, -bound, bound)
            return (W, b)

        def _lin(x, W, b):
            return jnp.einsum('bld,fd->blf', x, W) + b
        h = _lin(history_features, hW, hb)
        c = _lin(combined_features, cW, cb)
        q = _lin(h, qW, qb)
        k = _lin(c, kW, kb)
        v = _lin(c, vW, vb)
        scale = 1.0 / jnp.sqrt(jnp.float32(FUSION_DIM))
        scores = jnp.einsum('bqf,bkf->bqk', q, k) * scale
        attn = jax.nn.softmax(scores, axis=-1)
        attn_out = jnp.einsum('bqk,bkf->bqf', attn, v)
        return _lin(attn_out + q, oW, ob)

    def _L0_ffn_ref(x, norm_weight, gate_weight, gate_bias, mlp1_weight, mlp1_bias, mlp2_weight, mlp2_bias):
        import jax, jax.numpy as jnp
        import numpy as np
        B, S, H, I, E, K = (4, 512, 256, 256, 8, 2)
        LIMIT = 7.0
        ALPHA = 1.702
        EPS = 1e-05
        xc = x.astype(jnp.bfloat16)
        xf = xc.astype(jnp.float32)
        rms = jnp.mean(xf * xf, axis=-1, keepdims=True)
        normed = (xf * jax.lax.rsqrt(rms + EPS) * norm_weight).astype(jnp.bfloat16)
        nf = normed.astype(jnp.float32)
        logits = (jnp.einsum('bsh,eh->bse', nf, gate_weight.astype(jnp.float32)) + gate_bias.astype(jnp.float32)).astype(jnp.bfloat16).astype(jnp.float32)
        scores, idx = jax.lax.top_k(logits, K)
        w = jax.nn.softmax(scores, axis=-1)
        combine = jnp.sum(jax.nn.one_hot(idx, E, dtype=jnp.float32) * w[..., None], axis=-2)
        p1 = jnp.einsum('bsh,eoh->bseo', nf, mlp1_weight.astype(jnp.float32)) + mlp1_bias.astype(jnp.float32)
        g = jnp.minimum(p1[..., 0::2], LIMIT)
        lin = jnp.clip(p1[..., 1::2], -LIMIT, LIMIT)
        act = g * jax.nn.sigmoid(ALPHA * g) * (lin + 1.0)
        p2 = jnp.einsum('bsei,ehi->bseh', act, mlp2_weight.astype(jnp.float32)) + mlp2_bias.astype(jnp.float32)
        combined = jnp.einsum('bseh,bse->bsh', p2, combine)
        out = (xc + combined.astype(jnp.bfloat16)).astype(x.dtype)
        return out
    x = x + _L0_attn_ref(_layernorm(x, axis=-1), L0_attn_W_in, L0_attn_conv_w, L0_attn_conv_b, L0_attn_W_x, L0_attn_W_dt, L0_attn_b_dt, L0_attn_A_log, L0_attn_D, L0_attn_W_out)
    x = x + _L0_xattn_ref(_layernorm(x, axis=-1), ctx_1024, L0_xattn_hW, L0_xattn_hb, L0_xattn_cW, L0_xattn_cb, L0_xattn_qW, L0_xattn_qb, L0_xattn_kW, L0_xattn_kb, L0_xattn_vW, L0_xattn_vb, L0_xattn_oW, L0_xattn_ob)
    x = x + _L0_ffn_ref(_layernorm(x, axis=-1), L0_ffn_norm_weight, L0_ffn_gate_weight, L0_ffn_gate_bias, L0_ffn_mlp1_weight, L0_ffn_mlp1_bias, L0_ffn_mlp2_weight, L0_ffn_mlp2_bias)
    return x

_drawn_inputs = setup_inputs


def setup_inputs(seed=0):
    import zlib

    import numpy as np

    out = dict(_drawn_inputs(seed))
    spreads = {'L0_attn_conv_b': (0.0, 0.394),
     'L0_attn_b_dt': (0.0, 0.8),
     'L0_attn_D': (1.0, 0.6),
     'L0_ffn_norm_weight': (1.0, 0.2),
     'L0_ffn_gate_bias': (0.0, 0.1),
     'L0_ffn_mlp1_bias': (0.0, 0.271),
     'L0_ffn_mlp2_bias': (0.0, 0.318)}
    factors = {'L0_attn_W_in': 3.502,
     'L0_attn_conv_w': 5.995,
     'L0_attn_W_x': 8.0,
     'L0_attn_W_dt': 8.0,
     'L0_attn_A_log': 8.0,
     'L0_attn_W_out': 3.595,
     'L0_xattn_kW': 11.222,
     'L0_xattn_kb': 64.0,
     'L0_xattn_hb': 3.551,
     'L0_xattn_cb': 4.36,
     'L0_xattn_qb': 2.766,
     'L0_xattn_vb': 2.887}
    for name, (base, spread) in spreads.items():
        noise = np.random.default_rng([zlib.crc32(name.encode()), seed]).standard_normal(out[name].shape)
        drawn = base * np.exp(spread * noise) if base else spread * noise
        out[name] = jnp.asarray(drawn.astype(out[name].dtype))
    for name, factor in factors.items():
        out[name] = (out[name] * factor).astype(out[name].dtype)
    return out
```

```python
from contextlib import ExitStack

import concourse.bass as bass
from concourse import mybir

F32 = mybir.dt.float32
BF16 = mybir.dt.bfloat16
U32 = mybir.dt.uint32
ACT = mybir.ActivationFunctionType
ALU = mybir.AluOpType
AX_X = mybir.AxisListType.X

P = 128
HALF = 512
EPS = 1e-5
LIMIT = 7.0
ALPHA = 1.702
STEP_CAP = 30.0


def decoder_layer(nc, t, out):
    B, S, D = t["x"].shape
    DI = t["W_dt"].shape[0]
    N = t["A_log"].shape[1]
    KTAPS = t["conv_w"].shape[1]
    PAD = KTAPS - 1
    E = t["gate_wT"].shape[1]
    I = t["mlp2_wT"].shape[1]
    LK = t["ctxT"].shape[1] // B
    DK, CT, TT = D // P, DI // P, S // P
    NH = S // HALF
    TH = TT // NH
    KEYS = LK // 2
    ALLK = B * LK
    assert NH == 2 and DK == 2 and I == 2 * P and LK % 2 == 0 and KEYS <= P and E * NH == N

    bd = nc.dram_tensor("b_rows", (B * N, S), F32, kind="Internal").ap()
    combd = nc.dram_tensor("combine_rows", (B * E, S), F32, kind="Internal").ap()
    kqd = nc.dram_tensor("kq_rows", (B * P, DK * LK), F32, kind="Internal").ap()
    vod = nc.dram_tensor("vo_rows", (B * KEYS, 2 * D), F32, kind="Internal").ap()
    k_rowd = nc.dram_tensor("key_bias_rows", (B, LK), F32, kind="Internal").ap()
    x2d = nc.dram_tensor("x2_rows", (B * S, D), F32, kind="Internal").ap()
    x_rows = t["x"].rearrange("b s d -> (b s) d")
    out_rows = out.rearrange("b s d -> (b s) d")

    with ExitStack() as ctx:
        def sb(name, shape, dt=F32):
            return ctx.enter_context(nc.sbuf_tensor(name, shape, dt))

        def sem(name):
            return ctx.enter_context(nc.semaphore(name))

        w_in = sb("w_in", [P, DK, 2 * DI])
        w_dt = sb("w_dt", [P, CT, DI])
        w_out = sb("w_out", [P, CT, D])
        w_x = sb("w_x", [P, CT, 2 * N])
        conv_w = sb("conv_w_sb", [P, CT, KTAPS])
        chan = sb("chan", [P, 3, CT])
        a_neg = sb("a_neg", [P, CT * N])
        w1 = sb("w1", [P, E * DK * 2 * I], BF16)
        w2 = sb("w2", [P, E * 2 * D])
        bias1 = sb("bias1", [P, E * 4])
        bias2 = sb("bias2", [64, D])
        gate_w = sb("gate_w", [P, DK, E], BF16)
        gate_b = sb("gate_b", [P, 1, E], BF16)
        norm_w = sb("norm_w", [P, D])
        kq = sb("kq", [P, DK, LK])
        vo = sb("vo", [KEYS, 2, D])
        w_qo = sb("w_qo", [P, DK, D])
        rows = sb("rows", [64, S])
        ident = sb("ident", [P, P])
        ident16 = sb("ident16", [P, P], BF16)
        ones = sb("ones", [64, P])
        minus_half = sb("minus_half", [P, TT])
        iota = sb("iota", [P, 1, E])
        xt = sb("xt", [P, TT, D])
        xnT = sb("xnT", [P, DK, S])
        nfT = sb("nfT", [P, DK, S], BF16)
        xc = sb("xc", [P, CT, S])
        dt = sb("dt", [P, CT, S])
        dtu = sb("dtu", [P, CT, S])
        b_bc = sb("b_bc", [P, NH, HALF])
        c_tok = sb("c_tok", [P, TT, N])
        stage = sb("stage", [P, TT, DI])
        xn = stage
        xc16 = sb("xc16", [P, TT, D], BF16)
        work = sb("work", [P, 10240])
        wbc = sb("wbc", [P, 2, HALF])
        res = sb("res", [P, TH, D])
        stats = sb("stats", [P, TT, 6])
        mv = sb("mv", [P, TT, 2])
        ve = sb("ve", [P, TT])
        rstd = sb("rstd", [P, TT])
        ssq = sb("ssq", [P, TT])
        mx = sb("mx", [P, TT])
        negm = sb("negm", [P, TT])
        rsum = sb("rsum", [P, TT])
        rinv = sb("rinv", [P, TT])

        h = work[:, 0:4096].rearrange("p (c d t) -> p c d t", c=2, d=CT)
        dbu = work[:, 4096:6144].rearrange("p (r t) -> p r t", r=4)
        ex_g = work[:, 6144:7168].rearrange("p (j t) -> p j t", j=2)
        ex_t = work[:, 7168:8192].rearrange("p (j t) -> p j t", j=2)
        ex_l = work[:, 8192:9216].rearrange("p (j t) -> p j t", j=2)
        ex_a = work[:, 9216:10240].rearrange("p (j t) -> p j t", j=2)
        xp = dtu[:, :, :].rearrange("p a s -> p (a s)")[:, 0:2 * (PAD + S)].rearrange("p (r s) -> p r s", r=2)
        conv = work[:, 0:2048].rearrange("p (r t) -> p r t", r=2)
        tanh = work[:, 2048:4096].rearrange("p (r t) -> p r t", r=2)
        soft = work[:, 4096:5120].rearrange("p (r t) -> p r t", r=2)
        b_sb = work[0:N, 5120:6144]
        probs = work[:, 0:TT * LK].rearrange("p (a k) -> p a k", a=TT)
        probsT = work[:, 2048:4096].rearrange("p (k t) -> p k t", k=2)
        square = work[:, 4096:5120].bitcast(BF16).rearrange("p (a d) -> p a d", a=TT)
        nf = work[:, 5120:6144].bitcast(BF16).rearrange("p (a d) -> p a d", a=TT)
        mix = work[:, 6144:6656].bitcast(BF16)
        o = [6144]

        def small(*shape):
            n = 1
            for extent in shape:
                n *= extent
            o[0] += n
            names = "abcd"[:len(shape)]
            return work[:, o[0] - n:o[0]].rearrange(
                f"p ({' '.join(names)}) -> p {' '.join(names)}", **dict(zip(names[:-1], shape)))

        lg16 = small(TT, E // 2).bitcast(BF16)
        lg, m8, i8f, comb = (small(TT, E) for _ in range(4))
        i8 = small(TT, 8).bitcast(U32)
        tw = small(4, TT)
        tden = small(1, TT)[:, 0, :]
        eq = small(2, TT, E)
        o = [0]

        def part(n):
            o[0] += n
            return work[:, o[0] - n:o[0]]

        qwT, cwT, kwT, vwT, owT = (part(DK * D).rearrange("p (k f) -> p k f", k=DK) for _ in range(5))
        hwb = part(DK * (D + 1)).rearrange("p (k f) -> p k f", k=DK)
        wqh = part(DK * D).rearrange("p (k f) -> p k f", k=DK)
        ctxT, cT, kT = (part(DK * ALLK).rearrange("p (k f) -> p k f", k=DK) for _ in range(3))
        vT = ctxT
        fbias = part(4 * DK).rearrange("p (n k) -> p n k", n=4)
        bq = part(DK).rearrange("p (k n) -> p k n", n=1)
        o_row = part(D)
        ob_row = part(D)[0:1, :]
        a_log = part(CT * N)
        xc_flat = xc[:, :, :].rearrange("p a s -> p (a s)")
        bias1_raw = xc_flat[:, 0:E * 2].bitcast(BF16)
        bias2_raw = xc_flat[:, P:P + D // 2].bitcast(BF16)
        kq_all = part(DK * ALLK).rearrange("p (b k f) -> p b k f", b=B, k=DK)
        k_row = part(ALLK)[0:1, :]
        vo_all = dt[:, :, :].rearrange("p a s -> p (a s)")[0:KEYS, E * D:E * D + 2 * B * D]
        assert o[0] <= 10240
        w2_raw = dt[:, :, :].rearrange("p a d -> p (a d)")[:, 0:E * D].bitcast(BF16)

        ps = ctx.enter_context(nc.psum_tensor("ps", [P, 8, HALF], F32))

        w_early = sem("w_early")
        w_fold = sem("w_fold")
        w_late = sem("w_late")
        passed = sem("passed")
        consts = sem("consts")
        act_scaled = sem("act_scaled")
        dve_scaled = sem("dve_scaled")
        fold_ready = sem("fold_ready")
        fold_kept = sem("fold_kept")
        fold_stored = sem("fold_stored")
        kv_loaded = sem("kv_loaded")
        pad_ready = sem("pad_ready")
        x_in = [sem("x_in0"), sem("x_in1")]
        x2_stored = sem("x2_stored")
        b_stored = sem("b_stored")
        comb_stored = sem("comb_stored")
        b_loaded = [sem("b_loaded0"), sem("b_loaded1")]
        wbc_loaded = [sem("wbc_loaded0"), sem("wbc_loaded1")]
        res_loaded = sem("res_loaded")
        out_stored = sem("out_stored")
        chain = sem("chain")
        ve_ready = sem("ve_ready")
        rstd_ready = sem("rstd_ready")
        xn_ready = sem("xn_ready")
        mm_ready = sem("mm_ready")
        act_freed = sem("act_freed")
        dve_freed = sem("dve_freed")
        conv_done = sem("conv_done")
        tanh_done = sem("tanh_done")
        xc_ready = sem("xc_ready")
        cap_ready = sem("cap_ready")
        soft_ready = sem("soft_ready")
        dtu_ready = sem("dtu_ready")
        exp_ready = sem("exp_ready")
        dbu_ready = sem("dbu_ready")
        scan_done = sem("scan_done")
        hT_ready = sem("hT_ready")
        hT_used = sem("hT_used")
        p1_ready = sem("p1_ready")
        g_ready = sem("g_ready")
        l_ready = sem("l_ready")
        t_ready = sem("t_ready")
        u_ready = sem("u_ready")
        a_ready = sem("a_ready")
        aw_ready = sem("aw_ready")
        p2_ready = sem("p2_ready")
        mix_taken = sem("mix_taken")
        out_ready = sem("out_ready")
        gate_tanh = sem("gate_tanh")
        gated = sem("gated")
        negm_ready = sem("negm_ready")
        exp_probs = sem("exp_probs")
        probs_ready = sem("probs_ready")
        x16_ready = sem("x16_ready")
        ssq_ready = sem("ssq_ready")
        nf_ready = sem("nf_ready")
        gap_ready = sem("gap_ready")
        gap_exp = sem("gap_exp")
        comb_ready = sem("comb_ready")
        mix_added = sem("mix_added")

        halves = range(NH)
        jobs_a = ([("T", k, c) for c in halves for k in range(DK)] +
                  [("X", d, c) for d in range(CT) for c in halves] +
                  [("B", 0, c) for c in halves] + [("C", 0, 0)] +
                  [("S", d, c) for d in range(CT) for c in halves])
        jobs_c = ([("Z", d, c) for d in range(CT) for c in halves] +
                  [("Y", d, c) for d in range(CT) for c in halves] +
                  [("O", a, 0) for a in range(TT)] +
                  [("T2", k, c) for c in halves for k in range(DK)] +
                  [("Q", a, 0) for a in range(TT)] +
                  [("PT", k, c) for c in halves for k in range(2)] +
                  [("V", a, 0) for a in range(TT)] +
                  [("N", k, c) for c in halves for k in range(DK)] + [("G", 0, 0)] +
                  [("CT", 0, c) for c in halves])
        by_act = ("T", "X", "B", "T2", "Q", "PT", "N", "CT")
        n_jobs = len(jobs_a) + len(jobs_c)
        n_freed = {True: 0, False: 0}
        index, freed = {}, {}
        for i, job in enumerate(jobs_a + jobs_c):
            mine = job[0] in by_act
            n_freed[mine] += 1
            index[job], freed[job] = i + 1, (mine, n_freed[mine])

        def wait_apart(eng, sem, value):
            eng.wait_ge(sem, value)
            eng.sem_inc(passed, 1)

        def wait_mm(eng, b, job):
            eng.wait_ge(mm_ready, b * n_jobs + index[job])

        def wait_freed(eng, b, job):
            mine, n = freed[job]
            eng.wait_ge(act_freed if mine else dve_freed, b * n_freed[mine] + n)

        def bank_of(job):
            jobs = jobs_a if job in jobs_a else jobs_c
            return ps[:, jobs.index(job) % 8, :]

        FOLD_LOADS = 6 + 1 + 1 + 4
        fold_jobs = ([("WQH", k, 0) for k in range(DK)] + [("c", k, c) for k in range(DK) for c in range(2)] +
                     [("k", k, c) for k in range(DK) for c in range(2)] +
                     [("v", k, c) for k in range(DK) for c in range(2)] +
                     [("KQ", k, c) for k in range(DK) for c in range(2)] +
                     [("KROW", 0, c) for c in range(2)] + [("WQO", k, 0) for k in range(DK)] +
                     [("OROW", 0, 0)] + [("VO", i, 0) for i in range(2 * B)])
        KCH = ALLK // 2
        assert KCH <= HALF

        def fold_at(job):
            return fold_jobs.index(job) + 1

        units_row = N * NH

        def unit(b, hf, it, par, c):
            return b * units_row + hf * (units_row // 2) + it * 4 + par * 2 + c

        def state(b, hf, it, par):
            return b * N + hf * (N // 2) + it * 2 + par

        ITS = N // 4
        DBU_CREDIT, SCAN_CREDIT, HT_CREDIT, AW_CREDIT = 8, 4, 2, 4
        STORE_CREDIT = 16

        block = ctx.enter_context(nc.Block())

        def over_rows(eng, phase_a, loop, phase_c):
            phase_a(0)
            for hf in range(2):
                loop(0, None, hf)
            phase_c(0)
            with eng.Fori(1, B) as b:
                phase_a(b)
                for hf in range(2):
                    loop(b, b - 1, hf)
                phase_c(b)
            for hf in range(2):
                loop(None, B - 1, hf)

        @block.sync
        def _(sp):
            def load_x(b):
                for c in halves:
                    sp.dma_start(xt[:, c * TH:(c + 1) * TH, :],
                                 x_rows[bass.ds(b * S + c * HALF, HALF), :].rearrange("(a p) d -> p a d", p=P)
                                 ).then_inc(x_in[c], 16)

            load_x(0)
            for dst, name in ((w_in, "W_in"), (w_x, "W_x"), (w_dt, "W_dt"), (w_out, "W_out")):
                sp.dma_start(dst[:, :, :], t[name].rearrange("(k p) n -> p k n", p=P)).then_inc(w_early, 16)
            sp.dma_start(conv_w[:, :, :], t["conv_w"].rearrange("(k p) n -> p k n", p=P)).then_inc(w_early, 16)
            for i, name in enumerate(("conv_b", "b_dt", "D_skip")):
                sp.dma_start(chan[:, i, :], t[name].rearrange("(k p) -> p k", p=P),
                             allow_slow_non_contiguous=True).then_inc(w_early, 16)
            sp.dma_start(a_log.rearrange("p (k n) -> p k n", n=N),
                         t["A_log"].rearrange("(k p) n -> p k n", p=P)).then_inc(w_early, 16)
            sp.dma_start(w2_raw.rearrange("p (e k f) -> p e k f", e=E, k=2),
                         t["mlp2_wT"].rearrange("e (k p) f -> p e k f", p=P)).then_inc(w_late, 16)
            sp.dma_start(w1[:, :].rearrange("p (e k f) -> p e k f", e=E, k=DK),
                         t["mlp1_wT"].rearrange("e (k p) f -> p e k f", p=P)).then_inc(w_late, 16)
            sp.dma_start(bias1_raw[:, :], t["mlp1_bT"]).then_inc(w_late, 16)
            sp.dma_start(bias2_raw[32:32 + E, :], t["mlp2_b"]).then_inc(w_late, 16)
            sp.dma_start(gate_w[:, :, :], t["gate_wT"].rearrange("(k p) e -> p k e", p=P)).then_inc(w_late, 16)
            sp.dma_start(gate_b[:, :, :], t["gate_b"].partition_broadcast(P)).then_inc(w_late, 16)
            sp.dma_start(norm_w[:, :], t["norm_w"].partition_broadcast(P)).then_inc(w_late, 16)

            sp.wait_ge(fold_kept, len(fold_jobs))
            sp.dma_start(kqd.rearrange("(b p) (k f) -> p b k f", p=P, k=DK), kq_all).then_inc(fold_stored, 16)
            sp.dma_start(vod.rearrange("(b p) f -> p b f", p=KEYS),
                         vo_all.rearrange("p (b f) -> p b f", b=B)).then_inc(fold_stored, 16)
            sp.dma_start(k_rowd.rearrange("b (o f) -> o b f", o=1), k_row.rearrange("o (b f) -> o b f", b=B)
                         ).then_inc(fold_stored, 16)
            sp.wait_ge(fold_stored, 3 * 16)

            def phase_a(b):
                if not isinstance(b, int):
                    wait_apart(sp, x2_stored, b * 16)
                    wait_apart(sp, x16_ready, b * TT)
                    load_x(b)
                sp.dma_start(kq[:, :, :], kqd[bass.ds(b * P, P), :].rearrange("p (k f) -> p k f", k=DK)
                             ).then_inc(kv_loaded, 16)
                sp.dma_start(vo[:, :, :], vod[bass.ds(b * KEYS, KEYS), :].rearrange("p (k f) -> p k f", k=2)
                             ).then_inc(kv_loaded, 16)
                sp.dma_start(rows[0:1, 0:LK], k_rowd[bass.ds(b, 1), :]).then_inc(kv_loaded, 16)
                wait_freed(sp, b, ("B", 0, NH - 1))
                sp.dma_start(bd[bass.ds(b * N, N), :], b_sb).then_inc(b_stored, 16)
                wait_apart(sp, b_stored, b * 16 + 16)

            def loop(b, bp, hf):
                if bp is not None:
                    wait_apart(sp, out_stored, (bp * 2 + hf) * 16 + STORE_CREDIT)
                    sp.dma_start(res[:, :, :],
                                 x2d[bass.ds(bp * S + hf * HALF, HALF), :].rearrange("(a p) d -> p a d", p=P)
                                 ).then_inc(res_loaded, 16)
                with sp.Fori(0, ITS) as it:
                    for par in range(2):
                        if b is not None:
                            for c in halves:
                                wait_apart(sp, dbu_ready, unit(b, hf, it, par, c) * CT + CT)
                                sp.dma_start(b_bc[:, c:c + 1, :],
                                             bd[bass.ds(state(b, hf, it, par), 1),
                                                c * HALF:(c + 1) * HALF].partition_broadcast(P)
                                             ).then_inc(b_loaded[c], 16)
                        if bp is not None:
                            wait_apart(sp, aw_ready, state(bp, hf, it, par) * 2 + 2)
                            sp.dma_start(wbc[:, par:par + 1, :],
                                         combd[bass.ds(bp * E + it * 2 + par, 1),
                                               hf * HALF:(hf + 1) * HALF].partition_broadcast(P)
                                         ).then_inc(wbc_loaded[par], 16)

            def phase_c(b):
                wait_freed(sp, b, ("V", TT - 1, 0))
                sp.dma_start(x2d[bass.ds(b * S, S), :].rearrange("(a p) d -> p a d", p=P),
                             xt[:, :, :]).then_inc(x2_stored, 16)
                wait_freed(sp, b, ("CT", 0, NH - 1))
                sp.dma_start(combd[bass.ds(b * E, E), :], rows[32:32 + E, :]).then_inc(comb_stored, 16)
                wait_apart(sp, comb_stored, b * 16 + 16)
                wait_apart(sp, x2_stored, b * 16 + 16)

            sp.sem_inc(out_stored, STORE_CREDIT)
            over_rows(sp, phase_a, loop, phase_c)
            sp.wait_ge(out_stored, B * 2 * 16 + STORE_CREDIT)

        @block.gpsimd
        def _(pool):
            pool.sem_inc(dbu_ready, DBU_CREDIT)
            pool.sem_inc(aw_ready, AW_CREDIT)
            pool.memset(ident[:, :], 0.0).then_inc(consts, 1)
            pool.memset(ones[:, :], 1.0).then_inc(consts, 1)
            pool.memset(minus_half[:, :], -0.5).then_inc(consts, 1)
            pool.iota(iota[:, 0, :], [[1, E]], base=0, channel_multiplier=0,
                      allow_small_or_imprecise_dtypes=True).then_inc(consts, 1)
            pool.wait_ge(consts, 1)
            pool.affine_select(out=ident[:, :], in_=ident[:, :], compare_op=ALU.not_equal, fill=1.0, base=0,
                               pattern=[[-1, P]], channel_multiplier=1).then_inc(consts, 1)
            pool.wait_ge(consts, 5)
            pool.tensor_copy(ident16[:, :], ident[:, :]).then_inc(consts, 1)

            def norm_scale(n):
                pool.wait_ge(ve_ready, n + 1)
                pool.tensor_tensor(rstd[:, :], ve[:, :], minus_half[:, :], ALU.pow).then_inc(rstd_ready, 1)

            def phase_a(b):
                norm_scale(b * 4)
                pool.memset(xp[:, :, 0:PAD], 0.0).then_inc(pad_ready, 1)
                for d in range(CT):
                    for c in halves:
                        wait_freed(pool, b, ("S", d, c))
                        cols = slice(c * HALF, (c + 1) * HALF)
                        pool.tensor_tensor(dtu[:, d, cols], dt[:, d, cols], xc[:, d, cols],
                                           ALU.mult).then_inc(dtu_ready, 1)

            def loop(b, bp, hf):
                with pool.Fori(0, ITS) as it:
                    for par in range(2):
                        for c in halves:
                            if b is not None:
                                pool.wait_ge(b_loaded[c], state(b, hf, it, par) * 16 + 16)
                                pool.wait_ge(dtu_ready, b * CT * NH + CT * NH)
                                for d in range(CT):
                                    pool.wait_ge(scan_done, unit(b, hf, it, par, c) * CT + d + 1)
                                    pool.tensor_tensor(dbu[:, d, :], dtu[:, d, c * HALF:(c + 1) * HALF],
                                                       b_bc[:, c, :],
                                                       ALU.mult).then_inc(dbu_ready, 1)
                            if bp is not None:
                                j = c
                                if j == 0:
                                    pool.wait_ge(wbc_loaded[par], (bp * 2 * ITS + hf * ITS + it) * 16 + 16)
                                pool.wait_ge(a_ready, unit(bp, hf, it, par, j) + 1)
                                pool.tensor_tensor(ex_a[:, j, :], ex_l[:, j, :], wbc[:, par, :],
                                                   ALU.mult).then_inc(aw_ready, 1)

            def phase_c(b):
                for d in range(CT):
                    for c in halves:
                        wait_freed(pool, b, ("Y", d, c))
                        cols = slice(c * HALF, (c + 1) * HALF)
                        pool.tensor_tensor(xc[:, d, cols], xc[:, d, cols], dt[:, d, cols],
                                           ALU.mult).then_inc(gated, 1)
                norm_scale(b * 4 + 1)
                norm_scale(b * 4 + 2)
                norm_scale(b * 4 + 3)

            over_rows(pool, phase_a, loop, phase_c)

        @block.scalar
        def _(act):
            for dst, name in ((qwT, "qWT"), (cwT, "cWT"), (kwT, "kWT"), (vwT, "vWT"), (owT, "oWT")):
                act.dma_start(dst, t[name].rearrange("(k p) f -> p k f", p=P)).then_inc(w_fold, 16)
            act.dma_start(hwb[:, :, 0:D], t["hW"].rearrange("(k p) f -> p k f", p=P)).then_inc(w_fold, 16)
            act.dma_start(hwb[:, :, D:D + 1], t["hb"].rearrange("(k p o) -> p k o", p=P, o=1),
                          allow_slow_non_contiguous=True).then_inc(w_fold, 16)
            act.dma_start(ctxT, t["ctxT"].rearrange("(k p) f -> p k f", p=P)).then_inc(w_fold, 16)
            for i, name in enumerate(("qb", "cb", "kb", "vb")):
                act.dma_start(fbias[:, i, :], t[name].rearrange("(k p) -> p k", p=P),
                              allow_slow_non_contiguous=True).then_inc(w_fold, 16)
            act.dma_start(ob_row, t["ob"].rearrange("(a f) -> a f", a=1)).then_inc(w_fold, 16)

            act.wait_ge(w_early, 9 * 16)
            act.activation(a_neg[:, :], a_log, ACT.Exp).then_inc(act_scaled, 1)
            act.wait_ge(act_scaled, 1)
            act.activation(a_neg[:, :], a_neg[:, :], ACT.Copy, scale=-1.0).then_inc(act_scaled, 1)
            act.activation(w_out[:, :, :], w_out[:, :, :], ACT.Copy, scale=0.5).then_inc(act_scaled, 1)

            act.wait_ge(w_fold, (FOLD_LOADS + 1) * 16)
            for i, (what, k, c) in enumerate(fold_jobs):
                bank = ps[:, i % 8, :]
                keys = slice(c * KCH, (c + 1) * KCH)
                act.wait_ge(fold_ready, i + 1)
                if what == "WQH":
                    act.activation(wqh[:, k, :], bank[:, 0:D], ACT.Copy)
                    last = act.activation(bq[:, k, :], bank[:, D:D + 1], ACT.Identity, bias=fbias[:, 0, k:k + 1])
                elif what in "ckv":
                    dst = {"c": cT, "k": kT, "v": vT}[what]
                    last = act.activation(dst[:, k, keys], bank[:, 0:KCH], ACT.Identity,
                                          bias=fbias[:, 1 + "ckv".index(what), k:k + 1])
                elif what == "KQ":
                    last = act.activation(kq_all[:, c * (B // 2):(c + 1) * (B // 2), k, :],
                                          bank[:, 0:KCH].rearrange("p (b f) -> p b f", b=B // 2), ACT.Copy)
                elif what == "KROW":
                    last = act.activation(k_row[:, keys], bank[0:1, 0:KCH], ACT.Copy)
                elif what == "WQO":
                    last = act.activation(w_qo[:, k, :], bank[:, 0:D], ACT.Copy)
                elif what == "OROW":
                    last = act.activation(o_row[0:1, :], bank[0:1, 0:D], ACT.Copy)
                else:
                    last = act.activation(vo_all[:, k * D:(k + 1) * D], bank[0:KEYS, 0:D], ACT.Copy)
                last.then_inc(fold_kept, 1)

            def phase_a(b):
                for job in jobs_a[0:4]:
                    _, k, c = job
                    wait_mm(act, b, job)
                    act.activation(xnT[:, k, c * HALF:(c + 1) * HALF], bank_of(job), ACT.Copy
                                   ).then_inc(act_freed, 1)

                def conv_in(d):
                    for c in halves:
                        wait_mm(act, b, ("X", d, c))
                        act.activation(xp[:, d % 2, PAD + c * HALF:PAD + (c + 1) * HALF],
                                       bank_of(("X", d, c)), ACT.Copy).then_inc(act_freed, 1)

                def silu_tanh(d):
                    act.wait_ge(conv_done, b * CT * KTAPS + (d + 1) * KTAPS)
                    act.activation(tanh[:, d % 2, :], conv[:, d % 2, :], ACT.Tanh).then_inc(tanh_done, 1)

                conv_in(0)
                conv_in(1)
                for d in range(CT):
                    silu_tanh(d)
                    if d + 2 < CT:
                        conv_in(d + 2)
                for c in halves:
                    wait_mm(act, b, ("B", 0, c))
                    act.activation(b_sb[:, c * HALF:(c + 1) * HALF], bank_of(("B", 0, c))[0:N, :], ACT.Copy
                                   ).then_inc(act_freed, 1)
                for i in range(CT * NH):
                    act.wait_ge(cap_ready, b * CT * NH + i + 1)
                    act.activation(soft[:, i % 2, :], soft[:, i % 2, :], ACT.Exp).then_inc(soft_ready, 1)
                    act.wait_ge(soft_ready, b * 2 * CT * NH + 2 * i + 1)
                    act.activation(soft[:, i % 2, :], soft[:, i % 2, :], ACT.Ln, bias=1.0).then_inc(soft_ready, 1)
                wait_freed(act, b, ("S", CT - 1, NH - 1))

            def loop(b, bp, hf):
                with act.Fori(0, ITS) as it:
                    for par in range(2):
                        for c in halves:
                            if b is not None:
                                for d in range(CT):
                                    wait_apart(act, scan_done, unit(b, hf, it, par, c) * CT + d + 3)
                                    act.activation(ps[:, d % 2, :], dt[:, d, c * HALF:(c + 1) * HALF], ACT.Exp,
                                                   scale=a_neg[:, bass.ds(it * 2 + (d * N + hf * (N // 2) + par), 1)]
                                                   ).then_inc(exp_ready, 1)
                            if bp is not None:
                                act.wait_ge(g_ready, unit(bp, hf, it, par, c) + 2)
                                act.activation(ex_t[:, c, :], ex_g[:, c, :], ACT.Tanh, scale=ALPHA / 2
                                               ).then_inc(t_ready, 1)
                if bp is not None:
                    act.wait_ge(out_ready, bp * 2 + hf + 1)
                    act.dma_start(out_rows[bass.ds(bp * S + hf * HALF, HALF), :].rearrange("(a p) d -> p a d", p=P),
                                  res[:, :, :]).then_inc(out_stored, 16)

            def phase_c(b):
                for i, (_, d, c) in enumerate(jobs_c[0:8]):
                    job = ("Z", d, c)
                    wait_mm(act, b, job)
                    act.activation(dt[:, d, c * HALF:(c + 1) * HALF], bank_of(job), ACT.Tanh, scale=0.5
                                   ).then_inc(gate_tanh, 1)
                for c in halves:
                    for k in range(DK):
                        wait_mm(act, b, ("T2", k, c))
                        act.activation(xnT[:, k, c * HALF:(c + 1) * HALF], bank_of(("T2", k, c)), ACT.Copy
                                       ).then_inc(act_freed, 1)
                for a in range(TT):
                    act.wait_ge(negm_ready, b * TT + a + 1)
                    act.activation(probs[:, a, :], bank_of(("Q", a, 0))[:, 0:LK], ACT.Exp, scale=float(D) ** -0.5,
                                   bias=negm[:, a:a + 1], accum_out=rsum[:, a:a + 1]).then_inc(act_freed, 1)
                for c in halves:
                    for k in range(2):
                        wait_mm(act, b, ("PT", k, c))
                        act.activation(probsT[0:KEYS, k, c * HALF:(c + 1) * HALF],
                                       bank_of(("PT", k, c))[0:KEYS, :], ACT.Copy).then_inc(act_freed, 1)
                for a in range(TT):
                    act.wait_ge(x16_ready, b * TT + a + 1)
                    act.activation(square[:, a, :], xc16[:, a, :], ACT.Square, accum_out=ssq[:, a:a + 1]
                                   ).then_inc(ssq_ready, 1)
                for c in halves:
                    for k in range(DK):
                        wait_mm(act, b, ("N", k, c))
                        act.activation(nfT[:, k, c * HALF:(c + 1) * HALF],
                                       bank_of(("N", k, c)).bitcast(BF16)[:, 0:HALF], ACT.Copy
                                       ).then_inc(act_freed, 1)
                act.wait_ge(gap_ready, b + 1)
                act.activation(tw[:, 1, :], tw[:, 0, :], ACT.Exp).then_inc(gap_exp, 1)
                for c in halves:
                    wait_mm(act, b, ("CT", 0, c))
                    act.activation(rows[32:32 + E, c * HALF:(c + 1) * HALF], bank_of(("CT", 0, c))[0:E, :], ACT.Copy
                                   ).then_inc(act_freed, 1)

            over_rows(act, phase_a, loop, phase_c)

        @block.vector
        def _(dve):
            links = [0]
            per_row = [0]

            def link(b, ins):
                links[0] += 1
                ins.then_inc(chain, 1)
                if isinstance(b, int):
                    dve.wait_ge(chain, links[0])
                else:
                    wait_apart(dve, chain, b * per_row[0] + links[0])

            dve.sem_inc(scan_done, SCAN_CREDIT)
            dve.sem_inc(hT_used, HT_CREDIT)
            dve.sem_inc(g_ready, 1)
            dve.sem_inc(l_ready, 1)
            dve.sem_inc(mix_taken, 1)

            def norm(b, n, dst, done):
                for a in range(TT):
                    if n == 0 and a % TH == 0:
                        dve.wait_ge(x_in[a // TH], b * 16 + 16)
                    ins = dve.bn_stats(stats[:, a, :], xt[:, a, :])
                link(b, ins)
                for a in range(TT):
                    ins = dve.bn_aggr(mv[:, a, :], stats[:, a, :])
                link(b, ins)
                dve.tensor_scalar(ve[:, :], mv[:, :, 1], EPS, None, ALU.add).then_inc(ve_ready, 1)
                dve.wait_ge(rstd_ready, b * 4 + n + 1)
                for a in range(TT):
                    dve.tensor_scalar(dst[:, a, 0:D], xt[:, a, :], mv[:, a, 0:1], rstd[:, a:a + 1],
                                      ALU.subtract, ALU.mult).then_inc(done, 1)

            def phase_a(b):
                links[0] = 0
                norm(b, 0, xn, xn_ready)
                if isinstance(b, int):
                    dve.wait_ge(w_early, 9 * 16)
                    dve.tensor_scalar(conv_w[:, :, :], conv_w[:, :, :], 0.5, None, ALU.mult).then_inc(dve_scaled, 1)
                    dve.tensor_scalar(chan[:, 0, :], chan[:, 0, :], 0.5, None, ALU.mult).then_inc(dve_scaled, 1)
                    dve.wait_ge(w_late, 7 * 16)
                    dve.tensor_scalar(w2[:, :], w2_raw, 0.5, None, ALU.mult).then_inc(dve_scaled, 1)
                    dve.tensor_copy(bias2[32:32 + E, :], bias2_raw[32:32 + E, :]).then_inc(dve_scaled, 1)
                    b1v = bias1[:, :].rearrange("p (e g) -> p e g", g=4)
                    b1r = bias1_raw[:, :].rearrange("p (e g) -> p e g", g=4)
                    dve.tensor_copy(b1v[:, :, 0:2], b1r[:, :, 0:2]).then_inc(dve_scaled, 1)
                    dve.tensor_scalar(b1v[:, :, 2:4], b1r[:, :, 2:4], 1.0, None, ALU.add).then_inc(dve_scaled, 1)
                    dve.wait_ge(dve_scaled, 6)
                    dve.wait_ge(consts, 6)
                    dve.wait_ge(fold_stored, 3 * 16)

                def convolve(d):
                    wait_freed(dve, b, ("X", d, NH - 1))
                    if d == 0:
                        dve.wait_ge(pad_ready, b + 1)
                    if d >= 2:
                        dve.wait_ge(xc_ready, b * CT + d - 1)
                    v, base = conv[:, d % 2, :], b * CT * KTAPS + d * KTAPS
                    dve.tensor_scalar(v, xp[:, d % 2, 0:S], conv_w[:, d, 0:1], chan[:, 0, d:d + 1],
                                      ALU.mult, ALU.add).then_inc(conv_done, 1)
                    for k in range(1, KTAPS):
                        dve.wait_ge(conv_done, base + k)
                        dve.scalar_tensor_tensor(v, xp[:, d % 2, k:k + S], conv_w[:, d, k:k + 1], v,
                                                 ALU.mult, ALU.add).then_inc(conv_done, 1)

                def silu(d):
                    dve.wait_ge(tanh_done, b * CT + d + 1)
                    dve.scalar_tensor_tensor(xc[:, d, :], tanh[:, d % 2, :], 1.0, conv[:, d % 2, :],
                                             ALU.add, ALU.mult).then_inc(xc_ready, 1)

                convolve(0)
                for d in range(CT):
                    if d + 1 < CT:
                        convolve(d + 1)
                    silu(d)
                wait_mm(dve, b, ("C", 0, 0))
                dve.tensor_copy(c_tok[:, :, :].rearrange("p a n -> p (a n)"),
                                bank_of(("C", 0, 0))[:, 0:TT * N]).then_inc(dve_freed, 1)
                dve.memset(stage[:, :, :], 0.0)

                def cap(i):
                    job = ("S", i // NH, i % NH)
                    wait_mm(dve, b, job)
                    if i >= 2:
                        wait_freed(dve, b, ("S", (i - 2) // NH, i % NH))
                    dve.tensor_scalar(soft[:, i % 2, :], bank_of(job), chan[:, 1, i // NH:i // NH + 1], STEP_CAP,
                                      ALU.add, ALU.min).then_inc(cap_ready, 1)

                def step(i):
                    d, c = i // NH, i % NH
                    dve.wait_ge(soft_ready, b * 2 * CT * NH + 2 * i + 2)
                    dve.scalar_tensor_tensor(dt[:, d, c * HALF:(c + 1) * HALF], bank_of(("S", d, c)),
                                             chan[:, 1, d:d + 1], soft[:, i % 2, :],
                                             ALU.add, ALU.max).then_inc(dve_freed, 1)

                cap(0)
                for i in range(CT * NH):
                    if i + 1 < CT * NH:
                        cap(i + 1)
                    step(i)

            def loop(b, bp, hf):
                with dve.Fori(0, ITS) as it:
                    for par in range(2):
                        for c in halves:
                            if b is not None:
                                u = unit(b, hf, it, par, c)
                                for d in range(CT):
                                    dve.wait_ge(exp_ready, u * CT + d + 1)
                                    dve.wait_ge(dbu_ready, u * CT + d + 1 + DBU_CREDIT)
                                    first = 0.0 if c == 0 else h[:, 0, d, HALF - 1:HALF]
                                    dve.tensor_tensor_scan(h[:, c, d, :], ps[:, d % 2, :], dbu[:, d, :], first,
                                                           ALU.mult, ALU.add).then_inc(scan_done, 1)
                            if bp is not None:
                                s = unit(bp, hf, it, par, c)
                                col = it * 8 + (par * 4 + c)
                                dve.wait_ge(p1_ready, s * 2 + 1)
                                dve.tensor_scalar(ex_g[:, c, :], ps[:, 4, :], bias1[:, bass.ds(col, 1)], LIMIT,
                                                  ALU.add, ALU.min).then_inc(g_ready, 1)
                                dve.wait_ge(p1_ready, s * 2 + 2)
                                dve.tensor_scalar(ex_l[:, c, :], ps[:, 5, :], bias1[:, bass.ds(col + 2, 1)],
                                                  LIMIT + 1.0, ALU.add, ALU.min).then_inc(l_ready, 1)
                                dve.wait_ge(t_ready, s + 1)
                                dve.scalar_tensor_tensor(ex_t[:, c, :], ex_t[:, c, :], 1.0, ex_g[:, c, :],
                                                         ALU.add, ALU.mult).then_inc(u_ready, 1)
                                dve.wait_ge(u_ready, s + 1)
                                dve.scalar_tensor_tensor(ex_l[:, c, :], ex_l[:, c, :], 1.0 - LIMIT, ex_t[:, c, :],
                                                         ALU.max, ALU.mult).then_inc(a_ready, 1)
                            if b is not None:
                                for a in range(TH):
                                    ta = c * TH + a
                                    dve.wait_ge(hT_ready, u * TH + a + 1)
                                    dve.scalar_tensor_tensor(
                                        stage[:, ta, :], ps[:, 2 + a % 2, :],
                                        c_tok[:, ta, bass.ds(it * 2 + (hf * (N // 2) + par), 1)],
                                        stage[:, ta, :], ALU.mult, ALU.add).then_inc(hT_used, 1)
                if bp is not None:
                    dve.wait_ge(p2_ready, unit(bp, hf, ITS - 1, 1, 1) + 1)
                    dve.tensor_copy(mix[:, 0:HALF], ps[:, 6, :])
                    dve.tensor_copy(mix[:, HALF:2 * HALF], ps[:, 7, :]).then_inc(mix_taken, 1)
                    dve.wait_ge(mix_taken, bp * 2 + hf + 2)
                    flat16 = xc16[:, hf * TH:(hf + 1) * TH, :].rearrange("p a d -> p (a d)")
                    dve.tensor_tensor(mix[:, :], mix[:, :], flat16, ALU.add).then_inc(mix_added, 1)
                    dve.wait_ge(mix_added, bp * 2 + hf + 1)
                    dve.wait_ge(res_loaded, (bp * 2 + hf) * 16 + 16)
                    flat = res[:, :, :].rearrange("p a d -> p (a d)")
                    dve.tensor_tensor(flat, mix[:, :], flat, ALU.add).then_inc(out_ready, 1)
                    wait_apart(dve, out_ready, bp * 2 + hf + 1)

            def phase_c(b):
                for job in jobs_c[0:8]:
                    _, d, c = job
                    cols = slice(c * HALF, (c + 1) * HALF)
                    dve.wait_ge(gate_tanh, b * CT * NH + d * NH + c + 1)
                    dve.scalar_tensor_tensor(dt[:, d, cols], dt[:, d, cols], 1.0, bank_of(job),
                                             ALU.add, ALU.mult).then_inc(dve_freed, 1)
                for job in jobs_c[8:16]:
                    _, d, c = job
                    cols = slice(c * HALF, (c + 1) * HALF)
                    wait_mm(dve, b, job)
                    dve.scalar_tensor_tensor(xc[:, d, cols], xc[:, d, cols], chan[:, 2, d:d + 1], bank_of(job),
                                             ALU.mult, ALU.add).then_inc(dve_freed, 1)
                for a in range(TT):
                    job = ("O", a, 0)
                    wait_mm(dve, b, job)
                    ins = dve.tensor_tensor(xt[:, a, :], xt[:, a, :], bank_of(job)[:, 0:D], ALU.add
                                            ).then_inc(dve_freed, 1)
                wait_freed(dve, b, ("O", TT - 1, 0))
                norm(b, 1, xn, xn_ready)
                for a in range(TT):
                    job = ("Q", a, 0)
                    wait_mm(dve, b, job)
                    link(b, dve.reduce_max(mx[:, a:a + 1], bank_of(job)[:, 0:LK], AX_X))
                    dve.tensor_scalar(negm[:, a:a + 1], mx[:, a:a + 1], -(float(D) ** -0.5), None, ALU.mult
                                      ).then_inc(negm_ready, 1)
                for a in range(TT):
                    wait_freed(dve, b, ("Q", a, 0))
                    link(b, dve.reciprocal(rinv[:, a:a + 1], rsum[:, a:a + 1]))
                    dve.tensor_scalar(probs[:, a, :], probs[:, a, :], rinv[:, a:a + 1], None, ALU.mult
                                      ).then_inc(probs_ready, 1)
                for a in range(TT):
                    job = ("V", a, 0)
                    wait_mm(dve, b, job)
                    dve.tensor_tensor(xt[:, a, :], xt[:, a, :], bank_of(job)[:, 0:D], ALU.add
                                      ).then_inc(dve_freed, 1)
                wait_freed(dve, b, ("V", TT - 1, 0))
                norm(b, 2, xc16, x16_ready)
                dve.wait_ge(ssq_ready, b * TT + TT)
                dve.tensor_scalar(ve[:, :], ssq[:, :], 1.0 / D, EPS, ALU.mult, ALU.add).then_inc(ve_ready, 1)
                dve.wait_ge(rstd_ready, b * 4 + 4)
                for a in range(TT):
                    dve.scalar_tensor_tensor(nf[:, a, :], xc16[:, a, :], rstd[:, a:a + 1], norm_w[:, :],
                                             ALU.mult, ALU.mult).then_inc(nf_ready, 1)
                wait_mm(dve, b, ("G", 0, 0))
                dve.tensor_tensor(lg16[:, :, :], bank_of(("G", 0, 0))[:, 0:TT * E].rearrange("p (a e) -> p a e", e=E),
                                  gate_b[:, :, :].broadcast_to([P, TT, E]), ALU.add).then_inc(dve_freed, 1)
                wait_freed(dve, b, ("G", 0, 0))
                link(b, dve.tensor_copy(lg[:, :, :], lg16[:, :, :]))
                for a in range(TT):
                    ins = dve.max(m8[:, a, :], lg[:, a, :])
                link(b, ins)
                dve.tensor_tensor(tw[:, 0, :], m8[:, :, 1], m8[:, :, 0], ALU.subtract).then_inc(gap_ready, 1)
                for a in range(TT):
                    ins = dve.max_index(i8[:, a, :], m8[:, a, :], lg[:, a, :])
                link(b, ins)
                link(b, dve.tensor_copy(i8f[:, :, :], i8[:, :, :]))
                for n in range(2):
                    ins = dve.tensor_tensor(eq[:, n, :, :], iota[:, :, :].broadcast_to([P, TT, E]),
                                            i8f[:, :, n:n + 1].broadcast_to([P, TT, E]), ALU.is_equal)
                link(b, ins)
                dve.wait_ge(gap_exp, b + 1)
                link(b, dve.tensor_scalar(tden[:, :], tw[:, 1, :], 1.0, None, ALU.add))
                link(b, dve.reciprocal(tw[:, 2, :], tden[:, :]))
                link(b, dve.tensor_tensor(tw[:, 3, :], tw[:, 1, :], tw[:, 2, :], ALU.mult))
                for n in range(2):
                    ins = dve.tensor_tensor(eq[:, n, :, :], eq[:, n, :, :],
                                            tw[:, 2 + n, :].rearrange("p (a o) -> p a o", o=1).broadcast_to([P, TT, E]),
                                            ALU.mult)
                link(b, ins)
                dve.tensor_tensor(comb[:, :, :], eq[:, 0, :, :], eq[:, 1, :, :], ALU.add).then_inc(comb_ready, 1)
                if isinstance(b, int):
                    per_row[0] = links[0]

            over_rows(dve, phase_a, loop, phase_c)

        @block.tensor
        def _(pe):
            pe.wait_ge(w_fold, (FOLD_LOADS + 1) * 16)
            pe.wait_ge(consts, 6)
            for i, (what, k, c) in enumerate(fold_jobs):
                bank = ps[:, i % 8, :]
                cols = slice(k * P, (k + 1) * P)
                keys = slice(c * KCH, (c + 1) * KCH)
                need = {"WQH": 0, "c": 0, "k": fold_at(("c", 1, 1)), "v": fold_at(("k", 1, 1)),
                        "KQ": fold_at(("k", 1, 1)), "KROW": fold_at(("k", 1, 1)), "WQO": fold_at(("WQH", 1, 0)),
                        "OROW": fold_at(("WQH", 1, 0)), "VO": fold_at(("OROW", 0, 0))}[what]
                need = max(need, i - 7)
                if need:
                    pe.wait_ge(fold_kept, need)
                pairs = {"WQH": lambda: [(qwT[:, q, cols], hwb[:, q, :]) for q in range(DK)],
                         "c": lambda: [(cwT[:, q, cols], ctxT[:, q, keys]) for q in range(DK)],
                         "k": lambda: [(kwT[:, q, cols], cT[:, q, keys]) for q in range(DK)],
                         "v": lambda: [(vwT[:, q, cols], cT[:, q, keys]) for q in range(DK)],
                         "KQ": lambda: [(wqh[:, q, cols], kT[:, q, keys]) for q in range(DK)],
                         "KROW": lambda: [(bq[:, q, :], kT[:, q, keys]) for q in range(DK)],
                         "WQO": lambda: [(wqh[:, q, cols], owT[:, q, :]) for q in range(DK)],
                         "OROW": lambda: [(bq[:, q, :], owT[:, q, :]) for q in range(DK)] + [(ones[0:1, 0:1], ob_row)],
                         "VO": lambda: [(vT[:, q, k * KEYS:(k + 1) * KEYS], owT[:, q, :]) for q in range(DK)]
                               + [(ones[0:1, 0:KEYS], o_row[0:1, :])]}[what]()
                for n, (left, right) in enumerate(pairs):
                    dst = bank[0:left.shape[1], 0:right.shape[1]]
                    mm = pe.matmul(dst, left, right, start=(n == 0), stop=(n == len(pairs) - 1))
                mm.then_inc(fold_ready, 1)

            def product(bank, pairs):
                for n, (left, right) in enumerate(pairs):
                    mm = pe.matmul(bank, left, right, start=(n == 0), stop=(n == len(pairs) - 1))
                return mm

            def free_bank(b, jobs, job):
                i = jobs.index(job)
                if i >= 8:
                    wait_freed(pe, b, jobs[i - 8])

            def transposes(b, job, src, idn, n_norm):
                _, k, c = job
                bank = bank_of(job)
                for a in range(TH):
                    mm = pe.transpose(bank[:, a * P:(a + 1) * P], src[:, c * TH + a, k * P:(k + 1) * P], idn[:, :])
                return mm

            def phase_a(b):
                if not isinstance(b, int):
                    wait_freed(pe, b - 1, ("CT", 0, NH - 1))
                    wait_freed(pe, b - 1, ("G", 0, 0))
                else:
                    pe.wait_ge(fold_kept, len(fold_jobs))
                for c in halves:
                    pe.wait_ge(xn_ready, b * 2 * TT + (c + 1) * TH)
                    for k in range(DK):
                        transposes(b, ("T", k, c), xn, ident, 0).then_inc(mm_ready, 1)
                if isinstance(b, int):
                    pe.wait_ge(w_early, 9 * 16)
                for d in range(CT):
                    for c in halves:
                        job = ("X", d, c)
                        free_bank(b, jobs_a, job)
                        wait_freed(pe, b, ("T", DK - 1, c))
                        product(bank_of(job), [(w_in[:, k, d * P:(d + 1) * P], xnT[:, k, c * HALF:(c + 1) * HALF])
                                               for k in range(DK)]).then_inc(mm_ready, 1)
                pe.wait_ge(xc_ready, b * CT + CT)
                for c in halves:
                    job = ("B", 0, c)
                    free_bank(b, jobs_a, job)
                    product(bank_of(job)[0:N, :], [(w_x[:, d, 0:N], xc[:, d, c * HALF:(c + 1) * HALF])
                                                   for d in range(CT)]).then_inc(mm_ready, 1)
                job = ("C", 0, 0)
                free_bank(b, jobs_a, job)
                for a in range(TT):
                    mm = product(bank_of(job)[:, a * N:(a + 1) * N],
                                 [(xc[:, d, a * P:(a + 1) * P], w_x[:, d, N:2 * N]) for d in range(CT)])
                mm.then_inc(mm_ready, 1)
                for d in range(CT):
                    for c in halves:
                        job = ("S", d, c)
                        free_bank(b, jobs_a, job)
                        product(bank_of(job), [(w_dt[:, k, d * P:(d + 1) * P], xc[:, k, c * HALF:(c + 1) * HALF])
                                               for k in range(CT)]).then_inc(mm_ready, 1)
                wait_freed(pe, b, ("B", 0, NH - 1))
                wait_freed(pe, b, ("S", CT - 1, NH - 1))

            def loop(b, bp, hf):
                if bp is not None:
                    wait_freed(pe, bp, ("CT", 0, NH - 1))
                    pe.wait_ge(dve_scaled, 6)
                    pe.wait_ge(mix_taken, bp * 2 + hf + 1)
                    for a in range(TH):
                        tok = slice((hf * TH + a) * P, (hf * TH + a + 1) * P)
                        pe.matmul(ps[:, 6 + a // 2, (a % 2) * D:(a % 2 + 1) * D], rows[32:32 + E, tok], bias2[32:32 + E, :],
                                  start=(a % 2 == 0), stop=True, skip_group_check=True)
                with pe.Fori(0, ITS) as it:
                    for par in range(2):
                        for c in halves:
                            if bp is not None:
                                s = unit(bp, hf, it, par, c)
                                wcol = (it * 2 + par) * (DK * 2 * I) + c * P
                                for g, taken in ((0, g_ready), (1, l_ready)):
                                    pe.wait_ge(taken, s + 1)
                                    for k in range(DK):
                                        mm = pe.matmul(ps[:, 4 + g, :],
                                                       w1[:, bass.ds(wcol + (k * 2 * I + g * I), P)],
                                                       nfT[:, k, hf * HALF:(hf + 1) * HALF],
                                                       start=(k == 0), stop=(k == DK - 1))
                                    mm.then_inc(p1_ready, 1)
                            if b is not None:
                                u = unit(b, hf, it, par, c)
                                pe.wait_ge(scan_done, u * CT + CT + SCAN_CREDIT)
                                for a in range(TH):
                                    pe.wait_ge(hT_used, u * TH + a + 1)
                                    for d in range(CT):
                                        mm = pe.transpose(ps[:, 2 + a % 2, d * P:(d + 1) * P],
                                                          h[:, c, d, a * P:(a + 1) * P], ident[:, :])
                                    mm.then_inc(hT_ready, 1)
                            if bp is not None:
                                pe.wait_ge(aw_ready, s + 1 + AW_CREDIT)
                                for a in range(TH):
                                    mm = pe.matmul(ps[:, 6 + a // 2, (a % 2) * D:(a % 2 + 1) * D],
                                                   ex_a[:, c, a * P:(a + 1) * P],
                                                   w2[:, bass.ds((it * 2 + par) * (2 * D) + c * D, D)],
                                                   start=False, stop=True, skip_group_check=True)
                                mm.then_inc(p2_ready, 1)

            def phase_c(b):
                pe.wait_ge(hT_used, unit(b, 1, ITS - 1, 1, 1) * TH + TH + HT_CREDIT)
                if not isinstance(b, int):
                    pe.wait_ge(mix_taken, b * 2 + 1)
                for job in jobs_c[0:8]:
                    _, d, c = job
                    product(bank_of(job), [(w_in[:, k, DI + d * P:DI + (d + 1) * P], xnT[:, k, c * HALF:(c + 1) * HALF])
                                           for k in range(DK)]).then_inc(mm_ready, 1)
                for job in jobs_c[8:16]:
                    _, d, c = job
                    free_bank(b, jobs_c, job)
                    for a in range(TH):
                        mm = pe.transpose(bank_of(job)[:, a * P:(a + 1) * P],
                                          stage[:, c * TH + a, d * P:(d + 1) * P], ident[:, :])
                    mm.then_inc(mm_ready, 1)
                if isinstance(b, int):
                    pe.wait_ge(act_scaled, 3)
                for a in range(TT):
                    job = ("O", a, 0)
                    free_bank(b, jobs_c, job)
                    pe.wait_ge(gated, b * CT * NH + CT * NH)
                    product(bank_of(job)[:, 0:D], [(xc[:, d, a * P:(a + 1) * P], w_out[:, d, :])
                                                   for d in range(CT)]).then_inc(mm_ready, 1)
                for c in halves:
                    pe.wait_ge(xn_ready, b * 2 * TT + TT + (c + 1) * TH)
                    for k in range(DK):
                        free_bank(b, jobs_c, ("T2", k, c))
                        transposes(b, ("T2", k, c), xn, ident, 1).then_inc(mm_ready, 1)
                pe.wait_ge(kv_loaded, b * 48 + 48)
                for a in range(TT):
                    job = ("Q", a, 0)
                    free_bank(b, jobs_c, job)
                    wait_freed(pe, b, ("T2", DK - 1, a // TH))
                    tok = slice(a * P, (a + 1) * P)
                    dst = bank_of(job)[:, 0:LK]
                    for k in range(DK):
                        pe.matmul(dst, xnT[:, k, tok], kq[:, k, :], start=(k == 0), stop=False)
                    pe.matmul(dst, ones[0:1, :], rows[0:1, 0:LK],
                              start=False, stop=True).then_inc(mm_ready, 1)
                for c in halves:
                    pe.wait_ge(probs_ready, b * TT + (c + 1) * TH)
                    for k in range(2):
                        job = ("PT", k, c)
                        free_bank(b, jobs_c, job)
                        for a in range(TH):
                            mm = pe.transpose(bank_of(job)[0:KEYS, a * P:(a + 1) * P],
                                              probs[:, c * TH + a, k * KEYS:(k + 1) * KEYS], ident[:, :])
                        mm.then_inc(mm_ready, 1)
                for a in range(TT):
                    job = ("V", a, 0)
                    free_bank(b, jobs_c, job)
                    wait_freed(pe, b, ("PT", 1, a // TH))
                    tok = slice(a * P, (a + 1) * P)
                    dst = bank_of(job)[:, 0:D]
                    for k in range(DK):
                        pe.matmul(dst, xnT[:, k, tok], w_qo[:, k, :], start=(k == 0), stop=False)
                    for k in range(2):
                        mm = pe.matmul(dst, probsT[0:KEYS, k, tok], vo[:, k, :],
                                       start=False, stop=(k == 1))
                    mm.then_inc(mm_ready, 1)
                for c in halves:
                    pe.wait_ge(nf_ready, b * TT + (c + 1) * TH)
                    for k in range(DK):
                        job = ("N", k, c)
                        free_bank(b, jobs_c, job)
                        bank = bank_of(job).bitcast(BF16)
                        for a in range(TH):
                            mm = pe.transpose(bank[:, a * P:(a + 1) * P],
                                              nf[:, c * TH + a, k * P:(k + 1) * P], ident16[:, :])
                        mm.then_inc(mm_ready, 1)
                job = ("G", 0, 0)
                free_bank(b, jobs_c, job)
                wait_freed(pe, b, ("N", DK - 1, NH - 1))
                if isinstance(b, int):
                    pe.wait_ge(w_late, 7 * 16)
                for a in range(TT):
                    mm = product(bank_of(job)[:, a * E:(a + 1) * E],
                                 [(nfT[:, k, a * P:(a + 1) * P], gate_w[:, k, :]) for k in range(DK)])
                mm.then_inc(mm_ready, 1)
                pe.wait_ge(comb_ready, b + 1)
                for c in halves:
                    job = ("CT", 0, c)
                    free_bank(b, jobs_c, job)
                    for a in range(TH):
                        mm = pe.transpose(bank_of(job)[0:E, a * P:(a + 1) * P], comb[:, c * TH + a, :], ident[:, :])
                    mm.then_inc(mm_ready, 1)

            over_rows(pe, phase_a, loop, phase_c)


def kernel(**inputs):
    import concourse.bacc as bacc
    import numpy as np
    from concourse.bass_utils import run_bass_kernel_spmd

    v = {name: np.asarray(a) for name, a in inputs.items()}
    attn, cross, ffn = "L0_attn_", "L0_xattn_", "L0_ffn_"
    E, I2, D = v[ffn + "mlp1_weight"].shape
    w1 = v[ffn + "mlp1_weight"].reshape(E, I2 // 2, 2, D).transpose(0, 3, 2, 1).reshape(E, D, I2)
    b1 = v[ffn + "mlp1_bias"].reshape(E, I2 // 256, 128, 2).transpose(2, 0, 3, 1).reshape(128, E * I2 // 128)
    laid = {
        "x": v["x"], "ctxT": v["ctx_1024"].transpose(2, 0, 1).reshape(D, -1),
        "W_in": v[attn + "W_in"], "conv_w": v[attn + "conv_w"], "conv_b": v[attn + "conv_b"],
        "W_x": v[attn + "W_x"], "W_dt": v[attn + "W_dt"], "b_dt": v[attn + "b_dt"],
        "A_log": v[attn + "A_log"], "D_skip": v[attn + "D"], "W_out": v[attn + "W_out"],
        "hW": v[cross + "hW"], "qWT": v[cross + "qW"].T, "cWT": v[cross + "cW"].T, "kWT": v[cross + "kW"].T,
        "vWT": v[cross + "vW"].T, "oWT": v[cross + "oW"].T,
        "hb": v[cross + "hb"], "qb": v[cross + "qb"], "cb": v[cross + "cb"], "kb": v[cross + "kb"],
        "vb": v[cross + "vb"], "ob": v[cross + "ob"],
        "norm_w": v[ffn + "norm_weight"], "gate_wT": v[ffn + "gate_weight"].T,
        "gate_b": v[ffn + "gate_bias"].reshape(1, E), "mlp1_wT": w1, "mlp1_bT": b1,
        "mlp2_wT": v[ffn + "mlp2_weight"].transpose(0, 2, 1), "mlp2_b": v[ffn + "mlp2_bias"],
    }
    laid = {name: np.ascontiguousarray(a) for name, a in laid.items()}
    nc = bacc.Bacc("TRN2", target_bir_lowering=False, num_devices=1)
    t = {name: nc.dram_tensor(f"in_{name}", a.shape, mybir.dt.from_np(a.dtype), kind="ExternalInput").ap()
         for name, a in laid.items()}
    out = nc.dram_tensor("out_x", v["x"].shape, F32, kind="ExternalOutput").ap()
    decoder_layer(nc, t, out)
    r = run_bass_kernel_spmd(nc, [{f"in_{name}": a for name, a in laid.items()}], core_ids=[0])
    return r.results[0]["out_x"]
```

```python
from contextlib import ExitStack

import concourse.bass as bass
from concourse import mybir

F32 = mybir.dt.float32
BF16 = mybir.dt.bfloat16
U32 = mybir.dt.uint32
ACT = mybir.ActivationFunctionType
ALU = mybir.AluOpType
AX_X = mybir.AxisListType.X

P = 128
HALF = 512
EPS = 1e-5
LIMIT = 7.0
ALPHA = 1.702
STEP_CAP = 30.0


def decoder_layer(nc, t, out):
    B, S, D = t["x"].shape
    DI = t["W_dt"].shape[0]
    N = t["A_log"].shape[1]
    KTAPS = t["conv_w"].shape[1]
    PAD = KTAPS - 1
    E = t["gate_wT"].shape[1]
    I = t["mlp2_wT"].shape[1]
    LK = t["ctxT"].shape[1] // B
    DK, CT, TT = D // P, DI // P, S // P
    NH = S // HALF
    TH = TT // NH
    KEYS = LK // 2
    ALLK = B * LK
    assert NH == 2 and DK == 2 and I == 2 * P and LK % 2 == 0 and KEYS <= P and E * NH == N

    bd = nc.dram_tensor("b_rows", (B * N, S), F32, kind="Internal").ap()
    combd = nc.dram_tensor("combine_rows", (B * E, S), F32, kind="Internal").ap()
    kqd = nc.dram_tensor("kq_rows", (B * P, DK * LK), F32, kind="Internal").ap()
    vod = nc.dram_tensor("vo_rows", (B * KEYS, 2 * D), F32, kind="Internal").ap()
    k_rowd = nc.dram_tensor("key_bias_rows", (B, LK), F32, kind="Internal").ap()
    x2d = nc.dram_tensor("x2_rows", (B * S, D), F32, kind="Internal").ap()
    x_rows = t["x"].rearrange("b s d -> (b s) d")
    out_rows = out.rearrange("b s d -> (b s) d")

    with ExitStack() as ctx:
        def sb(name, shape, dt=F32):
            return ctx.enter_context(nc.sbuf_tensor(name, shape, dt))

        def sem(name):
            return ctx.enter_context(nc.semaphore(name))

        w_in = sb("w_in", [P, DK, 2 * DI])
        w_dt = sb("w_dt", [P, CT, DI])
        w_out = sb("w_out", [P, CT, D])
        w_x = sb("w_x", [P, CT, 2 * N])
        conv_w = sb("conv_w_sb", [P, CT, KTAPS])
        chan = sb("chan", [P, 3, CT])
        a_neg = sb("a_neg", [P, CT * N])
        w1 = sb("w1", [P, E * DK * 2 * I], BF16)
        w2 = sb("w2", [P, E * 2 * D])
        bias1 = sb("bias1", [P, E * 4])
        bias2 = sb("bias2", [64, D])
        gate_w = sb("gate_w", [P, DK, E], BF16)
        gate_b = sb("gate_b", [P, 1, E], BF16)
        norm_w = sb("norm_w", [P, D])
        kq = sb("kq", [P, DK, LK])
        vo = sb("vo", [KEYS, 2, D])
        w_qo = sb("w_qo", [P, DK, D])
        rows = sb("rows", [64, S])
        ident = sb("ident", [P, P])
        ident16 = sb("ident16", [P, P], BF16)
        ones = bias2[0:1, 0:P]
        minus_half = sb("minus_half", [P, TT])
        iota = sb("iota", [P, 1, E])
        shift = sb("shift", [P, 3])
        xt = sb("xt", [P, TT, D])
        xnT = sb("xnT", [P, DK, S])
        nfT = sb("nfT", [P, DK, S], BF16)
        xc = sb("xc", [P, CT, S])
        dt = sb("dt", [P, CT, S])
        dtu = sb("dtu", [P, CT, S])
        b_bc = sb("b_bc", [P, NH, HALF])
        c_tok = sb("c_tok", [P, TT, N])
        stage = sb("stage", [P, TT, DI])
        xn = stage
        xc16 = sb("xc16", [P, TT, D], BF16)
        work = sb("work", [P, 10240])
        wbc = sb("wbc", [P, 2, HALF])
        res = sb("res", [P, TH, D])
        mix = sb("mix", [P, TH * D], BF16)
        ve = sb("ve", [P, TT])
        rstd = sb("rstd", [P, TT])
        ssq = sb("ssq", [P, TT])
        mx = sb("mx", [P, TT])
        negm = sb("negm", [P, TT])
        rsum = sb("rsum", [P, TT])
        rinv = sb("rinv", [P, TT])

        h = work[:, 0:4096].rearrange("p (c d t) -> p c d t", c=2, d=CT)
        dbu = work[:, 4096:6144].rearrange("p (r t) -> p r t", r=4)
        ex_g = work[:, 6144:7168].rearrange("p (j t) -> p j t", j=2)
        ex_t = work[:, 7168:8192].rearrange("p (j t) -> p j t", j=2)
        ex_l = work[:, 8192:9216].rearrange("p (j t) -> p j t", j=2)
        ex_a = work[:, 9216:10240].rearrange("p (j t) -> p j t", j=2)
        xp = dtu[:, :, :].rearrange("p a s -> p (a s)")[:, 0:2 * (PAD + S)].rearrange("p (r s) -> p r s", r=2)
        soft = work[:, 0:CT * NH * HALF].rearrange("p (r t) -> p r t", r=CT * NH)
        bc_sb = work[0:2 * N, 4096:4096 + S]
        TANH_AT = 8192
        tanh = work[:, TANH_AT:TANH_AT + 2 * S].rearrange("p (r t) -> p r t", r=2)
        probs = work[:, 0:TT * LK].rearrange("p (a k) -> p a k", a=TT)
        probsT = work[:, 2048:4096].rearrange("p (k t) -> p k t", k=2)
        square = work[:, 4096:5120].bitcast(BF16).rearrange("p (a d) -> p a d", a=TT)
        nf = work[:, 5120:6144].bitcast(BF16).rearrange("p (a d) -> p a d", a=TT)
        o = [6144]

        def small(*shape):
            n = 1
            for extent in shape:
                n *= extent
            o[0] += n
            names = "abcd"[:len(shape)]
            return work[:, o[0] - n:o[0]].rearrange(
                f"p ({' '.join(names)}) -> p {' '.join(names)}", **dict(zip(names[:-1], shape)))

        lg16 = small(TT, E // 2).bitcast(BF16)
        lg, m8, i8f, comb = (small(TT, E) for _ in range(4))
        i8 = small(TT, 8).bitcast(U32)
        tw = small(4, TT)
        tden = small(1, TT)[:, 0, :]
        eq = small(2, TT, E)
        o = [0]

        def part(n):
            o[0] += n
            return work[:, o[0] - n:o[0]]

        qwT, cwT = (res[:, i * 2:i * 2 + 2, :] for i in range(2))
        kwT, vwT = (b_bc[:, i, :].rearrange("p (k f) -> p k f", k=DK) for i in range(2))
        owT = part(DK * D).rearrange("p (k f) -> p k f", k=DK)
        hwb = part(DK * (D + 1)).rearrange("p (k f) -> p k f", k=DK)
        wqh = part(DK * D).rearrange("p (k f) -> p k f", k=DK)
        ctxT, cT, kT = (part(DK * ALLK).rearrange("p (k f) -> p k f", k=DK) for _ in range(3))
        vT = ctxT
        fbias = part(4 * DK).rearrange("p (n k) -> p n k", n=4)
        bq = part(DK).rearrange("p (k n) -> p k n", n=1)
        o_row = part(D)
        ob_row = part(D)[0:1, :]
        a_log = part(CT * N)
        xc_flat = xc[:, :, :].rearrange("p a s -> p (a s)")
        stats = xc_flat[:, S:S + 6 * TT].rearrange("p (a n) -> p a n", n=6)
        mv = xc_flat[:, S + 6 * TT:S + 8 * TT].rearrange("p (a n) -> p a n", n=2)
        bias1_raw = wbc[:, 0, 0:E * 2].bitcast(BF16)
        bias2_raw = wbc[:, 1, 0:D // 2].bitcast(BF16)
        kq_all = part(DK * ALLK).rearrange("p (b k f) -> p b k f", b=B, k=DK)
        k_row = part(ALLK)[0:1, :]
        vo_all = dt[:, :, :].rearrange("p a s -> p (a s)")[0:KEYS, E * D:E * D + 2 * B * D]
        assert o[0] <= TANH_AT
        w2_raw = dt[:, :, :].rearrange("p a d -> p (a d)")[:, 0:E * D].bitcast(BF16)

        ps = ctx.enter_context(nc.psum_tensor("ps", [P, 8, HALF], F32))

        w_early = sem("w_early")
        w_fold = sem("w_fold")
        w_late = sem("w_late")
        passed = sem("passed")
        consts = sem("consts")
        shift_set = sem("shift_set")
        act_scaled = sem("act_scaled")
        dve_scaled = sem("dve_scaled")
        fold_ready = sem("fold_ready")
        fold_kept = sem("fold_kept")
        fold_stored = sem("fold_stored")
        kv_loaded = sem("kv_loaded")
        pad_ready = sem("pad_ready")
        x_in = [sem("x_in0"), sem("x_in1")]
        x2_stored = sem("x2_stored")
        b_stored = sem("b_stored")
        comb_stored = sem("comb_stored")
        b_loaded = [sem("b_loaded0"), sem("b_loaded1")]
        wbc_loaded = [sem("wbc_loaded0"), sem("wbc_loaded1")]
        res_loaded = sem("res_loaded")
        out_stored = sem("out_stored")
        chain = sem("chain")
        ve_ready = sem("ve_ready")
        rstd_ready = sem("rstd_ready")
        xn_ready = sem("xn_ready")
        mm_ready = sem("mm_ready")
        act_freed = sem("act_freed")
        dve_freed = sem("dve_freed")
        conv_done = sem("conv_done")
        tanh_done = sem("tanh_done")
        xc_ready = sem("xc_ready")
        cap_ready = sem("cap_ready")
        soft_exp = sem("soft_exp")
        soft_ready = sem("soft_ready")
        dtu_ready = sem("dtu_ready")
        exp_ready = sem("exp_ready")
        dbu_ready = sem("dbu_ready")
        scan_done = sem("scan_done")
        hT_ready = sem("hT_ready")
        hT_used = sem("hT_used")
        p1_ready = sem("p1_ready")
        g_ready = sem("g_ready")
        l_ready = sem("l_ready")
        t_ready = sem("t_ready")
        neg_ready = sem("neg_ready")
        lin_ready = sem("lin_ready")
        u_ready = sem("u_ready")
        a_ready = sem("a_ready")
        aw_ready = sem("aw_ready")
        p2_ready = sem("p2_ready")
        mix_taken = sem("mix_taken")
        out_ready = sem("out_ready")
        gate_tanh = sem("gate_tanh")
        gated = sem("gated")
        negm_ready = sem("negm_ready")
        exp_probs = sem("exp_probs")
        probs_ready = sem("probs_ready")
        x16_ready = sem("x16_ready")
        ssq_ready = sem("ssq_ready")
        nf_ready = sem("nf_ready")
        gap_ready = sem("gap_ready")
        gap_exp = sem("gap_exp")
        comb_ready = sem("comb_ready")
        mix_added = sem("mix_added")

        halves = range(NH)
        jobs_a = ([("T", k, c) for c in halves for k in range(DK)] +
                  [("X", d, c) for d in range(CT) for c in halves] +
                  [("B", 0, c) for c in halves] + [("C", 0, 0)] +
                  [("S", d, c) for d in range(CT) for c in halves])
        jobs_c = ([("Z", d, c) for d in range(CT) for c in halves] +
                  [("Y", d, c) for d in range(CT) for c in halves] +
                  [("O", a, 0) for a in range(TT)] +
                  [("T2", k, c) for c in halves for k in range(DK)] +
                  [("Q", a, 0) for a in range(TT)] +
                  [("PT", k, c) for c in halves for k in range(2)] +
                  [("V", a, 0) for a in range(TT)] +
                  [("N", k, c) for c in halves for k in range(DK)] + [("G", 0, 0)] +
                  [("CT", 0, c) for c in halves])
        jobs_s = jobs_a[-CT * NH:]
        BATCH = CT * NH - 2
        by_act = ("T", "X", "B", "T2", "Q", "PT", "N", "CT")
        n_jobs = len(jobs_a) + len(jobs_c)
        n_freed = {True: 0, False: 0}
        index, freed = {}, {}
        for i, job in enumerate(jobs_a + jobs_c):
            mine = job[0] in by_act
            n_freed[mine] += 1
            index[job], freed[job] = i + 1, (mine, n_freed[mine])

        def wait_apart(eng, sem, value):
            eng.wait_ge(sem, value)
            eng.sem_inc(passed, 1)

        def wait_mm(eng, b, job):
            eng.wait_ge(mm_ready, b * n_jobs + index[job])

        def wait_freed(eng, b, job):
            mine, n = freed[job]
            eng.wait_ge(act_freed if mine else dve_freed, b * n_freed[mine] + n)

        def bank_of(job):
            jobs = jobs_a if job in jobs_a else jobs_c
            return ps[:, jobs.index(job) % 8, :]

        FOLD_LOADS = 6 + 1 + 1 + 4
        fold_jobs = ([("WQH", k, 0) for k in range(DK)] + [("c", k, c) for k in range(DK) for c in range(2)] +
                     [("k", k, c) for k in range(DK) for c in range(2)] +
                     [("v", k, c) for k in range(DK) for c in range(2)] +
                     [("KQ", k, c) for k in range(DK) for c in range(2)] +
                     [("KROW", 0, c) for c in range(2)] + [("WQO", k, 0) for k in range(DK)] +
                     [("OROW", 0, 0)] + [("VO", i, 0) for i in range(2 * B)])
        KCH = ALLK // 2
        assert KCH <= HALF

        FOLD_BANK = 4 + CT * NH

        def fold_at(job):
            return fold_jobs.index(job) + 1

        units_row = N * NH

        def unit(b, hf, it, par, c):
            return b * units_row + hf * (units_row // 2) + it * 4 + par * 2 + c

        def state(b, hf, it, par):
            return b * N + hf * (N // 2) + it * 2 + par

        ITS = N // 4
        DBU_CREDIT, SCAN_CREDIT, HT_CREDIT, AW_CREDIT, A_CREDIT, P2_CREDIT = 8, 4, 2, 4, 2, 4

        def windows(eng, body):
            for hf in range(2):
                for par in range(2):
                    for c in range(NH):
                        body(hf, 0, par, c, par == 0 and c == 0)
                with eng.Fori(1, ITS) as it:
                    for par in range(2):
                        for c in range(NH):
                            body(hf, it, par, c, False)

        STORE_CREDIT = 16

        block = ctx.enter_context(nc.Block())

        def over_rows(eng, phase_a, loop, phase_c):
            phase_a(0)
            loop(0, None)
            phase_c(0)
            with eng.Fori(1, B) as b:
                phase_a(b)
                loop(b, b - 1)
                phase_c(b)
            loop(None, B - 1)

        @block.sync
        def _(sp):
            def load_x(b):
                for c in halves:
                    sp.dma_start(xt[:, c * TH:(c + 1) * TH, :],
                                 x_rows[bass.ds(b * S + c * HALF, HALF), :].rearrange("(a p) d -> p a d", p=P)
                                 ).then_inc(x_in[c], 16)

            load_x(0)
            for dst, name in ((w_in, "W_in"), (w_x, "W_x"), (w_dt, "W_dt"), (w_out, "W_out")):
                sp.dma_start(dst[:, :, :], t[name].rearrange("(k p) n -> p k n", p=P)).then_inc(w_early, 16)
            sp.dma_start(conv_w[:, :, :], t["conv_w"].rearrange("(k p) n -> p k n", p=P)).then_inc(w_early, 16)
            for i, name in enumerate(("conv_b", "b_dt", "D_skip")):
                sp.dma_start(chan[:, i, :], t[name].rearrange("(k p) -> p k", p=P),
                             allow_slow_non_contiguous=True).then_inc(w_early, 16)
            sp.dma_start(a_log.rearrange("p (k n) -> p k n", n=N),
                         t["A_log"].rearrange("(k p) n -> p k n", p=P)).then_inc(w_early, 16)
            sp.dma_start(w2_raw.rearrange("p (e k f) -> p e k f", e=E, k=2),
                         t["mlp2_wT"].rearrange("e (k p) f -> p e k f", p=P)).then_inc(w_late, 16)
            sp.dma_start(w1[:, :].rearrange("p (e k f) -> p e k f", e=E, k=DK),
                         t["mlp1_wT"].rearrange("e (k p) f -> p e k f", p=P)).then_inc(w_late, 16)
            sp.dma_start(bias1_raw[:, :], t["mlp1_bT"]).then_inc(w_late, 16)
            sp.dma_start(bias2_raw[32:32 + E, :], t["mlp2_b"]).then_inc(w_late, 16)
            sp.dma_start(gate_w[:, :, :], t["gate_wT"].rearrange("(k p) e -> p k e", p=P)).then_inc(w_late, 16)
            sp.dma_start(gate_b[:, :, :], t["gate_b"].partition_broadcast(P)).then_inc(w_late, 16)
            sp.dma_start(norm_w[:, :], t["norm_w"].partition_broadcast(P)).then_inc(w_late, 16)

            sp.wait_ge(fold_kept, len(fold_jobs))
            sp.dma_start(kqd.rearrange("(b p) (k f) -> p b k f", p=P, k=DK), kq_all).then_inc(fold_stored, 16)
            sp.dma_start(vod.rearrange("(b p) f -> p b f", p=KEYS),
                         vo_all.rearrange("p (b f) -> p b f", b=B)).then_inc(fold_stored, 16)
            sp.dma_start(k_rowd.rearrange("b (o f) -> o b f", o=1), k_row.rearrange("o (b f) -> o b f", b=B)
                         ).then_inc(fold_stored, 16)
            sp.wait_ge(fold_stored, 3 * 16)

            def phase_a(b):
                if not isinstance(b, int):
                    wait_apart(sp, x2_stored, b * 16)
                    wait_apart(sp, x16_ready, b * TT)
                    load_x(b)
                sp.dma_start(kq[:, :, :], kqd[bass.ds(b * P, P), :].rearrange("p (k f) -> p k f", k=DK)
                             ).then_inc(kv_loaded, 16)
                sp.dma_start(vo[:, :, :], vod[bass.ds(b * KEYS, KEYS), :].rearrange("p (k f) -> p k f", k=2)
                             ).then_inc(kv_loaded, 16)
                sp.dma_start(rows[0:1, 0:LK], k_rowd[bass.ds(b, 1), :]).then_inc(kv_loaded, 16)
                wait_freed(sp, b, ("B", 0, NH - 1))
                sp.dma_start(bd[bass.ds(b * N, N), :], bc_sb[0:N, :]).then_inc(b_stored, 16)
                wait_apart(sp, b_stored, b * 16 + 16)

            def loop(b, bp):
                def load_res(hf):
                    wait_apart(sp, out_stored, (bp * 2 + hf) * 16 + STORE_CREDIT)
                    sp.dma_start(res[:, :, :],
                                 x2d[bass.ds(bp * S + hf * HALF, HALF), :].rearrange("(a p) d -> p a d", p=P)
                                 ).then_inc(res_loaded, 16)

                def store_out(hf):
                    wait_apart(sp, out_ready, bp * 2 + hf + 1)
                    sp.dma_start(out_rows[bass.ds(bp * S + hf * HALF, HALF), :].rearrange("(a p) d -> p a d", p=P),
                                 res[:, :, :]).then_inc(out_stored, 16)

                if bp is not None:
                    load_res(0)
                for hf in range(2):
                    with sp.Fori(0, ITS) as it:
                        for par in range(2):
                            if b is not None:
                                for c in halves:
                                    wait_apart(sp, dbu_ready, unit(b, hf, it, par, c) * CT + CT)
                                    sp.dma_start(b_bc[:, c:c + 1, :],
                                                 bd[bass.ds(state(b, hf, it, par), 1),
                                                    c * HALF:(c + 1) * HALF].partition_broadcast(P)
                                                 ).then_inc(b_loaded[c], 16)
                            if bp is not None:
                                wait_apart(sp, aw_ready, state(bp, hf, it, par) * 2 + 2)
                                sp.dma_start(wbc[:, par:par + 1, :],
                                             combd[bass.ds(bp * E + it * 2 + par, 1),
                                                   hf * HALF:(hf + 1) * HALF].partition_broadcast(P)
                                             ).then_inc(wbc_loaded[par], 16)
                if bp is not None:
                    store_out(0)
                    load_res(1)
                    store_out(1)

            def phase_c(b):
                wait_freed(sp, b, ("V", TT - 1, 0))
                sp.dma_start(x2d[bass.ds(b * S, S), :].rearrange("(a p) d -> p a d", p=P),
                             xt[:, :, :]).then_inc(x2_stored, 16)
                wait_freed(sp, b, ("CT", 0, NH - 1))
                sp.dma_start(combd[bass.ds(b * E, E), :], rows[32:32 + E, :]).then_inc(comb_stored, 16)
                wait_apart(sp, comb_stored, b * 16 + 16)
                wait_apart(sp, x2_stored, b * 16 + 16)

            sp.sem_inc(out_stored, STORE_CREDIT)
            over_rows(sp, phase_a, loop, phase_c)
            sp.wait_ge(out_stored, B * 2 * 16 + STORE_CREDIT)

        @block.gpsimd
        def _(pool):
            pool.sem_inc(dbu_ready, DBU_CREDIT)
            pool.sem_inc(aw_ready, AW_CREDIT)
            for i, value in enumerate((-LIMIT, ALPHA / 2 * LIMIT, 2 * LIMIT)):
                pool.memset(shift[:, i:i + 1], value).then_inc(shift_set, 1)
            pool.memset(ident[:, :], 0.0).then_inc(consts, 1)
            pool.memset(ones, 1.0).then_inc(consts, 1)
            pool.memset(minus_half[:, :], -0.5).then_inc(consts, 1)
            pool.iota(iota[:, 0, :], [[1, E]], base=0, channel_multiplier=0,
                      allow_small_or_imprecise_dtypes=True).then_inc(consts, 1)
            pool.wait_ge(consts, 1)
            pool.affine_select(out=ident[:, :], in_=ident[:, :], compare_op=ALU.not_equal, fill=1.0, base=0,
                               pattern=[[-1, P]], channel_multiplier=1).then_inc(consts, 1)
            pool.wait_ge(consts, 5)
            pool.tensor_copy(ident16[:, :], ident[:, :]).then_inc(consts, 1)

            def norm_scale(n):
                pool.wait_ge(ve_ready, n + 1)
                pool.tensor_tensor(rstd[:, :], ve[:, :], minus_half[:, :], ALU.pow).then_inc(rstd_ready, 1)

            def phase_a(b):
                norm_scale(b * 4)
                pool.memset(xp[:, :, 0:PAD], 0.0).then_inc(pad_ready, 1)
                for _, d, c in jobs_s[0:BATCH]:
                        wait_freed(pool, b, ("S", d, c))
                        cols = slice(c * HALF, (c + 1) * HALF)
                        pool.tensor_tensor(dtu[:, d, cols], dt[:, d, cols], xc[:, d, cols],
                                           ALU.mult).then_inc(dtu_ready, 1)

            def loop(b, bp):
                def weigh(hf, it, par, c):
                    s = unit(bp, hf, it, par, c)
                    if c == 0:
                        pool.wait_ge(wbc_loaded[1 - par], (bp * 2 * ITS + hf * ITS + it) * 16 + 16 * par)
                    wait_apart(pool, p2_ready, s - 3 + P2_CREDIT)
                    pool.wait_ge(a_ready, s - 1 + A_CREDIT)
                    pool.tensor_tensor(ex_a[:, c, :], ex_l[:, c, :], wbc[:, 1 - par, :],
                                       ALU.mult).then_inc(aw_ready, 1)

                def body(hf, it, par, c, first):
                    if b is not None:
                        pool.wait_ge(b_loaded[c], state(b, hf, it, par) * 16 + 16)
                        pool.wait_ge(dtu_ready, b * CT * NH + CT * NH)
                        for d in range(CT):
                            pool.wait_ge(scan_done, unit(b, hf, it, par, c) * CT + d + 1)
                            pool.tensor_tensor(dbu[:, d, :], dtu[:, d, c * HALF:(c + 1) * HALF],
                                               b_bc[:, c, :], ALU.mult).then_inc(dbu_ready, 1)
                            if d == 0 and bp is not None and started[0] >= 2:
                                weigh(hf, it, par, c)
                    elif started[0] >= 2:
                        weigh(hf, it, par, c)
                    started[0] += 1

                started = [0]
                windows(pool, body)
                if bp is not None:
                    for c in range(NH):
                        weigh(1, ITS, 0, c)

            def phase_c(b):
                for d in range(CT):
                    for c in halves:
                        wait_freed(pool, b, ("Y", d, c))
                        cols = slice(c * HALF, (c + 1) * HALF)
                        pool.tensor_tensor(xc[:, d, cols], xc[:, d, cols], dt[:, d, cols],
                                           ALU.mult).then_inc(gated, 1)
                norm_scale(b * 4 + 1)
                norm_scale(b * 4 + 2)
                norm_scale(b * 4 + 3)

            over_rows(pool, phase_a, loop, phase_c)

        @block.scalar
        def _(act):
            act.sem_inc(g_ready, 1)
            act.sem_inc(l_ready, 1)
            for dst, name in ((qwT, "qWT"), (cwT, "cWT"), (kwT, "kWT"), (vwT, "vWT"), (owT, "oWT")):
                act.dma_start(dst, t[name].rearrange("(k p) f -> p k f", p=P)).then_inc(w_fold, 16)
            act.dma_start(hwb[:, :, 0:D], t["hW"].rearrange("(k p) f -> p k f", p=P)).then_inc(w_fold, 16)
            act.dma_start(hwb[:, :, D:D + 1], t["hb"].rearrange("(k p o) -> p k o", p=P, o=1),
                          allow_slow_non_contiguous=True).then_inc(w_fold, 16)
            act.dma_start(ctxT, t["ctxT"].rearrange("(k p) f -> p k f", p=P)).then_inc(w_fold, 16)
            for i, name in enumerate(("qb", "cb", "kb", "vb")):
                act.dma_start(fbias[:, i, :], t[name].rearrange("(k p) -> p k", p=P),
                              allow_slow_non_contiguous=True).then_inc(w_fold, 16)
            act.dma_start(ob_row, t["ob"].rearrange("(a f) -> a f", a=1)).then_inc(w_fold, 16)

            act.wait_ge(w_early, 9 * 16)
            act.activation(a_neg[:, :], a_log, ACT.Exp).then_inc(act_scaled, 1)
            act.wait_ge(act_scaled, 1)
            act.activation(a_neg[:, :], a_neg[:, :], ACT.Copy, scale=-1.0).then_inc(act_scaled, 1)
            act.activation(w_out[:, :, :], w_out[:, :, :], ACT.Copy, scale=0.5).then_inc(act_scaled, 1)

            def keep_folded(first, last_one):
                act.wait_ge(w_fold, (FOLD_LOADS + 1) * 16)
                for i in range(first, min(last_one, len(fold_jobs))):
                    what, k, c = fold_jobs[i]
                    bank = ps[:, (FOLD_BANK + i) % 8, :]
                    keys = slice(c * KCH, (c + 1) * KCH)
                    act.wait_ge(fold_ready, i + 1)
                    if what == "WQH":
                        act.activation(wqh[:, k, :], bank[:, 0:D], ACT.Copy)
                        last = act.activation(bq[:, k, :], bank[:, D:D + 1], ACT.Identity, bias=fbias[:, 0, k:k + 1])
                    elif what in "ckv":
                        dst = {"c": cT, "k": kT, "v": vT}[what]
                        last = act.activation(dst[:, k, keys], bank[:, 0:KCH], ACT.Identity,
                                              bias=fbias[:, 1 + "ckv".index(what), k:k + 1])
                    elif what == "KQ":
                        last = act.activation(kq_all[:, c * (B // 2):(c + 1) * (B // 2), k, :],
                                              bank[:, 0:KCH].rearrange("p (b f) -> p b f", b=B // 2), ACT.Copy)
                    elif what == "KROW":
                        last = act.activation(k_row[:, keys], bank[0:1, 0:KCH], ACT.Copy)
                    elif what == "WQO":
                        last = act.activation(w_qo[:, k, :], bank[:, 0:D], ACT.Copy)
                    elif what == "OROW":
                        last = act.activation(o_row[0:1, :], bank[0:1, 0:D], ACT.Copy)
                    else:
                        last = act.activation(vo_all[:, k * D:(k + 1) * D], bank[0:KEYS, 0:D], ACT.Copy)
                    last.then_inc(fold_kept, 1)

            def phase_a(b):
                for job in jobs_a[0:4]:
                    _, k, c = job
                    wait_mm(act, b, job)
                    act.activation(xnT[:, k, c * HALF:(c + 1) * HALF], bank_of(job), ACT.Copy
                                   ).then_inc(act_freed, 1)

                def conv_in(d):
                    for c in halves:
                        wait_mm(act, b, ("X", d, c))
                        act.activation(xp[:, d % 2, PAD + c * HALF:PAD + (c + 1) * HALF],
                                       bank_of(("X", d, c)), ACT.Copy).then_inc(act_freed, 1)

                def silu_tanh(d):
                    act.wait_ge(conv_done, b * CT * KTAPS + (d + 1) * KTAPS)
                    act.activation(tanh[:, d % 2, :], xc[:, d, :], ACT.Tanh).then_inc(tanh_done, 1)

                conv_in(0)
                conv_in(1)
                for d in range(CT):
                    silu_tanh(d)
                    if d + 2 < CT:
                        conv_in(d + 2)
                    if isinstance(b, int) and d:
                        keep_folded((d - 1) * 8, d * 8 if d < CT - 1 else len(fold_jobs))
                if isinstance(b, int):
                    act.wait_ge(fold_stored, 3 * 16)
                for c in halves:
                    wait_mm(act, b, ("B", 0, c))
                    act.activation(bc_sb[:, c * HALF:(c + 1) * HALF], bank_of(("B", 0, c))[0:2 * N, :], ACT.Copy
                                   ).then_inc(act_freed, 1)
                for batch in (range(BATCH), range(BATCH, CT * NH)):
                    for i in batch:
                        act.wait_ge(cap_ready, b * CT * NH + i + 1)
                        act.activation(soft[:, i, :], soft[:, i, :], ACT.Exp).then_inc(soft_exp, 1)
                    for i in batch:
                        act.wait_ge(soft_exp, b * CT * NH + i + 1)
                        act.activation(soft[:, i, :], soft[:, i, :], ACT.Ln, bias=1.0).then_inc(soft_ready, 1)
                wait_freed(act, b, ("S", CT - 1, NH - 1))

            def loop(b, bp):
                if bp is not None:
                    act.wait_ge(shift_set, 3)
                    act.wait_ge(dve_scaled, 5)

                def body(hf, it, par, c):
                    def decay(d):
                        wait_apart(act, scan_done, unit(b, hf, it, par, c) * CT + d + 3)
                        act.activation(ps[:, d % 2, :], dt[:, d, c * HALF:(c + 1) * HALF], ACT.Exp,
                                       scale=a_neg[:, bass.ds(it * 2 + (d * N + hf * (N // 2) + par), 1)]
                                       ).then_inc(exp_ready, 1)

                    def gate_in():
                        wait_apart(act, a_ready, s - 1 + A_CREDIT)
                        wait_apart(act, p1_ready, s * 2 + 1)
                        act.activation(ex_g[:, c, :], ps[:, 4, :], ACT.Relu, scale=-1.0,
                                       bias=bias1[:, bass.ds(col, 1)]).then_inc(g_ready, 1)

                    def linear_in():
                        wait_apart(act, aw_ready, s - 1 + AW_CREDIT)
                        wait_apart(act, p1_ready, s * 2 + 2)
                        act.activation(ex_l[:, c, :], ps[:, 5, :], ACT.Relu, scale=-1.0,
                                       bias=bias1[:, bass.ds(col + 2, 1)]).then_inc(l_ready, 1)

                    def gate_tanh_():
                        wait_apart(act, g_ready, s + 2)
                        act.activation(ex_t[:, c, :], ex_g[:, c, :], ACT.Tanh, scale=-ALPHA / 2,
                                       bias=shift[:, 1:2]).then_inc(t_ready, 1)

                    def negated():
                        wait_apart(act, t_ready, s + 1)
                        act.activation(ex_g[:, c, :], ex_g[:, c, :], ACT.Identity, bias=shift[:, 0:1]
                                       ).then_inc(neg_ready, 1)

                    def linear():
                        wait_apart(act, l_ready, s + 2)
                        act.activation(ex_l[:, c, :], ex_l[:, c, :], ACT.Relu, scale=-1.0,
                                       bias=shift[:, 2:3]).then_inc(lin_ready, 1)

                    if bp is not None:
                        s = unit(bp, hf, it, par, c)
                        col = it * 8 + (par * 4 + c)
                    expert = (gate_in, linear_in, gate_tanh_, negated, linear) if bp is not None else ()
                    if b is not None:
                        decay(0)
                        decay(1)
                    for step in expert[0:2]:
                        step()
                    if b is not None:
                        decay(2)
                    for step in expert[2:3]:
                        step()
                    if b is not None:
                        decay(3)
                        for step in expert[3:5]:
                            step()

                for hf in range(2):
                    with act.Fori(0, ITS) as it:
                        for par in range(2):
                            for c in halves:
                                body(hf, it, par, c)

            def phase_c(b):
                for i, (_, d, c) in enumerate(jobs_c[0:8]):
                    job = ("Z", d, c)
                    wait_mm(act, b, job)
                    act.activation(dt[:, d, c * HALF:(c + 1) * HALF], bank_of(job), ACT.Tanh, scale=0.5
                                   ).then_inc(gate_tanh, 1)
                for c in halves:
                    for k in range(DK):
                        wait_mm(act, b, ("T2", k, c))
                        act.activation(xnT[:, k, c * HALF:(c + 1) * HALF], bank_of(("T2", k, c)), ACT.Copy
                                       ).then_inc(act_freed, 1)
                for a in range(TT):
                    act.wait_ge(negm_ready, b * TT + a + 1)
                    act.activation(probs[:, a, :], bank_of(("Q", a, 0))[:, 0:LK], ACT.Exp, scale=float(D) ** -0.5,
                                   bias=negm[:, a:a + 1], accum_out=rsum[:, a:a + 1]).then_inc(act_freed, 1)
                for c in halves:
                    for k in range(2):
                        wait_mm(act, b, ("PT", k, c))
                        act.activation(probsT[0:KEYS, k, c * HALF:(c + 1) * HALF],
                                       bank_of(("PT", k, c))[0:KEYS, :], ACT.Copy).then_inc(act_freed, 1)
                for a in range(TT):
                    act.wait_ge(x16_ready, b * TT + a + 1)
                    act.activation(square[:, a, :], xc16[:, a, :], ACT.Square, accum_out=ssq[:, a:a + 1]
                                   ).then_inc(ssq_ready, 1)
                for c in halves:
                    for k in range(DK):
                        wait_mm(act, b, ("N", k, c))
                        act.activation(nfT[:, k, c * HALF:(c + 1) * HALF],
                                       bank_of(("N", k, c)).bitcast(BF16)[:, 0:HALF], ACT.Copy
                                       ).then_inc(act_freed, 1)
                act.wait_ge(gap_ready, b + 1)
                act.activation(tw[:, 1, :], tw[:, 0, :], ACT.Exp).then_inc(gap_exp, 1)
                for c in halves:
                    wait_mm(act, b, ("CT", 0, c))
                    act.activation(rows[32:32 + E, c * HALF:(c + 1) * HALF], bank_of(("CT", 0, c))[0:E, :], ACT.Copy
                                   ).then_inc(act_freed, 1)

            over_rows(act, phase_a, loop, phase_c)

        @block.vector
        def _(dve):
            links = [0]
            per_row = [0]

            def link(b, ins):
                links[0] += 1
                ins.then_inc(chain, 1)
                if isinstance(b, int):
                    dve.wait_ge(chain, links[0])
                else:
                    wait_apart(dve, chain, b * per_row[0] + links[0])

            dve.sem_inc(scan_done, SCAN_CREDIT)
            dve.sem_inc(hT_used, HT_CREDIT)
            dve.sem_inc(a_ready, A_CREDIT)
            dve.sem_inc(mix_taken, 1)

            def norm(b, n, dst, done):
                for a in range(TT):
                    if n == 0 and a % TH == 0:
                        dve.wait_ge(x_in[a // TH], b * 16 + 16)
                    ins = dve.bn_stats(stats[:, a, :], xt[:, a, :])
                link(b, ins)
                for a in range(TT):
                    ins = dve.bn_aggr(mv[:, a, :], stats[:, a, :])
                link(b, ins)
                dve.tensor_scalar(ve[:, :], mv[:, :, 1], EPS, None, ALU.add).then_inc(ve_ready, 1)
                dve.wait_ge(rstd_ready, b * 4 + n + 1)
                for a in range(TT):
                    dve.tensor_scalar(dst[:, a, 0:D], xt[:, a, :], mv[:, a, 0:1], rstd[:, a:a + 1],
                                      ALU.subtract, ALU.mult).then_inc(done, 1)

            def phase_a(b):
                links[0] = 0
                norm(b, 0, xn, xn_ready)
                if isinstance(b, int):
                    dve.wait_ge(w_early, 9 * 16)
                    dve.tensor_scalar(conv_w[:, :, :], conv_w[:, :, :], 0.5, None, ALU.mult).then_inc(dve_scaled, 1)
                    dve.tensor_scalar(chan[:, 0, :], chan[:, 0, :], 0.5, None, ALU.mult).then_inc(dve_scaled, 1)
                    dve.wait_ge(dve_scaled, 2)

                def convolve(d):
                    wait_freed(dve, b, ("X", d, NH - 1))
                    if d == 0:
                        dve.wait_ge(pad_ready, b + 1)
                    v, base = xc[:, d, :], b * CT * KTAPS + d * KTAPS
                    dve.tensor_scalar(v, xp[:, d % 2, 0:S], conv_w[:, d, 0:1], chan[:, 0, d:d + 1],
                                      ALU.mult, ALU.add).then_inc(conv_done, 1)
                    for k in range(1, KTAPS):
                        dve.wait_ge(conv_done, base + k)
                        dve.scalar_tensor_tensor(v, xp[:, d % 2, k:k + S], conv_w[:, d, k:k + 1], v,
                                                 ALU.mult, ALU.add).then_inc(conv_done, 1)

                def silu(d):
                    dve.wait_ge(tanh_done, b * CT + d + 1)
                    dve.scalar_tensor_tensor(xc[:, d, :], tanh[:, d % 2, :], 1.0, xc[:, d, :],
                                             ALU.add, ALU.mult).then_inc(xc_ready, 1)

                convolve(0)
                for d in range(CT):
                    if d + 1 < CT:
                        convolve(d + 1)
                    silu(d)
                if isinstance(b, int):
                    dve.wait_ge(w_late, 7 * 16)
                    dve.tensor_scalar(w2[:, :], w2_raw, -0.5, None, ALU.mult).then_inc(dve_scaled, 1)
                    dve.tensor_copy(bias2[32:32 + E, :], bias2_raw[32:32 + E, :]).then_inc(dve_scaled, 1)
                    dve.tensor_scalar(bias1[:, :], bias1_raw[:, :], -1.0, LIMIT, ALU.mult, ALU.add
                                      ).then_inc(dve_scaled, 1)
                    dve.wait_ge(dve_scaled, 5)
                    dve.wait_ge(fold_stored, 3 * 16)
                wait_mm(dve, b, ("C", 0, 0))
                dve.tensor_copy(c_tok[:, :, :],
                                bank_of(("C", 0, 0)).rearrange("p (a n) -> p a n", n=2 * N)[:, 0:TT, N:2 * N]
                                ).then_inc(dve_freed, 1)
                dve.memset(stage[:, :, :], 0.0)

                def cap(i):
                    job = ("S", i // NH, i % NH)
                    wait_mm(dve, b, job)
                    dve.tensor_scalar(soft[:, i, :], bank_of(job), chan[:, 1, i // NH:i // NH + 1], STEP_CAP,
                                      ALU.add, ALU.min).then_inc(cap_ready, 1)

                def step(i):
                    d, c = i // NH, i % NH
                    dve.wait_ge(soft_ready, b * CT * NH + i + 1)
                    dve.scalar_tensor_tensor(dt[:, d, c * HALF:(c + 1) * HALF], bank_of(("S", d, c)),
                                             chan[:, 1, d:d + 1], soft[:, i, :],
                                             ALU.add, ALU.max).then_inc(dve_freed, 1)

                for i in range(BATCH):
                    cap(i)
                for i in range(CT * NH):
                    if BATCH <= i + 2 < CT * NH:
                        cap(i + 2)
                    step(i)
                for i in range(BATCH, CT * NH):
                    d, c = i // NH, i % NH
                    wait_freed(dve, b, ("S", d, c))
                    dve.tensor_tensor(dtu[:, d, c * HALF:(c + 1) * HALF], dt[:, d, c * HALF:(c + 1) * HALF],
                                      xc[:, d, c * HALF:(c + 1) * HALF], ALU.mult).then_inc(dtu_ready, 1)

            def loop(b, bp):
                def accumulate(hf, it, par, c, a):
                    u = unit(b, hf, it, par, c) - 1
                    ta = (1 - c) * TH + a
                    n = it * 2 + (hf * (N // 2) + par - (1 if c == 0 else 0))
                    dve.wait_ge(hT_ready, u * TH + a + 1)
                    dve.scalar_tensor_tensor(stage[:, ta, :], ps[:, 2 + a % 2, :], c_tok[:, ta, bass.ds(n, 1)],
                                             stage[:, ta, :], ALU.mult, ALU.add).then_inc(hT_used, 1)

                def finalize(hf):
                    dve.wait_ge(p2_ready, unit(bp, hf, ITS - 1, 1, 1) + 1 + P2_CREDIT)
                    dve.tensor_copy(mix[:, 0:HALF], ps[:, 6, :])
                    dve.tensor_copy(mix[:, HALF:2 * HALF], ps[:, 7, :]).then_inc(mix_taken, 1)
                    dve.wait_ge(mix_taken, bp * 2 + hf + 2)
                    flat16 = xc16[:, hf * TH:(hf + 1) * TH, :].rearrange("p a d -> p (a d)")
                    dve.tensor_tensor(mix[:, :], mix[:, :], flat16, ALU.add).then_inc(mix_added, 1)
                    dve.wait_ge(mix_added, bp * 2 + hf + 1)
                    dve.wait_ge(res_loaded, (bp * 2 + hf) * 16 + 16)
                    flat = res[:, :, :].rearrange("p a d -> p (a d)")
                    dve.tensor_tensor(flat, mix[:, :], flat, ALU.add).then_inc(out_ready, 1)
                    wait_apart(dve, out_ready, bp * 2 + hf + 1)

                def body(hf, it, par, c, first):
                    if b is not None:
                        u = unit(b, hf, it, par, c)
                    if bp is not None:
                        s = unit(bp, hf, it, par, c)
                    for d in range(CT):
                        if b is not None:
                            dve.wait_ge(exp_ready, u * CT + d + 1)
                            dve.wait_ge(dbu_ready, u * CT + d + 1 + DBU_CREDIT)
                            start = 0.0 if c == 0 else h[:, 0, d, HALF - 1:HALF]
                            dve.tensor_tensor_scan(h[:, c, d, :], ps[:, d % 2, :], dbu[:, d, :], start,
                                                   ALU.mult, ALU.add).then_inc(scan_done, 1)
                        if bp is not None and d == CT - 1:
                            if b is None:
                                wait_apart(dve, t_ready, s + 1)
                                dve.tensor_scalar(ex_g[:, c, :], ex_g[:, c, :], LIMIT, None, ALU.subtract
                                                  ).then_inc(neg_ready, 1)
                                dve.wait_ge(l_ready, s + 2)
                                dve.tensor_scalar(ex_l[:, c, :], ex_l[:, c, :], 2 * LIMIT, -1.0, ALU.min, ALU.mult
                                                  ).then_inc(lin_ready, 1)
                            wait_apart(dve, neg_ready, s + 1)
                            dve.scalar_tensor_tensor(ex_t[:, c, :], ex_t[:, c, :], 1.0, ex_g[:, c, :],
                                                     ALU.add, ALU.mult).then_inc(u_ready, 1)
                        if b is not None and not (hf == 0 and first):
                            accumulate(hf, it, par, c, d)
                    if bp is not None:
                        wait_apart(dve, lin_ready, s + 1)
                        dve.wait_ge(u_ready, s + 1)
                        dve.scalar_tensor_tensor(ex_l[:, c, :], ex_l[:, c, :],
                                                 1.0 - LIMIT if b is not None else 1.0 + LIMIT, ex_t[:, c, :],
                                                 ALU.add, ALU.mult).then_inc(a_ready, 1)
                        if hf == 1 and isinstance(it, int) and par * NH + c == (0 if b is not None else 1):
                            finalize(0)

                windows(dve, body)
                if b is not None:
                    for a in range(TH):
                        accumulate(1, ITS, 0, 0, a)
                if bp is not None:
                    finalize(1)

            def phase_c(b):
                for job in jobs_c[0:8]:
                    _, d, c = job
                    cols = slice(c * HALF, (c + 1) * HALF)
                    dve.wait_ge(gate_tanh, b * CT * NH + d * NH + c + 1)
                    dve.scalar_tensor_tensor(dt[:, d, cols], dt[:, d, cols], 1.0, bank_of(job),
                                             ALU.add, ALU.mult).then_inc(dve_freed, 1)
                for job in jobs_c[8:16]:
                    _, d, c = job
                    cols = slice(c * HALF, (c + 1) * HALF)
                    wait_mm(dve, b, job)
                    dve.scalar_tensor_tensor(xc[:, d, cols], xc[:, d, cols], chan[:, 2, d:d + 1], bank_of(job),
                                             ALU.mult, ALU.add).then_inc(dve_freed, 1)
                for a in range(TT):
                    job = ("O", a, 0)
                    wait_mm(dve, b, job)
                    ins = dve.tensor_tensor(xt[:, a, :], xt[:, a, :], bank_of(job)[:, 0:D], ALU.add
                                            ).then_inc(dve_freed, 1)
                wait_freed(dve, b, ("O", TT - 1, 0))
                norm(b, 1, xn, xn_ready)
                for a in range(TT):
                    job = ("Q", a, 0)
                    wait_mm(dve, b, job)
                    link(b, dve.reduce_max(mx[:, a:a + 1], bank_of(job)[:, 0:LK], AX_X))
                    dve.tensor_scalar(negm[:, a:a + 1], mx[:, a:a + 1], -(float(D) ** -0.5), None, ALU.mult
                                      ).then_inc(negm_ready, 1)
                for a in range(TT):
                    wait_freed(dve, b, ("Q", a, 0))
                    link(b, dve.reciprocal(rinv[:, a:a + 1], rsum[:, a:a + 1]))
                    dve.tensor_scalar(probs[:, a, :], probs[:, a, :], rinv[:, a:a + 1], None, ALU.mult
                                      ).then_inc(probs_ready, 1)
                for a in range(TT):
                    job = ("V", a, 0)
                    wait_mm(dve, b, job)
                    dve.tensor_tensor(xt[:, a, :], xt[:, a, :], bank_of(job)[:, 0:D], ALU.add
                                      ).then_inc(dve_freed, 1)
                wait_freed(dve, b, ("V", TT - 1, 0))
                norm(b, 2, xc16, x16_ready)
                dve.wait_ge(ssq_ready, b * TT + TT)
                dve.tensor_scalar(ve[:, :], ssq[:, :], 1.0 / D, EPS, ALU.mult, ALU.add).then_inc(ve_ready, 1)
                dve.wait_ge(rstd_ready, b * 4 + 4)
                for a in range(TT):
                    dve.scalar_tensor_tensor(nf[:, a, :], xc16[:, a, :], rstd[:, a:a + 1], norm_w[:, :],
                                             ALU.mult, ALU.mult).then_inc(nf_ready, 1)
                wait_mm(dve, b, ("G", 0, 0))
                dve.tensor_tensor(lg16[:, :, :], bank_of(("G", 0, 0))[:, 0:TT * E].rearrange("p (a e) -> p a e", e=E),
                                  gate_b[:, :, :].broadcast_to([P, TT, E]), ALU.add).then_inc(dve_freed, 1)
                wait_freed(dve, b, ("G", 0, 0))
                link(b, dve.tensor_copy(lg[:, :, :], lg16[:, :, :]))
                for a in range(TT):
                    ins = dve.max(m8[:, a, :], lg[:, a, :])
                link(b, ins)
                dve.tensor_tensor(tw[:, 0, :], m8[:, :, 1], m8[:, :, 0], ALU.subtract).then_inc(gap_ready, 1)
                for a in range(TT):
                    ins = dve.max_index(i8[:, a, :], m8[:, a, :], lg[:, a, :])
                link(b, ins)
                link(b, dve.tensor_copy(i8f[:, :, :], i8[:, :, :]))
                for n in range(2):
                    ins = dve.tensor_tensor(eq[:, n, :, :], iota[:, :, :].broadcast_to([P, TT, E]),
                                            i8f[:, :, n:n + 1].broadcast_to([P, TT, E]), ALU.is_equal)
                link(b, ins)
                dve.wait_ge(gap_exp, b + 1)
                link(b, dve.tensor_scalar(tden[:, :], tw[:, 1, :], 1.0, None, ALU.add))
                link(b, dve.reciprocal(tw[:, 2, :], tden[:, :]))
                link(b, dve.tensor_tensor(tw[:, 3, :], tw[:, 1, :], tw[:, 2, :], ALU.mult))
                for n in range(2):
                    ins = dve.tensor_tensor(eq[:, n, :, :], eq[:, n, :, :],
                                            tw[:, 2 + n, :].rearrange("p (a o) -> p a o", o=1).broadcast_to([P, TT, E]),
                                            ALU.mult)
                link(b, ins)
                dve.tensor_tensor(comb[:, :, :], eq[:, 0, :, :], eq[:, 1, :, :], ALU.add).then_inc(comb_ready, 1)
                if isinstance(b, int):
                    per_row[0] = links[0]

            over_rows(dve, phase_a, loop, phase_c)

        @block.tensor
        def _(pe):
            pe.sem_inc(p2_ready, P2_CREDIT)

            def fold():
                pe.wait_ge(w_fold, (FOLD_LOADS + 1) * 16)
                pe.wait_ge(consts, 6)
                for i, (what, k, c) in enumerate(fold_jobs):
                    bank = ps[:, (FOLD_BANK + i) % 8, :]
                    cols = slice(k * P, (k + 1) * P)
                    keys = slice(c * KCH, (c + 1) * KCH)
                    need = {"WQH": 0, "c": 0, "k": fold_at(("c", 1, 1)), "v": fold_at(("k", 1, 1)),
                            "KQ": fold_at(("k", 1, 1)), "KROW": fold_at(("k", 1, 1)), "WQO": fold_at(("WQH", 1, 0)),
                            "OROW": fold_at(("WQH", 1, 0)), "VO": fold_at(("OROW", 0, 0))}[what]
                    need = max(need, i - 7)
                    if i < 8:
                        wait_freed(pe, 0, jobs_a[FOLD_BANK + i - 8])
                    if need:
                        pe.wait_ge(fold_kept, need)
                    pairs = {"WQH": lambda: [(qwT[:, q, cols], hwb[:, q, :]) for q in range(DK)],
                             "c": lambda: [(cwT[:, q, cols], ctxT[:, q, keys]) for q in range(DK)],
                             "k": lambda: [(kwT[:, q, cols], cT[:, q, keys]) for q in range(DK)],
                             "v": lambda: [(vwT[:, q, cols], cT[:, q, keys]) for q in range(DK)],
                             "KQ": lambda: [(wqh[:, q, cols], kT[:, q, keys]) for q in range(DK)],
                             "KROW": lambda: [(bq[:, q, :], kT[:, q, keys]) for q in range(DK)],
                             "WQO": lambda: [(wqh[:, q, cols], owT[:, q, :]) for q in range(DK)],
                             "OROW": lambda: [(bq[:, q, :], owT[:, q, :]) for q in range(DK)] + [(ones[0:1, 0:1], ob_row)],
                             "VO": lambda: [(vT[:, q, k * KEYS:(k + 1) * KEYS], owT[:, q, :]) for q in range(DK)]
                                   + [(ones[0:1, 0:KEYS], o_row[0:1, :])]}[what]()
                    for n, (left, right) in enumerate(pairs):
                        dst = bank[0:left.shape[1], 0:right.shape[1]]
                        mm = pe.matmul(dst, left, right, start=(n == 0), stop=(n == len(pairs) - 1))
                    mm.then_inc(fold_ready, 1)

            def product(bank, pairs):
                for n, (left, right) in enumerate(pairs):
                    mm = pe.matmul(bank, left, right, start=(n == 0), stop=(n == len(pairs) - 1))
                return mm

            def free_bank(b, jobs, job):
                i = jobs.index(job)
                if i >= 8:
                    wait_freed(pe, b, jobs[i - 8])

            def transposes(b, job, src, idn, n_norm):
                _, k, c = job
                bank = bank_of(job)
                for a in range(TH):
                    mm = pe.transpose(bank[:, a * P:(a + 1) * P], src[:, c * TH + a, k * P:(k + 1) * P], idn[:, :])
                return mm

            def phase_a(b):
                if not isinstance(b, int):
                    wait_freed(pe, b - 1, ("CT", 0, NH - 1))
                    wait_freed(pe, b - 1, ("G", 0, 0))
                else:
                    pe.wait_ge(consts, 6)
                for c in halves:
                    pe.wait_ge(xn_ready, b * 2 * TT + (c + 1) * TH)
                    for k in range(DK):
                        transposes(b, ("T", k, c), xn, ident, 0).then_inc(mm_ready, 1)
                if isinstance(b, int):
                    pe.wait_ge(w_early, 9 * 16)
                for d in range(CT):
                    for c in halves:
                        job = ("X", d, c)
                        free_bank(b, jobs_a, job)
                        wait_freed(pe, b, ("T", DK - 1, c))
                        product(bank_of(job), [(w_in[:, k, d * P:(d + 1) * P], xnT[:, k, c * HALF:(c + 1) * HALF])
                                               for k in range(DK)]).then_inc(mm_ready, 1)
                if isinstance(b, int):
                    fold()
                    pe.wait_ge(fold_kept, len(fold_jobs))
                pe.wait_ge(xc_ready, b * CT + CT)
                for c in halves:
                    job = ("B", 0, c)
                    free_bank(b, jobs_a, job)
                    product(bank_of(job)[0:2 * N, :], [(w_x[:, d, :], xc[:, d, c * HALF:(c + 1) * HALF])
                                                   for d in range(CT)]).then_inc(mm_ready, 1)
                job = ("C", 0, 0)
                free_bank(b, jobs_a, job)
                wait_freed(pe, b, ("B", 0, NH - 1))
                pe.sem_inc(passed, 1)
                for a in range(TT):
                    mm = pe.transpose(bank_of(job)[:, a * 2 * N:(a + 1) * 2 * N], bc_sb[:, a * P:(a + 1) * P],
                                      ident[0:2 * N, 0:2 * N])
                mm.then_inc(mm_ready, 1)
                for d in range(CT):
                    for c in halves:
                        job = ("S", d, c)
                        free_bank(b, jobs_a, job)
                        product(bank_of(job), [(w_dt[:, k, d * P:(d + 1) * P], xc[:, k, c * HALF:(c + 1) * HALF])
                                               for k in range(CT)]).then_inc(mm_ready, 1)
                wait_freed(pe, b, ("B", 0, NH - 1))
                wait_freed(pe, b, ("S", CT - 1, NH - 1))

            def loop(b, bp):
                if bp is not None:
                    wait_freed(pe, bp, ("CT", 0, NH - 1))
                    pe.wait_ge(dve_scaled, 5)

                def transpose_states(u, c, tiles):
                    for a in tiles:
                        pe.wait_ge(hT_used, u * TH + a + 1)
                        for d in range(CT):
                            mm = pe.transpose(ps[:, 2 + a % 2, d * P:(d + 1) * P],
                                              h[:, c, d, a * P:(a + 1) * P], ident[:, :])
                        mm.then_inc(hT_ready, 1)

                def bias_product(hf):
                    pe.wait_ge(mix_taken, bp * 2 + hf + 1)
                    for a in range(TH):
                        tok = slice((hf * TH + a) * P, (hf * TH + a + 1) * P)
                        pe.matmul(ps[:, 6 + a // 2, (a % 2) * D:(a % 2 + 1) * D], rows[32:32 + E, tok],
                                  bias2[32:32 + E, :], start=(a % 2 == 0), stop=True, skip_group_check=True)

                def down_product(s, c, col):
                    pe.wait_ge(aw_ready, s + 1 + AW_CREDIT)
                    for a in range(TH):
                        mm = pe.matmul(ps[:, 6 + a // 2, (a % 2) * D:(a % 2 + 1) * D],
                                       ex_a[:, c, a * P:(a + 1) * P], w2[:, bass.ds(col, D)],
                                       start=False, stop=True, skip_group_check=True)
                    mm.then_inc(p2_ready, 1)

                def body(hf, it, par, c, first):
                    if bp is not None:
                        s = unit(bp, hf, it, par, c)
                        wcol = (it * 2 + par) * (DK * 2 * I) + c * P
                        for g, taken in ((0, g_ready), (1, l_ready)):
                            pe.wait_ge(taken, s + 1)
                            for k in range(DK):
                                mm = pe.matmul(ps[:, 4 + g, :], w1[:, bass.ds(wcol + (k * 2 * I + g * I), P)],
                                               nfT[:, k, hf * HALF:(hf + 1) * HALF],
                                               start=(k == 0), stop=(k == DK - 1))
                            mm.then_inc(p1_ready, 1)
                    if b is not None and not (hf == 0 and first):
                        transpose_states(unit(b, hf, it, par, c) - 1, 1 - c, range(2, TH))
                    if bp is not None:
                        lag = 1 if b is not None else 2
                        place = par * NH + c - lag
                        if isinstance(it, int) and place == 0:
                            bias_product(hf)
                        if not isinstance(it, int) or place >= 0:
                            down_product(s - lag, (c - lag) % NH, it * (4 * D) + place * D)
                        elif hf == 1:
                            down_product(s - lag, (c - lag) % NH, (2 * E + place) * D)
                    if b is not None:
                        u = unit(b, hf, it, par, c)
                        pe.wait_ge(scan_done, u * CT + CT + SCAN_CREDIT)
                        transpose_states(u, c, range(2))

                windows(pe, body)
                if b is not None:
                    transpose_states(unit(b, 1, ITS - 1, 1, 1), 1, range(2, TH))
                if bp is not None:
                    for c in range(1 if b is not None else 0, NH):
                        down_product(unit(bp, 1, ITS - 1, 1, c), c, (2 * E - NH + c) * D)

            def phase_c(b):
                pe.wait_ge(hT_used, unit(b, 1, ITS - 1, 1, 1) * TH + TH + HT_CREDIT)
                if not isinstance(b, int):
                    pe.wait_ge(mix_taken, b * 2 + 1)
                for job in jobs_c[0:8]:
                    _, d, c = job
                    product(bank_of(job), [(w_in[:, k, DI + d * P:DI + (d + 1) * P], xnT[:, k, c * HALF:(c + 1) * HALF])
                                           for k in range(DK)]).then_inc(mm_ready, 1)
                for job in jobs_c[8:16]:
                    _, d, c = job
                    free_bank(b, jobs_c, job)
                    for a in range(TH):
                        mm = pe.transpose(bank_of(job)[:, a * P:(a + 1) * P],
                                          stage[:, c * TH + a, d * P:(d + 1) * P], ident[:, :])
                    mm.then_inc(mm_ready, 1)
                if isinstance(b, int):
                    pe.wait_ge(act_scaled, 3)
                for a in range(TT):
                    job = ("O", a, 0)
                    free_bank(b, jobs_c, job)
                    pe.wait_ge(gated, b * CT * NH + CT * NH)
                    product(bank_of(job)[:, 0:D], [(xc[:, d, a * P:(a + 1) * P], w_out[:, d, :])
                                                   for d in range(CT)]).then_inc(mm_ready, 1)
                for c in halves:
                    pe.wait_ge(xn_ready, b * 2 * TT + TT + (c + 1) * TH)
                    for k in range(DK):
                        free_bank(b, jobs_c, ("T2", k, c))
                        transposes(b, ("T2", k, c), xn, ident, 1).then_inc(mm_ready, 1)
                pe.wait_ge(kv_loaded, b * 48 + 48)
                for a in range(TT):
                    job = ("Q", a, 0)
                    free_bank(b, jobs_c, job)
                    wait_freed(pe, b, ("T2", DK - 1, a // TH))
                    tok = slice(a * P, (a + 1) * P)
                    dst = bank_of(job)[:, 0:LK]
                    for k in range(DK):
                        pe.matmul(dst, xnT[:, k, tok], kq[:, k, :], start=(k == 0), stop=False)
                    pe.matmul(dst, ones[0:1, :], rows[0:1, 0:LK],
                              start=False, stop=True).then_inc(mm_ready, 1)
                for c in halves:
                    pe.wait_ge(probs_ready, b * TT + (c + 1) * TH)
                    for k in range(2):
                        job = ("PT", k, c)
                        free_bank(b, jobs_c, job)
                        for a in range(TH):
                            mm = pe.transpose(bank_of(job)[0:KEYS, a * P:(a + 1) * P],
                                              probs[:, c * TH + a, k * KEYS:(k + 1) * KEYS], ident[:, :])
                        mm.then_inc(mm_ready, 1)
                for a in range(TT):
                    job = ("V", a, 0)
                    free_bank(b, jobs_c, job)
                    wait_freed(pe, b, ("PT", 1, a // TH))
                    tok = slice(a * P, (a + 1) * P)
                    dst = bank_of(job)[:, 0:D]
                    for k in range(DK):
                        pe.matmul(dst, xnT[:, k, tok], w_qo[:, k, :], start=(k == 0), stop=False)
                    for k in range(2):
                        mm = pe.matmul(dst, probsT[0:KEYS, k, tok], vo[:, k, :],
                                       start=False, stop=(k == 1))
                    mm.then_inc(mm_ready, 1)
                for c in halves:
                    pe.wait_ge(nf_ready, b * TT + (c + 1) * TH)
                    for k in range(DK):
                        job = ("N", k, c)
                        free_bank(b, jobs_c, job)
                        bank = bank_of(job).bitcast(BF16)
                        for a in range(TH):
                            mm = pe.transpose(bank[:, a * P:(a + 1) * P],
                                              nf[:, c * TH + a, k * P:(k + 1) * P], ident16[:, :])
                        mm.then_inc(mm_ready, 1)
                job = ("G", 0, 0)
                free_bank(b, jobs_c, job)
                wait_freed(pe, b, ("N", DK - 1, NH - 1))
                if isinstance(b, int):
                    pe.wait_ge(w_late, 7 * 16)
                for a in range(TT):
                    mm = product(bank_of(job)[:, a * E:(a + 1) * E],
                                 [(nfT[:, k, a * P:(a + 1) * P], gate_w[:, k, :]) for k in range(DK)])
                mm.then_inc(mm_ready, 1)
                pe.wait_ge(comb_ready, b + 1)
                for c in halves:
                    job = ("CT", 0, c)
                    free_bank(b, jobs_c, job)
                    for a in range(TH):
                        mm = pe.transpose(bank_of(job)[0:E, a * P:(a + 1) * P], comb[:, c * TH + a, :], ident[:, :])
                    mm.then_inc(mm_ready, 1)

            over_rows(pe, phase_a, loop, phase_c)


def kernel(**inputs):
    import concourse.bacc as bacc
    import numpy as np
    from concourse.bass_utils import run_bass_kernel_spmd

    v = {name: np.asarray(a) for name, a in inputs.items()}
    attn, cross, ffn = "L0_attn_", "L0_xattn_", "L0_ffn_"
    E, I2, D = v[ffn + "mlp1_weight"].shape
    w1 = v[ffn + "mlp1_weight"].reshape(E, I2 // 2, 2, D).transpose(0, 3, 2, 1).reshape(E, D, I2)
    b1 = v[ffn + "mlp1_bias"].reshape(E, I2 // 256, 128, 2).transpose(2, 0, 3, 1).reshape(128, E * I2 // 128)
    laid = {
        "x": v["x"], "ctxT": v["ctx_1024"].transpose(2, 0, 1).reshape(D, -1),
        "W_in": v[attn + "W_in"], "conv_w": v[attn + "conv_w"], "conv_b": v[attn + "conv_b"],
        "W_x": v[attn + "W_x"], "W_dt": v[attn + "W_dt"], "b_dt": v[attn + "b_dt"],
        "A_log": v[attn + "A_log"], "D_skip": v[attn + "D"], "W_out": v[attn + "W_out"],
        "hW": v[cross + "hW"], "qWT": v[cross + "qW"].T, "cWT": v[cross + "cW"].T, "kWT": v[cross + "kW"].T,
        "vWT": v[cross + "vW"].T, "oWT": v[cross + "oW"].T,
        "hb": v[cross + "hb"], "qb": v[cross + "qb"], "cb": v[cross + "cb"], "kb": v[cross + "kb"],
        "vb": v[cross + "vb"], "ob": v[cross + "ob"],
        "norm_w": v[ffn + "norm_weight"], "gate_wT": v[ffn + "gate_weight"].T,
        "gate_b": v[ffn + "gate_bias"].reshape(1, E), "mlp1_wT": w1, "mlp1_bT": b1,
        "mlp2_wT": v[ffn + "mlp2_weight"].transpose(0, 2, 1), "mlp2_b": v[ffn + "mlp2_bias"],
    }
    laid = {name: np.ascontiguousarray(a) for name, a in laid.items()}
    nc = bacc.Bacc("TRN2", target_bir_lowering=False, num_devices=1)
    t = {name: nc.dram_tensor(f"in_{name}", a.shape, mybir.dt.from_np(a.dtype), kind="ExternalInput").ap()
         for name, a in laid.items()}
    out = nc.dram_tensor("out_x", v["x"].shape, F32, kind="ExternalOutput").ap()
    decoder_layer(nc, t, out)
    r = run_bass_kernel_spmd(nc, [{f"in_{name}": a for name, a in laid.items()}], core_ids=[0])
    return r.results[0]["out_x"]
```

```python
from contextlib import ExitStack

import concourse.bass as bass
from concourse import mybir

F32 = mybir.dt.float32
BF16 = mybir.dt.bfloat16
U32 = mybir.dt.uint32
ACT = mybir.ActivationFunctionType
ALU = mybir.AluOpType
AX_X = mybir.AxisListType.X

P = 128
HALF = 512
EPS = 1e-5
LIMIT = 7.0
ALPHA = 1.702
STEP_CAP = 30.0


def decoder_layer(nc, t, out):
    B, S, D = t["x"].shape
    DI = t["W_dt"].shape[0]
    N = t["A_log"].shape[1]
    KTAPS = t["conv_w"].shape[1]
    PAD = KTAPS - 1
    E = t["gate_wT"].shape[1]
    I = t["mlp2_wT"].shape[1]
    LK = t["ctxT"].shape[1] // B
    DK, CT, TT = D // P, DI // P, S // P
    NH = S // HALF
    TH = TT // NH
    KEYS = LK // 2
    ALLK = B * LK
    assert NH == 2 and DK == 2 and I == 2 * P and LK % 2 == 0 and KEYS <= P and E * NH == N

    bd = nc.dram_tensor("b_rows", (B * N, S), F32, kind="Internal").ap()
    combd = nc.dram_tensor("combine_rows", (B * E, S), F32, kind="Internal").ap()
    kqd = nc.dram_tensor("kq_rows", (B * P, DK * LK), F32, kind="Internal").ap()
    vod = nc.dram_tensor("vo_rows", (B * KEYS, 2 * D), F32, kind="Internal").ap()
    k_rowd = nc.dram_tensor("key_bias_rows", (B, LK), F32, kind="Internal").ap()
    w_outd = nc.dram_tensor("halved_w_out", (P, CT * D), F32, kind="Internal").ap()
    x2d = nc.dram_tensor("x2_rows", (B * S, D), F32, kind="Internal").ap()
    x_rows = t["x"].rearrange("b s d -> (b s) d")
    out_rows = out.rearrange("b s d -> (b s) d")

    with ExitStack() as ctx:
        def sb(name, shape, dt=F32):
            return ctx.enter_context(nc.sbuf_tensor(name, shape, dt))

        def sem(name):
            return ctx.enter_context(nc.semaphore(name))

        w_in = sb("w_in", [P, DK, 2 * DI])
        w_dt = sb("w_dt", [P, CT, DI])
        w_out = sb("w_out", [P, CT, D])
        w_x = sb("w_x", [P, CT, 2 * N])
        conv_w = sb("conv_w_sb", [P, CT, KTAPS])
        chan = sb("chan", [P, 3, CT])
        a_neg = sb("a_neg", [P, CT * N])
        w1 = sb("w1", [P, E * DK * 2 * I], BF16)
        w2 = sb("w2", [P, E * 2 * D])
        bias1 = sb("bias1", [P, E * 4])
        bias2 = sb("bias2", [64, D])
        gate_w = sb("gate_w", [P, DK, E], BF16)
        gate_b = sb("gate_b", [P, 1, E], BF16)
        norm_w = sb("norm_w", [P, D])
        kq = sb("kq", [P, DK, LK])
        vo = sb("vo", [KEYS, 2, D])
        w_qo = sb("w_qo", [P, DK, D])
        rows = sb("rows", [64, S])
        ident = sb("ident", [P, P])
        ident16 = sb("ident16", [P, P], BF16)
        ones = bias2[0:1, 0:P]
        minus_half = sb("minus_half", [P, TT])
        iota = sb("iota", [P, 1, E])
        shift = sb("shift", [P, 3])
        xt = sb("xt", [P, TT, D])
        xnT = sb("xnT", [P, DK, S])
        nfT = sb("nfT", [P, DK, S], BF16)
        xc = sb("xc", [P, CT, S])
        dt = sb("dt", [P, CT, S])
        dtu = sb("dtu", [P, CT, S])
        b_bc = sb("b_bc", [P, NH, HALF])
        c_tok = sb("c_tok", [P, TT, N])
        stage = sb("stage", [P, TT, DI])
        xn_a = stage[:, :, D:2 * D]
        xn_c = stage[:, :, 0:D]
        xc16 = sb("xc16", [P, TT, D], BF16)
        work = sb("work", [P, 10240])
        wbc = sb("wbc", [P, 2, HALF])
        res = sb("res", [P, TH, D])
        mix = sb("mix", [P, TH * D], BF16)
        ve = sb("ve", [P, TT])
        rstd = sb("rstd", [P, TT])
        ssq = sb("ssq", [P, TT])
        mx = sb("mx", [P, TT])
        negm = sb("negm", [P, TT])
        rsum = sb("rsum", [P, TT])
        rinv = sb("rinv", [P, TT])

        slots = work[:, 0:8 * S].rearrange("p (n t) -> p n t", n=8)

        def slot(par, d, alone):
            if d < 2:
                return slots[:, par * 2 + d, :]
            return slots[:, (par * 2 if alone else 0) + 2 + d, :]

        ex_sets = [[work[:, at + i * NH * HALF:at + (i + 1) * NH * HALF].rearrange("p (j t) -> p j t", j=2)
                    for i in range(4)] for at in (6144, 0)]
        decays = xt[:, :, :].rearrange("p a d -> p (a d)").rearrange("p (r t) -> p r t", r=2)
        b_bcs = [b_bc[:, :, :].rearrange("p c t -> p (c t)"), w_out[:, :, :].rearrange("p k n -> p (k n)")]
        xp = dtu[:, :, :].rearrange("p a s -> p (a s)")[:, 0:2 * (PAD + S)].rearrange("p (r s) -> p r s", r=2)
        soft = work[:, 0:CT * NH * HALF].rearrange("p (r t) -> p r t", r=CT * NH)
        bc_sb = work[0:2 * N, 6912:6912 + S]
        TANH_AT = 8192
        NORM_AT = TANH_AT - 8 * TT
        stats = work[:, NORM_AT:NORM_AT + 6 * TT].rearrange("p (a n) -> p a n", n=6)
        mv = work[:, NORM_AT + 6 * TT:TANH_AT].rearrange("p (a n) -> p a n", n=2)
        assert 6912 + S <= NORM_AT
        tanh = work[:, TANH_AT:TANH_AT + 2 * S].rearrange("p (r t) -> p r t", r=2)
        xcT = dt[:, 0:DK, :]
        probs = work[:, 0:TT * LK].rearrange("p (a k) -> p a k", a=TT)
        probsT = work[:, 2048:4096].rearrange("p (k t) -> p k t", k=2)
        square = work[:, 4096:5120].bitcast(BF16).rearrange("p (a d) -> p a d", a=TT)
        nf = work[:, 5120:6144].bitcast(BF16).rearrange("p (a d) -> p a d", a=TT)
        o = [6144]

        def small(*shape):
            n = 1
            for extent in shape:
                n *= extent
            o[0] += n
            names = "abcd"[:len(shape)]
            return work[:, o[0] - n:o[0]].rearrange(
                f"p ({' '.join(names)}) -> p {' '.join(names)}", **dict(zip(names[:-1], shape)))

        lg16 = small(TT, E // 2).bitcast(BF16)
        lg, m8, i8f, comb = (small(TT, E) for _ in range(4))
        i8 = small(TT, 8).bitcast(U32)
        tw = small(4, TT)
        tden = small(1, TT)[:, 0, :]
        eq = small(2, TT, E)
        o = [0]

        def part(n):
            o[0] += n
            return work[:, o[0] - n:o[0]]

        qwT, cwT = (res[:, i * 2:i * 2 + 2, :] for i in range(2))
        kwT, vwT = (b_bc[:, i, :].rearrange("p (k f) -> p k f", k=DK) for i in range(2))
        owT = part(DK * D).rearrange("p (k f) -> p k f", k=DK)
        hwb = part(DK * (D + 1)).rearrange("p (k f) -> p k f", k=DK)
        wqh = part(DK * D).rearrange("p (k f) -> p k f", k=DK)
        ctxT, cT, kT = (part(DK * ALLK).rearrange("p (k f) -> p k f", k=DK) for _ in range(3))
        vT = ctxT
        fbias = part(4 * DK).rearrange("p (n k) -> p n k", n=4)
        bq = part(DK).rearrange("p (k n) -> p k n", n=1)
        o_row = part(D)
        ob_row = part(D)[0:1, :]
        a_log = part(CT * N)
        bias1_raw = wbc[:, 0, 0:E * 2].bitcast(BF16)
        bias2_raw = wbc[:, 1, 0:D // 2].bitcast(BF16)
        kq_all = part(DK * ALLK).rearrange("p (b k f) -> p b k f", b=B, k=DK)
        k_row = part(ALLK)[0:1, :]
        vo_all = dt[:, :, :].rearrange("p a s -> p (a s)")[0:KEYS, E * D:E * D + 2 * B * D]
        assert o[0] <= NORM_AT
        w2_raw = dt[:, :, :].rearrange("p a d -> p (a d)")[:, 0:E * D].bitcast(BF16)

        ps = ctx.enter_context(nc.psum_tensor("ps", [P, 8, HALF], F32))

        w_first = sem("w_first")
        w_early = sem("w_early")
        w_fold = sem("w_fold")
        w_late = sem("w_late")
        passed = sem("passed")
        consts = sem("consts")
        shift_set = sem("shift_set")
        act_scaled = sem("act_scaled")
        dve_scaled = sem("dve_scaled")
        fold_ready = sem("fold_ready")
        fold_kept = sem("fold_kept")
        fold_stored = sem("fold_stored")
        kv_loaded = sem("kv_loaded")
        pad_ready = sem("pad_ready")
        x_in = [sem("x_in0"), sem("x_in1")]
        xt_loaded = sem("xt_loaded")
        w_out_saved = sem("w_out_saved")
        w_out_loaded = sem("w_out_loaded")
        y_zeroed = sem("y_zeroed")
        x2_stored = sem("x2_stored")
        b_stored = sem("b_stored")
        comb_stored = sem("comb_stored")
        b_loaded = [sem("b_loaded0"), sem("b_loaded1")]
        wbc_loaded = [sem("wbc_loaded0"), sem("wbc_loaded1")]
        res_loaded = sem("res_loaded")
        out_stored = sem("out_stored")
        chain = {"a": sem("chain_a"), "c": sem("chain_c")}
        ve_ready = [sem(f"ve_ready{n}") for n in range(4)]
        rstd_ready = [sem(f"rstd_ready{n}") for n in range(4)]
        xn_a_ready = sem("xn_a_ready")
        xn_c_ready = sem("xn_c_ready")
        mm_ready = sem("mm_ready")
        act_freed = sem("act_freed")
        dve_freed = sem("dve_freed")
        conv_done = sem("conv_done")
        tanh_done = sem("tanh_done")
        xc_ready = sem("xc_ready")
        cap_ready = sem("cap_ready")
        soft_exp = sem("soft_exp")
        soft_ready = sem("soft_ready")
        dtu_ready = [sem("dtu_ready_first"), sem("dtu_ready_last")]
        exp_ready = sem("exp_ready")
        dbu_ready = sem("dbu_ready")
        scan_done = sem("scan_done")
        hT_ready = sem("hT_ready")
        hT_used = sem("hT_used")
        p1_ready = sem("p1_ready")
        g_ready = sem("g_ready")
        l_ready = sem("l_ready")
        t_ready = sem("t_ready")
        neg_ready = sem("neg_ready")
        lin_ready = sem("lin_ready")
        u_ready = sem("u_ready")
        a_ready = sem("a_ready")
        aw_ready = sem("aw_ready")
        p2_ready = sem("p2_ready")
        mix_taken = sem("mix_taken")
        out_ready = sem("out_ready")
        gate_tanh = sem("gate_tanh")
        gated = [sem("gated_low"), sem("gated_high")]
        negm_ready = sem("negm_ready")
        exp_probs = sem("exp_probs")
        probs_ready = sem("probs_ready")
        x16_ready = sem("x16_ready")
        ssq_ready = sem("ssq_ready")
        nf_ready = sem("nf_ready")
        gap_ready = sem("gap_ready")
        gap_exp = sem("gap_exp")
        comb_ready = sem("comb_ready")
        mix_added = sem("mix_added")

        halves = range(NH)

        def x_jobs(tiles):
            return [("X", d, c) for d in tiles for c in halves]

        steps = [("S", d, c) for c in halves for d in range(CT)]
        BATCH = CT * NH - 3
        assert BATCH == CT + 1

        def tiles_of(kind, c):
            if kind in ("O", "Q", "V"):
                return [(kind, c * TH + a, 0) for a in range(TH)]
            return [(kind, k, c) for k in range(CT if kind in ("Z", "Y") else DK)]

        def both(kind):
            return tiles_of(kind, 0) + tiles_of(kind, 1)

        head = [job for c in halves for kind in ("Z", "Y") for job in tiles_of(kind, c)] + both("O")
        tail = ([("B", 0, c) for c in halves] + [("C", 0, 0)] + steps[0:2] + both("N") + steps[2:3] +
                [("G", 0, 0)] + steps[3:5] + [("CT", 0, c) for c in halves] + steps[5:])
        all_jobs = (head + both("T") + x_jobs((0, 1)) + both("T2") + x_jobs((2, 3)) + both("Q") + both("PT") +
                    both("V") + tail)
        alone_jobs = (head + [job for c in halves for kind in ("T2", "Q") for job in tiles_of(kind, c)] +
                      [job for c in halves for kind in ("PT", "V") for job in tiles_of(kind, c)] + tail)
        late_banks = {**{job: i for i, job in enumerate(steps[0:6])}, steps[6]: 7, steps[7]: 6,
                      **{("N", k, c): 6 + k for c in halves for k in range(DK)}, ("G", 0, 0): 6, ("CT", 0, 0): 7, ("CT", 0, 1): 6}
        kinds_a = ("T", "X", "B", "C", "S")
        act_late = both("PT") + [("B", 0, c) for c in halves] + both("N") + [("CT", 0, c) for c in halves]
        act_order = both("T") + x_jobs((0, 1)) + both("T2") + x_jobs((2, 3)) + both("Q") + act_late
        act_alone = [job for c in halves for kind in ("T2", "Q") for job in tiles_of(kind, c)] + act_late
        dve_order = ([job for c in halves for kind in ("Z", "Y") for job in tiles_of(kind, c)] + both("O") +
                     both("V") + [("C", 0, 0), ("G", 0, 0)] + steps)

        class Phase:

            def __init__(self, c_row, a_row, with_c, with_a, before):
                self.c_row, self.a_row, self.before = c_row, a_row, before
                self.jobs = [j for j in (all_jobs if with_a else alone_jobs)
                             if (with_a if j[0] in kinds_a else with_c)]
                self.banks = [late_banks.get(j, i % 8) for i, j in enumerate(self.jobs)]
                self.taken = [[j for j in order if j in self.jobs]
                              for order in (act_order if with_a else act_alone, dve_order)]

            def total(self):
                return [len(self.jobs), len(self.taken[0]), len(self.taken[1])]

            def bank(self, job):
                return ps[:, self.banks[self.jobs.index(job)], :]

            def wait_mm(self, eng, job):
                eng.wait_ge(mm_ready, self.before[0] + self.jobs.index(job) + 1)

            def wait_taken(self, eng, job):
                by_dve = job in self.taken[1]
                eng.wait_ge(dve_freed if by_dve else act_freed,
                            self.before[1 + by_dve] + self.taken[by_dve].index(job) + 1)

            def wait_bank(self, eng, job):
                i = self.jobs.index(job)
                same = [n for n in range(i) if self.banks[n] == self.banks[i]]
                if same:
                    self.wait_taken(eng, self.jobs[same[-1]])

            def wait_all_taken(self, eng):
                for by_dve, freed in enumerate((act_freed, dve_freed)):
                    if self.taken[by_dve]:
                        self.wait_taken(eng, self.taken[by_dve][-1])

        total_a = Phase(None, 0, False, True, [0, 0, 0]).total()
        total_both = Phase(0, 1, True, True, [0, 0, 0]).total()

        def phase_between(b):
            if isinstance(b, int) and b == 0:
                return Phase(None, 0, False, True, [0, 0, 0])
            before = [n + (b - 1) * m for n, m in zip(total_a, total_both)]
            if isinstance(b, int):
                return Phase(b - 1, None, True, False, before)
            return Phase(b - 1, b, True, True, before)

        def wait_apart(eng, sem, value):
            eng.wait_ge(sem, value)
            eng.sem_inc(passed, 1)

        FOLD_LOADS = 6 + 1 + 1 + 4
        fold_jobs = ([("WQH", k, 0) for k in range(DK)] + [("c", k, c) for k in range(DK) for c in range(2)] +
                     [("k", k, c) for k in range(DK) for c in range(2)] +
                     [("v", k, c) for k in range(DK) for c in range(2)] +
                     [("KQ", k, c) for k in range(DK) for c in range(2)] +
                     [("KROW", 0, c) for c in range(2)] + [("WQO", k, 0) for k in range(DK)] +
                     [("OROW", 0, 0)] + [("VO", i, 0) for i in range(2 * B)])
        KCH = ALLK // 2
        assert KCH <= HALF

        FOLD_BANK = 4 + CT * NH

        def fold_at(job):
            return fold_jobs.index(job) + 1


        def state(b, hf, it, par):
            return b * N + hf * (N // 2) + it * 2 + par

        ITS = N // 4
        DBU_CREDIT, SCAN_CREDIT, HT_CREDIT, HT_READY_CREDIT = 8, 4, 4, 16
        EX_CREDIT = 2


        def turns(eng, body):
            for hf in range(2):
                for par in range(2):
                    body(hf, 0, par, par == 0)
                with eng.Fori(1, ITS) as it:
                    for par in range(2):
                        body(hf, it, par, False)

        STORE_CREDIT = 16

        block = ctx.enter_context(nc.Block())

        def over_rows(eng, phases, loop):
            phases(phase_between(0))
            loop(0, None)
            with eng.Fori(1, B) as b:
                phases(phase_between(b))
                loop(b, b - 1)
            phases(phase_between(B))
            loop(None, B - 1)

        @block.sync
        def _(sp):
            def load_x(b, dst, loaded):
                for c in halves:
                    sp.dma_start(dst[:, c * TH:(c + 1) * TH, :],
                                 x_rows[bass.ds(b * S + c * HALF, HALF), :].rearrange("(a p) d -> p a d", p=P)
                                 ).then_inc(loaded[c], 16)

            load_x(0, xn_a, x_in)
            sp.dma_start(w_in[:, :, :], t["W_in"].rearrange("(k p) n -> p k n", p=P)).then_inc(w_first, 16)
            sp.dma_start(conv_w[:, :, :], t["conv_w"].rearrange("(k p) n -> p k n", p=P)).then_inc(w_first, 16)
            for i, name in enumerate(("conv_b", "b_dt", "D_skip")):
                sp.dma_start(chan[:, i, :], t[name].rearrange("(k p) -> p k", p=P),
                             allow_slow_non_contiguous=True).then_inc(w_first, 16)
            for dst, name in ((w_x, "W_x"), (w_dt, "W_dt"), (w_out, "W_out")):
                sp.dma_start(dst[:, :, :], t[name].rearrange("(k p) n -> p k n", p=P)).then_inc(w_early, 16)
            sp.dma_start(a_log.rearrange("p (k n) -> p k n", n=N),
                         t["A_log"].rearrange("(k p) n -> p k n", p=P)).then_inc(w_early, 16)
            sp.dma_start(w2_raw.rearrange("p (e k f) -> p e k f", e=E, k=2),
                         t["mlp2_wT"].rearrange("e (k p) f -> p e k f", p=P)).then_inc(w_late, 16)
            sp.dma_start(w1[:, :].rearrange("p (e k f) -> p e k f", e=E, k=DK),
                         t["mlp1_wT"].rearrange("e (k p) f -> p e k f", p=P)).then_inc(w_late, 16)
            sp.dma_start(bias1_raw[:, :], t["mlp1_bT"]).then_inc(w_late, 16)
            sp.dma_start(bias2_raw[32:32 + E, :], t["mlp2_b"]).then_inc(w_late, 16)
            sp.dma_start(gate_w[:, :, :], t["gate_wT"].rearrange("(k p) e -> p k e", p=P)).then_inc(w_late, 16)
            sp.dma_start(gate_b[:, :, :], t["gate_b"].partition_broadcast(P)).then_inc(w_late, 16)
            sp.dma_start(norm_w[:, :], t["norm_w"].partition_broadcast(P)).then_inc(w_late, 16)

            sp.wait_ge(act_scaled, 3)
            sp.dma_start(w_outd, w_out[:, :, :].rearrange("p k n -> p (k n)")).then_inc(w_out_saved, 16)

            sp.wait_ge(fold_kept, len(fold_jobs))
            sp.dma_start(kqd.rearrange("(b p) (k f) -> p b k f", p=P, k=DK), kq_all).then_inc(fold_stored, 16)
            sp.dma_start(vod.rearrange("(b p) f -> p b f", p=KEYS),
                         vo_all.rearrange("p (b f) -> p b f", b=B)).then_inc(fold_stored, 16)
            sp.dma_start(k_rowd.rearrange("b (o f) -> o b f", o=1), k_row.rearrange("o (b f) -> o b f", b=B)
                         ).then_inc(fold_stored, 16)
            sp.wait_ge(fold_stored, 3 * 16)

            def phases(ph):
                r, b = ph.c_row, ph.a_row
                if r is not None:
                    wait_apart(sp, scan_done, (r + 1) * (N * CT) + SCAN_CREDIT)
                    sp.dma_start(w_out[:, :, :].rearrange("p k n -> p (k n)"), w_outd).then_inc(w_out_loaded, 16)
                    load_x(r, xt, [xt_loaded, xt_loaded])
                else:
                    sp.wait_ge(w_out_saved, 16)
                if r is not None and b is not None:
                    ph.wait_mm(sp, ("Y", CT - 1, NH - 1))
                    sp.sem_inc(passed, 1)
                    load_x(b, xn_a, x_in)
                if r is not None:
                    ph.wait_taken(sp, ("V", TT - 1, 0))
                    sp.dma_start(x2d[bass.ds(r * S, S), :].rearrange("(a p) d -> p a d", p=P),
                                 xt[:, :, :]).then_inc(x2_stored, 16)
                if b is not None:
                    sp.dma_start(kq[:, :, :], kqd[bass.ds(b * P, P), :].rearrange("p (k f) -> p k f", k=DK)
                                 ).then_inc(kv_loaded, 16)
                    sp.dma_start(vo[:, :, :], vod[bass.ds(b * KEYS, KEYS), :].rearrange("p (k f) -> p k f", k=2)
                                 ).then_inc(kv_loaded, 16)
                    sp.dma_start(rows[0:1, 0:LK], k_rowd[bass.ds(b, 1), :]).then_inc(kv_loaded, 16)
                    ph.wait_taken(sp, ("B", 0, NH - 1))
                    sp.dma_start(bd[bass.ds(b * N, N), :], bc_sb[0:N, :]).then_inc(b_stored, 16)
                if r is not None:
                    wait_apart(sp, x2_stored, r * 16 + 16)
                    ph.wait_taken(sp, ("CT", 0, NH - 1))
                    sp.dma_start(combd[bass.ds(r * E, E), :], rows[32:32 + E, :]).then_inc(comb_stored, 16)
                    wait_apart(sp, comb_stored, r * 16 + 16)
                if b is not None:
                    wait_apart(sp, b_stored, b * 16 + 16)

            def loop(b, bp):
                def load_res(hf):
                    wait_apart(sp, out_stored, (bp * 2 + hf) * 16 + STORE_CREDIT)
                    sp.dma_start(res[:, :, :],
                                 x2d[bass.ds(bp * S + hf * HALF, HALF), :].rearrange("(a p) d -> p a d", p=P)
                                 ).then_inc(res_loaded, 16)

                def store_out(hf):
                    wait_apart(sp, out_ready, bp * 2 + hf + 1)
                    sp.dma_start(out_rows[bass.ds(bp * S + hf * HALF, HALF), :].rearrange("(a p) d -> p a d", p=P),
                                 res[:, :, :]).then_inc(out_stored, 16)

                if bp is not None:
                    load_res(0)
                def loads(hf, first, last):
                    with sp.Fori(first, last) as it:
                        for par in range(2):
                            if b is not None:
                                wait_apart(sp, dbu_ready, state(b, hf, it, par) * CT + CT)
                                sp.dma_start(b_bcs[par].rearrange("p (o t) -> p o t", o=1),
                                             bd[bass.ds(state(b, hf, it, par), 1), :].partition_broadcast(P)
                                             ).then_inc(b_loaded[par], 16)
                            if bp is not None:
                                wait_apart(sp, aw_ready, state(bp, hf, it, par) - 1 + EX_CREDIT)
                                sp.dma_start(wbc[:, par:par + 1, :],
                                             combd[bass.ds(bp * E + it * 2 + par, 1),
                                                   hf * HALF:(hf + 1) * HALF].partition_broadcast(P)
                                             ).then_inc(wbc_loaded[par], 16)
                loads(0, 0, ITS)
                loads(1, 0, 2)
                if bp is not None:
                    store_out(0)
                loads(1, 2, ITS - 1)
                if bp is not None:
                    load_res(1)
                loads(1, ITS - 1, ITS)
                if bp is not None:
                    store_out(1)

            sp.sem_inc(out_stored, STORE_CREDIT)
            over_rows(sp, phases, loop)
            sp.wait_ge(out_stored, B * 2 * 16 + STORE_CREDIT)

        @block.gpsimd
        def _(pool):
            pool.sem_inc(dbu_ready, DBU_CREDIT)
            pool.sem_inc(aw_ready, EX_CREDIT)
            for i, value in enumerate((-LIMIT, ALPHA / 2 * LIMIT, 2 * LIMIT)):
                pool.memset(shift[:, i:i + 1], value).then_inc(shift_set, 1)
            pool.memset(ident[:, :], 0.0).then_inc(consts, 1)
            pool.memset(ones, 1.0).then_inc(consts, 1)
            pool.memset(minus_half[:, :], -0.5).then_inc(consts, 1)
            pool.iota(iota[:, 0, :], [[1, E]], base=0, channel_multiplier=0,
                      allow_small_or_imprecise_dtypes=True).then_inc(consts, 1)
            pool.wait_ge(consts, 1)
            pool.affine_select(out=ident[:, :], in_=ident[:, :], compare_op=ALU.not_equal, fill=1.0, base=0,
                               pattern=[[-1, P]], channel_multiplier=1).then_inc(consts, 1)
            pool.wait_ge(consts, 5)
            pool.tensor_copy(ident16[:, :], ident[:, :]).then_inc(consts, 1)

            def norm_scale(n, row, c):
                tiles = slice(c * TH, (c + 1) * TH)
                pool.wait_ge(ve_ready[n], row * NH + c + 1)
                pool.tensor_tensor(rstd[:, tiles], ve[:, tiles], minus_half[:, tiles], ALU.pow
                                   ).then_inc(rstd_ready[n], 1)

            def phases(ph):
                r, b = ph.c_row, ph.a_row
                if r is not None:
                    for c in halves:
                        for d in range(CT // 2):
                            ph.wait_taken(pool, ("Y", d, c))
                            cols = slice(c * HALF, (c + 1) * HALF)
                            pool.tensor_tensor(xc[:, d, cols], xc[:, d, cols], dt[:, d, cols],
                                               ALU.mult).then_inc(gated[0], 1)
                if b is not None:
                    for c in halves:
                        norm_scale(0, b, c)
                    pool.memset(xp[:, :, 0:PAD], 0.0).then_inc(pad_ready, 1)
                if r is not None:
                    for c in halves:
                        norm_scale(1, r, c)
                if b is not None:
                    ph.wait_mm(pool, ("T2" if r is not None else "T", DK - 1, NH - 1))
                    pool.sem_inc(passed, 1)
                    pool.memset(stage[:, :, :], 0.0).then_inc(y_zeroed, 1)
                if r is not None:
                    for n in (2, 3):
                        for c in halves:
                            norm_scale(n, r, c)
                if b is not None:
                    for job in steps[0:BATCH]:
                        _, d, c = job
                        ph.wait_taken(pool, job)
                        cols = slice(c * HALF, (c + 1) * HALF)
                        pool.tensor_tensor(dtu[:, d, cols], dt[:, d, cols], xc[:, d, cols],
                                           ALU.mult).then_inc(dtu_ready[0], 1)

            def loop(b, bp):
                def weigh(hf, it, par):
                    ex_a = ex_sets[0][3]
                    pool.wait_ge(wbc_loaded[1 - par], (bp * 2 * ITS + hf * ITS + it) * 16 + 16 * par)
                    pool.wait_ge(a_ready, state(bp, hf, it, par) + EX_CREDIT)
                    pool.tensor_tensor(ex_a, ex_a, wbc[:, 1 - par:2 - par, :].broadcast_to([P, 2, HALF]),
                                       ALU.mult).then_inc(aw_ready, 1)

                def body(hf, it, par, first):
                    if b is not None:
                        w = state(b, hf, it, par)
                        pool.wait_ge(b_loaded[par], (b * 2 * ITS + hf * ITS + it) * 16 + 16)
                        if hf == 0 and first:
                            pool.wait_ge(dtu_ready[0], b * BATCH + BATCH)
                    for d in range(CT):
                        if d == 2 and bp is not None and not (hf == 0 and first):
                            weigh(hf, it, par)
                        if d >= 1 and b is not None and hf == 0 and first:
                            pool.wait_ge(dtu_ready[1], b * (CT * NH - BATCH) + d)
                        if b is not None:
                            pool.wait_ge(hT_ready, (w + (-1 if d < 2 or bp is None else 0)) * TT + HT_READY_CREDIT)
                            pool.tensor_tensor(slot(par, d, bp is None), dtu[:, d, :], b_bcs[par], ALU.mult
                                               ).then_inc(dbu_ready, 1)

                if b is None:
                    return
                turns(pool, body)
                if bp is not None:
                    weigh(1, ITS, 0)

            over_rows(pool, phases, loop)

        @block.scalar
        def _(act):
            act.sem_inc(g_ready, 1)
            act.sem_inc(l_ready, 1)
            for dst, name in ((qwT, "qWT"), (cwT, "cWT"), (kwT, "kWT"), (vwT, "vWT"), (owT, "oWT")):
                act.dma_start(dst, t[name].rearrange("(k p) f -> p k f", p=P)).then_inc(w_fold, 16)
            act.dma_start(hwb[:, :, 0:D], t["hW"].rearrange("(k p) f -> p k f", p=P)).then_inc(w_fold, 16)
            act.dma_start(hwb[:, :, D:D + 1], t["hb"].rearrange("(k p o) -> p k o", p=P, o=1),
                          allow_slow_non_contiguous=True).then_inc(w_fold, 16)
            act.dma_start(ctxT, t["ctxT"].rearrange("(k p) f -> p k f", p=P)).then_inc(w_fold, 16)
            for i, name in enumerate(("qb", "cb", "kb", "vb")):
                act.dma_start(fbias[:, i, :], t[name].rearrange("(k p) -> p k", p=P),
                              allow_slow_non_contiguous=True).then_inc(w_fold, 16)
            act.dma_start(ob_row, t["ob"].rearrange("(a f) -> a f", a=1)).then_inc(w_fold, 16)

            def scale_weights():
                act.wait_ge(w_early, 4 * 16)
                act.activation(a_neg[:, :], a_log, ACT.Exp).then_inc(act_scaled, 1)
                act.wait_ge(act_scaled, 1)
                act.activation(a_neg[:, :], a_neg[:, :], ACT.Copy, scale=-1.0).then_inc(act_scaled, 1)
                act.activation(w_out[:, :, :], w_out[:, :, :], ACT.Copy, scale=0.5).then_inc(act_scaled, 1)

            def keep_folded(first, last_one):
                act.wait_ge(w_fold, (FOLD_LOADS + 1) * 16)
                for i in range(first, min(last_one, len(fold_jobs))):
                    what, k, c = fold_jobs[i]
                    bank = ps[:, (FOLD_BANK + i) % 8, :]
                    keys = slice(c * KCH, (c + 1) * KCH)
                    act.wait_ge(fold_ready, i + 1)
                    if what == "WQH":
                        act.activation(wqh[:, k, :], bank[:, 0:D], ACT.Copy)
                        last = act.activation(bq[:, k, :], bank[:, D:D + 1], ACT.Identity, bias=fbias[:, 0, k:k + 1])
                    elif what in "ckv":
                        dst = {"c": cT, "k": kT, "v": vT}[what]
                        last = act.activation(dst[:, k, keys], bank[:, 0:KCH], ACT.Identity,
                                              bias=fbias[:, 1 + "ckv".index(what), k:k + 1])
                    elif what == "KQ":
                        last = act.activation(kq_all[:, c * (B // 2):(c + 1) * (B // 2), k, :],
                                              bank[:, 0:KCH].rearrange("p (b f) -> p b f", b=B // 2), ACT.Copy)
                    elif what == "KROW":
                        last = act.activation(k_row[:, keys], bank[0:1, 0:KCH], ACT.Copy)
                    elif what == "WQO":
                        last = act.activation(w_qo[:, k, :], bank[:, 0:D], ACT.Copy)
                    elif what == "OROW":
                        last = act.activation(o_row[0:1, :], bank[0:1, 0:D], ACT.Copy)
                    else:
                        last = act.activation(vo_all[:, k * D:(k + 1) * D], bank[0:KEYS, 0:D], ACT.Copy)
                    last.then_inc(fold_kept, 1)

            def phases(ph):
                r, b = ph.c_row, ph.a_row

                def conv_in(d):
                    for c in halves:
                        ph.wait_mm(act, ("X", d, c))
                        act.activation(xp[:, d % 2, PAD + c * HALF:PAD + (c + 1) * HALF],
                                       ph.bank(("X", d, c)), ACT.Copy).then_inc(act_freed, 1)

                def silu_tanh(d):
                    act.wait_ge(conv_done, b * CT * KTAPS + (d + 1) * KTAPS)
                    act.activation(tanh[:, d % 2, :], xc[:, d, :], ACT.Tanh).then_inc(tanh_done, 1)

                def soft_exps(batch):
                    for i in batch:
                        act.wait_ge(cap_ready, b * CT * NH + i + 1)
                        act.activation(soft[:, i, :], soft[:, i, :], ACT.Exp).then_inc(soft_exp, 1)

                def soft_logs(batch):
                    for i in batch:
                        act.wait_ge(soft_exp, b * CT * NH + i + 1)
                        act.activation(soft[:, i, :], soft[:, i, :], ACT.Ln, bias=1.0).then_inc(soft_ready, 1)

                def keep_normed(kind, dst, c):
                    for job in tiles_of(kind, c):
                        ph.wait_mm(act, job)
                        act.activation(dst[:, job[1], c * HALF:(c + 1) * HALF], ph.bank(job), ACT.Copy
                                       ).then_inc(act_freed, 1)

                def score_exps(c):
                    act.wait_ge(negm_ready, r * NH + c + 1)
                    for job in tiles_of("Q", c):
                        a = job[1]
                        act.activation(probs[:, a, :], ph.bank(job)[:, 0:LK], ACT.Exp,
                                       scale=float(D) ** -0.5, bias=negm[:, a:a + 1], accum_out=rsum[:, a:a + 1]
                                       ).then_inc(act_freed, 1)

                if r is not None:
                    for c in halves:
                        for job in tiles_of("Z", c):
                            d = job[1]
                            ph.wait_mm(act, job)
                            act.activation(dt[:, d, c * HALF:(c + 1) * HALF], ph.bank(job), ACT.Tanh, scale=0.5
                                           ).then_inc(gate_tanh, 1)
                if b is not None:
                    for c in halves:
                        keep_normed("T", xnT, c)
                    conv_in(0)
                    conv_in(1)
                if r is not None:
                    for c in halves:
                        keep_normed("T2", xcT, c)
                        if b is None:
                            score_exps(c)
                if b is not None:
                    for d in (0, 1):
                        silu_tanh(d)
                        conv_in(d + 2)
                if r is not None:
                    if b is not None:
                        for c in halves:
                            score_exps(c)
                    for c in halves:
                        for job in tiles_of("PT", c):
                            ph.wait_mm(act, job)
                            act.activation(probsT[0:KEYS, job[1], c * HALF:(c + 1) * HALF],
                                           ph.bank(job)[0:KEYS, :], ACT.Copy).then_inc(act_freed, 1)
                if b is not None:
                    for d in (2, 3):
                        if r is None:
                            keep_folded((d - 2) * 8, (d - 1) * 8)
                        silu_tanh(d)
                    if r is None:
                        keep_folded(16, len(fold_jobs))
                        scale_weights()
                        act.wait_ge(fold_stored, 3 * 16)
                    for c in halves:
                        ph.wait_mm(act, ("B", 0, c))
                        act.activation(bc_sb[:, c * HALF:(c + 1) * HALF], ph.bank(("B", 0, c))[0:2 * N, :], ACT.Copy
                                       ).then_inc(act_freed, 1)
                if r is not None:
                    for a in range(TT):
                        act.wait_ge(x16_ready, r * TT + a + 1)
                        act.activation(square[:, a, :], xc16[:, a, :], ACT.Square, accum_out=ssq[:, a:a + 1]
                                       ).then_inc(ssq_ready, 1)
                if b is not None:
                    soft_exps(range(2))
                if r is not None:
                    for _, k, c in both("N"):
                        ph.wait_mm(act, ("N", k, c))
                        act.activation(nfT[:, k, c * HALF:(c + 1) * HALF],
                                       ph.bank(("N", k, c)).bitcast(BF16)[:, 0:HALF], ACT.Copy
                                       ).then_inc(act_freed, 1)
                if b is not None:
                    soft_exps(range(2, 3))
                if r is not None:
                    act.wait_ge(gap_ready, r + 1)
                    act.activation(tw[:, 1, :], tw[:, 0, :], ACT.Exp).then_inc(gap_exp, 1)
                if b is not None:
                    soft_exps(range(3, 5))
                if r is not None:
                    for c in halves:
                        ph.wait_mm(act, ("CT", 0, c))
                        act.activation(rows[32:32 + E, c * HALF:(c + 1) * HALF], ph.bank(("CT", 0, c))[0:E, :],
                                       ACT.Copy).then_inc(act_freed, 1)
                if b is not None:
                    soft_exps(range(5, BATCH))
                    soft_logs(range(BATCH))
                    soft_exps(range(BATCH, CT * NH))
                    soft_logs(range(BATCH, CT * NH))
                if b is None:
                    ph.wait_all_taken(act)
                else:
                    ph.wait_taken(act, steps[BATCH])
                    if r is not None:
                        wait_apart(act, x2_stored, b * 16)
                        wait_apart(act, x16_ready, b * TT)
                        wait_apart(act, b_stored, b * 16 + 16)

            def loop(b, bp):
                if bp is not None:
                    act.wait_ge(shift_set, 3)
                    act.wait_ge(dve_scaled, 5)
                back = 1 if b is not None else 2

                def body(hf, it, par):
                    def decay(d):
                        wait_apart(act, scan_done, state(b, hf, it, par) * CT + d - 1 + SCAN_CREDIT)
                        act.activation(decays[:, d % 2, :], dt[:, d, :], ACT.Exp,
                                       scale=a_neg[:, bass.ds(it * 2 + (d * N + hf * (N // 2) + par), 1)]
                                       ).then_inc(exp_ready, 1)

                    def gate_in(j):
                        if j == 0:
                            wait_apart(act, u_ready, s + 1 - back + EX_CREDIT)
                        wait_apart(act, p1_ready, s * 4 + (j * 2 + 1))
                        act.activation(ex_g[:, j, :], ps[:, 4, :], ACT.Relu, scale=-1.0,
                                       bias=bias1[:, bass.ds(col + j, 1)]).then_inc(g_ready, 1)

                    def linear_in(j):
                        if j == 0:
                            wait_apart(act, a_ready, s + 1 - back + EX_CREDIT)
                        wait_apart(act, p1_ready, s * 4 + (j * 2 + 2))
                        act.activation(ex_l[:, j, :], ps[:, 5, :], ACT.Relu, scale=-1.0,
                                       bias=bias1[:, bass.ds(col + (2 + j), 1)]).then_inc(l_ready, 1)

                    if b is not None:
                        decay(0)
                        decay(1)
                    if bp is not None:
                        ex_g, ex_t, ex_l, _ = ex_sets[par if b is None else 0]
                        s = state(bp, hf, it, par)
                        col = it * 8 + par * 4
                        for j in range(2):
                            gate_in(j)
                            linear_in(j)
                    head = it == 0 and par == 0
                    if b is not None and head:
                        decay(2)
                    if bp is not None:
                        wait_apart(act, g_ready, s * 2 + 3)
                        act.activation(ex_t, ex_g, ACT.Tanh, scale=-ALPHA / 2, bias=shift[:, 1:2]
                                       ).then_inc(t_ready, 1)
                    if bp is not None and b is not None:
                        wait_apart(act, t_ready, s + 1)
                        act.activation(ex_g, ex_g, ACT.Identity, bias=shift[:, 0:1]).then_inc(neg_ready, 1)
                    if b is not None:
                        decay(3 if head else 2)
                    if bp is not None and b is not None:
                        wait_apart(act, l_ready, s * 2 + 3)
                        act.activation(ex_l, ex_l, ACT.Relu, scale=-1.0, bias=shift[:, 2:3]
                                       ).then_inc(lin_ready, 1)
                    if b is not None and not head:
                        decay(3)

                with act.Fori(0, 2) as hf:
                    for it in range(ITS):
                        for par in range(2):
                            body(hf, it, par)

            over_rows(act, phases, loop)

        @block.vector
        def _(dve):
            links = {"a": 0, "c": 0}
            LINKS_A, LINKS_C = 4, 21

            def link(ph, kind, ins):
                row, per_row = (ph.a_row, LINKS_A) if kind == "a" else (ph.c_row, LINKS_C)
                n = links[kind] % per_row + 1
                links[kind] += 1
                ins.then_inc(chain[kind], 1)
                wait_apart(dve, chain[kind], row * per_row + n)

            dve.sem_inc(scan_done, SCAN_CREDIT)
            dve.sem_inc(hT_used, HT_CREDIT)
            dve.sem_inc(a_ready, EX_CREDIT)
            dve.sem_inc(u_ready, EX_CREDIT)
            dve.sem_inc(mix_taken, 1)

            def norm_stats(ph, n, src, c):
                kind, row = ("a", ph.a_row) if n == 0 else ("c", ph.c_row)
                tiles = range(c * TH, (c + 1) * TH)
                if n == 0:
                    dve.wait_ge(x_in[c], row * 16 + 16)
                for a in tiles:
                    ins = dve.bn_stats(stats[:, a, :], src[:, a, :])
                link(ph, kind, ins)
                for a in tiles:
                    ins = dve.bn_aggr(mv[:, a, :], stats[:, a, :])
                link(ph, kind, ins)
                dve.tensor_scalar(ve[:, c * TH:(c + 1) * TH], mv[:, c * TH:(c + 1) * TH, 1], EPS, None, ALU.add
                                  ).then_inc(ve_ready[n], 1)

            def norm_apply(ph, n, src, dst, done, c):
                dve.wait_ge(rstd_ready[n], (ph.a_row if n == 0 else ph.c_row) * NH + c + 1)
                for a in range(c * TH, (c + 1) * TH):
                    dve.tensor_scalar(dst[:, a, :], src[:, a, :], mv[:, a, 0:1], rstd[:, a:a + 1],
                                      ALU.subtract, ALU.mult).then_inc(done, 1)

            def phases(ph):
                r, b = ph.c_row, ph.a_row

                def convolve(d):
                    ph.wait_mm(dve, ("X", d, NH - 1))
                    ph.wait_taken(dve, ("X", d, NH - 1))
                    if d == 0:
                        dve.wait_ge(pad_ready, b + 1)
                    v, base = xc[:, d, :], b * CT * KTAPS + d * KTAPS
                    dve.tensor_scalar(v, xp[:, d % 2, 0:S], conv_w[:, d, 0:1], chan[:, 0, d:d + 1],
                                      ALU.mult, ALU.add).then_inc(conv_done, 1)
                    for k in range(1, KTAPS):
                        dve.wait_ge(conv_done, base + k)
                        dve.scalar_tensor_tensor(v, xp[:, d % 2, k:k + S], conv_w[:, d, k:k + 1], v,
                                                 ALU.mult, ALU.add).then_inc(conv_done, 1)

                def silu(d):
                    dve.wait_ge(tanh_done, b * CT + d + 1)
                    dve.scalar_tensor_tensor(xc[:, d, :], tanh[:, d % 2, :], 1.0, xc[:, d, :],
                                             ALU.add, ALU.mult).then_inc(xc_ready, 1)

                def cap(i):
                    ph.wait_mm(dve, steps[i])
                    dve.tensor_scalar(soft[:, i, :], ph.bank(steps[i]), chan[:, 1, i % CT:i % CT + 1], STEP_CAP,
                                      ALU.add, ALU.min).then_inc(cap_ready, 1)

                def step(i):
                    _, d, c = steps[i]
                    dve.wait_ge(soft_ready, b * CT * NH + i + 1)
                    dve.scalar_tensor_tensor(dt[:, d, c * HALF:(c + 1) * HALF], ph.bank(steps[i]),
                                             chan[:, 1, d:d + 1], soft[:, i, :],
                                             ALU.add, ALU.max).then_inc(dve_freed, 1)

                def add_to_stream(kind, c):
                    for job in tiles_of(kind, c):
                        a = job[1]
                        ph.wait_mm(dve, job)
                        dve.tensor_tensor(xt[:, a, :], xt[:, a, :], ph.bank(job)[:, 0:D], ALU.add
                                          ).then_inc(dve_freed, 1)
                    ph.wait_taken(dve, tiles_of(kind, c)[-1])

                def score_max(c):
                    tiles = slice(c * TH, (c + 1) * TH)
                    for job in tiles_of("Q", c):
                        ph.wait_mm(dve, job)
                        ins = dve.reduce_max(mx[:, job[1]:job[1] + 1], ph.bank(job)[:, 0:LK], AX_X)
                    link(ph, "c", ins)
                    dve.tensor_scalar(negm[:, tiles], mx[:, tiles], -(float(D) ** -0.5), None, ALU.mult
                                      ).then_inc(negm_ready, 1)

                def mean_square(c):
                    tiles = slice(c * TH, (c + 1) * TH)
                    dve.wait_ge(ssq_ready, r * TT + (c + 1) * TH)
                    dve.tensor_scalar(ve[:, tiles], ssq[:, tiles], 1.0 / D, EPS, ALU.mult, ALU.add
                                      ).then_inc(ve_ready[3], 1)

                def expert_input(c):
                    dve.wait_ge(rstd_ready[3], r * NH + c + 1)
                    for a in range(c * TH, (c + 1) * TH):
                        dve.scalar_tensor_tensor(nf[:, a, :], xc16[:, a, :], rstd[:, a:a + 1], norm_w[:, :],
                                                 ALU.mult, ALU.mult).then_inc(nf_ready, 1)

                if r is not None:
                    for c in halves:
                        cols = slice(c * HALF, (c + 1) * HALF)
                        for d in range(CT):
                            dve.wait_ge(gate_tanh, r * CT * NH + c * CT + d + 1)
                            dve.scalar_tensor_tensor(dt[:, d, cols], dt[:, d, cols], 1.0, ph.bank(("Z", d, c)),
                                                     ALU.add, ALU.mult).then_inc(dve_freed, 1)
                        for d in range(CT):
                            job = ("Y", d, c)
                            ph.wait_mm(dve, job)
                            dve.scalar_tensor_tensor(xc[:, d, cols], xc[:, d, cols], chan[:, 2, d:d + 1],
                                                     ph.bank(job), ALU.mult, ALU.add).then_inc(dve_freed, 1)
                        for d in range(CT // 2, CT):
                            ph.wait_taken(dve, ("Y", d, c))
                            dve.tensor_tensor(xc[:, d, cols], xc[:, d, cols], dt[:, d, cols],
                                              ALU.mult).then_inc(gated[1], 1)
                if b is not None:
                    for c in halves:
                        norm_stats(ph, 0, xn_a, c)
                    for c in halves:
                        norm_apply(ph, 0, xn_a, xn_a, xn_a_ready, c)
                if r is not None:
                    dve.wait_ge(xt_loaded, r * 32 + 32)
                    add_to_stream("O", 0)
                    norm_stats(ph, 1, xt, 0)
                    add_to_stream("O", 1)
                    norm_apply(ph, 1, xt, xn_c, xn_c_ready, 0)
                    norm_stats(ph, 1, xt, 1)
                    if b is None:
                        score_max(0)
                    norm_apply(ph, 1, xt, xn_c, xn_c_ready, 1)
                if b is not None:
                    if r is None:
                        dve.wait_ge(w_first, 5 * 16)
                        dve.tensor_scalar(conv_w[:, :, :], conv_w[:, :, :], 0.5, None, ALU.mult
                                          ).then_inc(dve_scaled, 1)
                        dve.tensor_scalar(chan[:, 0, :], chan[:, 0, :], 0.5, None, ALU.mult).then_inc(dve_scaled, 1)
                        dve.wait_ge(dve_scaled, 2)
                    for d in (0, 1):
                        convolve(d)
                    for d in (0, 1):
                        silu(d)
                if r is not None:
                    for c in halves if b is not None else (1,):
                        score_max(c)
                    for c in halves:
                        tiles = slice(c * TH, (c + 1) * TH)
                        ph.wait_taken(dve, ("Q", c * TH + TH - 1, 0))
                        link(ph, "c", dve.reciprocal(rinv[:, tiles], rsum[:, tiles]))
                        for a in range(TT)[tiles]:
                            dve.tensor_scalar(probs[:, a, :], probs[:, a, :], rinv[:, a:a + 1], None, ALU.mult
                                              ).then_inc(probs_ready, 1)
                if b is not None:
                    for d in (2, 3):
                        convolve(d)
                    for d in (2, 3):
                        silu(d)
                if r is not None:
                    add_to_stream("V", 0)
                    norm_stats(ph, 2, xt, 0)
                    add_to_stream("V", 1)
                    norm_apply(ph, 2, xt, xc16, x16_ready, 0)
                    norm_stats(ph, 2, xt, 1)
                    norm_apply(ph, 2, xt, xc16, x16_ready, 1)
                    mean_square(0)
                if b is not None:
                    if r is None:
                        dve.wait_ge(w_late, 7 * 16)
                        dve.tensor_scalar(w2[:, :], w2_raw, -0.5, None, ALU.mult).then_inc(dve_scaled, 1)
                        dve.tensor_copy(bias2[32:32 + E, :], bias2_raw[32:32 + E, :]).then_inc(dve_scaled, 1)
                        dve.tensor_scalar(bias1[:, :], bias1_raw[:, :], -1.0, LIMIT, ALU.mult, ALU.add
                                          ).then_inc(dve_scaled, 1)
                        dve.wait_ge(dve_scaled, 5)
                        dve.wait_ge(fold_stored, 3 * 16)
                    ph.wait_mm(dve, ("C", 0, 0))
                    dve.tensor_copy(c_tok[:, :, :],
                                    ph.bank(("C", 0, 0)).rearrange("p (a n) -> p a n", n=2 * N)[:, 0:TT, N:2 * N]
                                    ).then_inc(dve_freed, 1)
                if r is not None:
                    mean_square(1)
                    for c in halves:
                        expert_input(c)
                if b is not None:
                    for i in range(3):
                        cap(i)
                if r is not None:
                    route(ph)
                if b is not None:
                    for i in range(3, BATCH):
                        cap(i)
                    for i in range(CT * NH):
                        if BATCH <= i + 2 < CT * NH:
                            cap(i + 2)
                        step(i)
                        if i >= BATCH:
                            _, d, c = steps[i]
                            cols = slice(c * HALF, (c + 1) * HALF)
                            ph.wait_taken(dve, steps[i])
                            dve.tensor_tensor(dtu[:, d, cols], dt[:, d, cols], xc[:, d, cols], ALU.mult
                                              ).then_inc(dtu_ready[1], 1)
                    wait_apart(dve, y_zeroed, b + 1)

            def route(ph):
                r = ph.c_row
                ph.wait_mm(dve, ("G", 0, 0))
                dve.tensor_tensor(lg16[:, :, :], ph.bank(("G", 0, 0))[:, 0:TT * E].rearrange("p (a e) -> p a e", e=E),
                                  gate_b[:, :, :].broadcast_to([P, TT, E]), ALU.add).then_inc(dve_freed, 1)
                ph.wait_taken(dve, ("G", 0, 0))
                link(ph, "c", dve.tensor_copy(lg[:, :, :], lg16[:, :, :]))
                for a in range(TT):
                    ins = dve.max(m8[:, a, :], lg[:, a, :])
                link(ph, "c", ins)
                dve.tensor_tensor(tw[:, 0, :], m8[:, :, 1], m8[:, :, 0], ALU.subtract).then_inc(gap_ready, 1)
                for a in range(TT):
                    ins = dve.max_index(i8[:, a, :], m8[:, a, :], lg[:, a, :])
                link(ph, "c", ins)
                link(ph, "c", dve.tensor_copy(i8f[:, :, :], i8[:, :, :]))
                for n in range(2):
                    ins = dve.tensor_tensor(eq[:, n, :, :], iota[:, :, :].broadcast_to([P, TT, E]),
                                            i8f[:, :, n:n + 1].broadcast_to([P, TT, E]), ALU.is_equal)
                link(ph, "c", ins)
                dve.wait_ge(gap_exp, r + 1)
                link(ph, "c", dve.tensor_scalar(tden[:, :], tw[:, 1, :], 1.0, None, ALU.add))
                link(ph, "c", dve.reciprocal(tw[:, 2, :], tden[:, :]))
                link(ph, "c", dve.tensor_tensor(tw[:, 3, :], tw[:, 1, :], tw[:, 2, :], ALU.mult))
                for n in range(2):
                    ins = dve.tensor_tensor(eq[:, n, :, :], eq[:, n, :, :],
                                            tw[:, 2 + n, :].rearrange("p (a o) -> p a o", o=1).broadcast_to([P, TT, E]),
                                            ALU.mult)
                link(ph, "c", ins)
                dve.tensor_tensor(comb[:, :, :], eq[:, 0, :, :], eq[:, 1, :, :], ALU.add).then_inc(comb_ready, 1)
            def loop(b, bp):
                back = 1 if b is not None else 2

                def accumulate(hf, it, par, a):
                    w = state(b, hf, it, par) - 1
                    n = it * 2 + (hf * (N // 2) + par - 1)
                    dve.wait_ge(hT_ready, w * TT + (a + 1 + HT_READY_CREDIT))
                    dve.scalar_tensor_tensor(stage[:, a, :], ps[:, a % 4, :], c_tok[:, a, bass.ds(n, 1)],
                                             stage[:, a, :], ALU.mult, ALU.add).then_inc(hT_used, 1)

                def finalize(hf, part):
                    flat16 = xc16[:, hf * TH:(hf + 1) * TH, :].rearrange("p a d -> p (a d)")
                    flat = res[:, :, :].rearrange("p a d -> p (a d)")
                    first_half, last_half = slice(0, HALF), slice(HALF, 2 * HALF)
                    if part == 0:
                        dve.wait_ge(p2_ready, state(bp, hf, ITS - 1, 1) + 1 + EX_CREDIT)
                        dve.wait_ge(res_loaded, (bp * 2 + hf) * 16 + 16)
                        dve.tensor_copy(mix[:, first_half], ps[:, 6, :])
                    elif part == 1:
                        dve.tensor_copy(mix[:, last_half], ps[:, 7, :]).then_inc(mix_taken, 1)
                    elif part == 2:
                        dve.wait_ge(mix_taken, bp * 2 + hf + 2)
                        dve.tensor_tensor(mix[:, :], mix[:, :], flat16, ALU.add).then_inc(mix_added, 1)
                    elif part == 3:
                        dve.wait_ge(mix_added, bp * 2 + hf + 1)
                        dve.tensor_tensor(flat[:, first_half], mix[:, first_half], flat[:, first_half], ALU.add)
                    else:
                        dve.tensor_tensor(flat[:, last_half], mix[:, last_half], flat[:, last_half], ALU.add
                                          ).then_inc(out_ready, 1)

                def body(hf, it, par, first):
                    if b is not None:
                        w = state(b, hf, it, par)
                    if bp is not None:
                        s = state(bp, hf, it, par)
                        ex_g, ex_t, ex_l, ex_a = ex_sets[par if b is None else 0]
                    second = hf == 1 and isinstance(it, int) and par == 1
                    running = b is not None and not (hf == 0 and first)

                    def scan(d):
                        dve.wait_ge(exp_ready, w * CT + d + 1)
                        dve.wait_ge(dbu_ready, w * CT + d + 1 + DBU_CREDIT)
                        h = slot(par, d, bp is None)
                        dve.tensor_tensor_scan(h, decays[:, d % 2, :], h, 0.0,
                                               ALU.mult, ALU.add).then_inc(scan_done, 1)

                    if running:
                        if bp is None:
                            scan(0)
                        for a in range(4):
                            accumulate(hf, it, par, a)
                            if bp is not None and second and a < 3:
                                finalize(0, 2 + a)
                        if bp is not None:
                            scan(0)
                        scan(1)
                        accumulate(hf, it, par, 4)
                        accumulate(hf, it, par, 5)
                    elif b is not None:
                        for d in range(CT):
                            scan(d)
                    if bp is not None:
                        if b is None:
                            if second:
                                finalize(0, 0)
                                finalize(0, 1)
                            wait_apart(dve, t_ready, s + 1)
                            dve.tensor_scalar(ex_g, ex_g, LIMIT, None, ALU.subtract).then_inc(neg_ready, 1)
                            dve.wait_ge(l_ready, s * 2 + 3)
                            dve.tensor_scalar(ex_l, ex_l, 2 * LIMIT, -1.0, ALU.min, ALU.mult).then_inc(lin_ready, 1)
                        wait_apart(dve, neg_ready, s + 1)
                        dve.scalar_tensor_tensor(ex_t, ex_t, 1.0, ex_g, ALU.add, ALU.mult).then_inc(u_ready, 1)
                    if running:
                        scan(2)
                        scan(3)
                        if bp is not None and hf == 1 and first:
                            finalize(0, 0)
                            finalize(0, 1)
                        accumulate(hf, it, par, 6)
                        accumulate(hf, it, par, 7)
                    if bp is not None:
                        wait_apart(dve, p2_ready, s + 1 - back + EX_CREDIT)
                        wait_apart(dve, lin_ready, s + 1)
                        dve.wait_ge(u_ready, s + 1 + EX_CREDIT)
                        dve.scalar_tensor_tensor(ex_a, ex_l, 1.0 - LIMIT if b is not None else 1.0 + LIMIT, ex_t,
                                                 ALU.add, ALU.mult).then_inc(a_ready, 1)
                        if b is None:
                            dve.wait_ge(wbc_loaded[par], (bp * 2 * ITS + hf * ITS + it) * 16 + 16)
                            dve.wait_ge(a_ready, s + 1 + EX_CREDIT)
                            dve.tensor_tensor(ex_a, ex_a, wbc[:, par:par + 1, :].broadcast_to([P, 2, HALF]),
                                              ALU.mult).then_inc(aw_ready, 1)
                        if b is None and second:
                            for part in range(2, 5):
                                finalize(0, part)

                turns(dve, body)
                if b is not None:
                    for a in range(TT):
                        accumulate(1, ITS, 0, a)
                if bp is not None:
                    for part in range(5):
                        finalize(1, part)

            over_rows(dve, phases, loop)
            assert links == {"a": LINKS_A * 2, "c": LINKS_C * 2}

        @block.tensor
        def _(pe):
            pe.sem_inc(p2_ready, EX_CREDIT)
            pe.sem_inc(hT_ready, HT_READY_CREDIT)

            def fold(ph):
                pe.wait_ge(w_fold, (FOLD_LOADS + 1) * 16)
                pe.wait_ge(consts, 6)
                for i, (what, k, c) in enumerate(fold_jobs):
                    bank = ps[:, (FOLD_BANK + i) % 8, :]
                    cols = slice(k * P, (k + 1) * P)
                    keys = slice(c * KCH, (c + 1) * KCH)
                    need = {"WQH": 0, "c": 0, "k": fold_at(("c", 1, 1)), "v": fold_at(("k", 1, 1)),
                            "KQ": fold_at(("k", 1, 1)), "KROW": fold_at(("k", 1, 1)), "WQO": fold_at(("WQH", 1, 0)),
                            "OROW": fold_at(("WQH", 1, 0)), "VO": fold_at(("OROW", 0, 0))}[what]
                    need = max(need, i - 7)
                    if i < 8:
                        ph.wait_taken(pe, ph.jobs[FOLD_BANK + i - 8])
                    if need:
                        pe.wait_ge(fold_kept, need)
                    pairs = {"WQH": lambda: [(qwT[:, q, cols], hwb[:, q, :]) for q in range(DK)],
                             "c": lambda: [(cwT[:, q, cols], ctxT[:, q, keys]) for q in range(DK)],
                             "k": lambda: [(kwT[:, q, cols], cT[:, q, keys]) for q in range(DK)],
                             "v": lambda: [(vwT[:, q, cols], cT[:, q, keys]) for q in range(DK)],
                             "KQ": lambda: [(wqh[:, q, cols], kT[:, q, keys]) for q in range(DK)],
                             "KROW": lambda: [(bq[:, q, :], kT[:, q, keys]) for q in range(DK)],
                             "WQO": lambda: [(wqh[:, q, cols], owT[:, q, :]) for q in range(DK)],
                             "OROW": lambda: [(bq[:, q, :], owT[:, q, :]) for q in range(DK)] + [(ones[0:1, 0:1], ob_row)],
                             "VO": lambda: [(vT[:, q, k * KEYS:(k + 1) * KEYS], owT[:, q, :]) for q in range(DK)]
                                   + [(ones[0:1, 0:KEYS], o_row[0:1, :])]}[what]()
                    for n, (left, right) in enumerate(pairs):
                        dst = bank[0:left.shape[1], 0:right.shape[1]]
                        mm = pe.matmul(dst, left, right, start=(n == 0), stop=(n == len(pairs) - 1))
                    mm.then_inc(fold_ready, 1)

            def product(bank, pairs):
                for n, (left, right) in enumerate(pairs):
                    mm = pe.matmul(bank, left, right, start=(n == 0), stop=(n == len(pairs) - 1))
                return mm

            def transposes(ph, job, src, idn):
                _, k, c = job
                ph.wait_bank(pe, job)
                for a in range(TH):
                    mm = pe.transpose(ph.bank(job)[:, a * P:(a + 1) * P], src[:, c * TH + a, k * P:(k + 1) * P],
                                      idn[:, :])
                mm.then_inc(mm_ready, 1)

            def phases(ph):
                r, b = ph.c_row, ph.a_row
                if r is None:
                    pe.wait_ge(consts, 6)
                for job in ph.jobs:
                    {"Z": job_z, "Y": job_y, "O": job_o, "T": job_t, "X": job_x, "T2": job_t2, "Q": job_q,
                     "PT": job_pt, "V": job_v, "B": job_b, "C": job_c, "S": job_s, "N": job_n, "G": job_g,
                     "CT": job_ct}[job[0]](ph, r, b, job)
                if b is not None:
                    ph.wait_taken(pe, ("B", 0, NH - 1) if r is None else ("CT", 0, NH - 1))
                    ph.wait_taken(pe, steps[5])

            def job_z(ph, r, b, job):
                _, d, c = job
                ph.wait_bank(pe, job)
                if c == 0:
                    pe.wait_ge(hT_used, r * (N * TT) + (N * TT - CT + d + 1 + HT_CREDIT))
                product(ph.bank(job), [(w_in[:, k, DI + d * P:DI + (d + 1) * P], xnT[:, k, c * HALF:(c + 1) * HALF])
                                       for k in range(DK)]).then_inc(mm_ready, 1)

            def job_y(ph, r, b, job):
                if job == ("Y", 2, 0):
                    pe.wait_ge(mix_taken, r * 2 + 1)
                transposes(ph, job, stage, ident)

            def job_o(ph, r, b, job):
                a = job[1]
                ph.wait_bank(pe, job)
                if a == 0:
                    pe.wait_ge(act_scaled, 3)
                pe.wait_ge(w_out_loaded, r * 16 + 16)
                for count in gated:
                    pe.wait_ge(count, r * CT + (a // TH + 1) * (CT // 2))
                product(ph.bank(job)[:, 0:D], [(xc[:, d, a * P:(a + 1) * P], w_out[:, d, :])
                                               for d in range(CT)]).then_inc(mm_ready, 1)

            def job_t(ph, r, b, job):
                pe.wait_ge(xn_a_ready, b * TT + (job[2] + 1) * TH)
                transposes(ph, job, xn_a, ident)

            def job_x(ph, r, b, job):
                _, d, c = job
                if r is None:
                    pe.wait_ge(w_first, 5 * 16)
                ph.wait_bank(pe, job)
                ph.wait_taken(pe, ("T", DK - 1, c))
                product(ph.bank(job), [(w_in[:, k, d * P:(d + 1) * P], xnT[:, k, c * HALF:(c + 1) * HALF])
                                       for k in range(DK)]).then_inc(mm_ready, 1)

            def job_t2(ph, r, b, job):
                pe.wait_ge(xn_c_ready, r * TT + (job[2] + 1) * TH)
                transposes(ph, job, xn_c, ident)

            def job_q(ph, r, b, job):
                a = job[1]
                pe.wait_ge(kv_loaded, r * 48 + 48)
                ph.wait_bank(pe, job)
                ph.wait_taken(pe, ("T2", DK - 1, a // TH))
                dst = ph.bank(job)[:, 0:LK]
                for k in range(DK):
                    pe.matmul(dst, xcT[:, k, a * P:(a + 1) * P], kq[:, k, :], start=(k == 0), stop=False)
                pe.matmul(dst, ones[0:1, :], rows[0:1, 0:LK], start=False, stop=True).then_inc(mm_ready, 1)

            def job_pt(ph, r, b, job):
                _, k, c = job
                pe.wait_ge(probs_ready, r * TT + (c + 1) * TH)
                ph.wait_bank(pe, job)
                for a in range(TH):
                    mm = pe.transpose(ph.bank(job)[0:KEYS, a * P:(a + 1) * P],
                                      probs[:, c * TH + a, k * KEYS:(k + 1) * KEYS], ident[:, :])
                mm.then_inc(mm_ready, 1)

            def job_v(ph, r, b, job):
                a = job[1]
                ph.wait_bank(pe, job)
                ph.wait_taken(pe, ("PT", 1, a // TH))
                tok = slice(a * P, (a + 1) * P)
                dst = ph.bank(job)[:, 0:D]
                for k in range(DK):
                    pe.matmul(dst, xcT[:, k, tok], w_qo[:, k, :], start=(k == 0), stop=False)
                for k in range(2):
                    mm = pe.matmul(dst, probsT[0:KEYS, k, tok], vo[:, k, :], start=False, stop=(k == 1))
                mm.then_inc(mm_ready, 1)

            def job_b(ph, r, b, job):
                c = job[2]
                if r is None and c == 0:
                    fold(ph)
                    pe.wait_ge(fold_kept, len(fold_jobs))
                if r is None:
                    pe.wait_ge(w_early, 4 * 16)
                ph.wait_bank(pe, job)
                pe.wait_ge(xc_ready, b * CT + CT)
                product(ph.bank(job)[0:2 * N, :], [(w_x[:, d, :], xc[:, d, c * HALF:(c + 1) * HALF])
                                                   for d in range(CT)]).then_inc(mm_ready, 1)

            def job_c(ph, r, b, job):
                ph.wait_bank(pe, job)
                ph.wait_taken(pe, ("B", 0, NH - 1))
                pe.sem_inc(passed, 1)
                for a in range(TT):
                    mm = pe.transpose(ph.bank(job)[:, a * 2 * N:(a + 1) * 2 * N], bc_sb[:, a * P:(a + 1) * P],
                                      ident[0:2 * N, 0:2 * N])
                mm.then_inc(mm_ready, 1)

            def job_s(ph, r, b, job):
                _, d, c = job
                ph.wait_bank(pe, job)
                product(ph.bank(job), [(w_dt[:, k, d * P:(d + 1) * P], xc[:, k, c * HALF:(c + 1) * HALF])
                                       for k in range(CT)]).then_inc(mm_ready, 1)

            def job_n(ph, r, b, job):
                _, k, c = job
                pe.wait_ge(nf_ready, r * TT + (c + 1) * TH)
                ph.wait_bank(pe, job)
                bank = ph.bank(job).bitcast(BF16)
                for a in range(TH):
                    mm = pe.transpose(bank[:, a * P:(a + 1) * P], nf[:, c * TH + a, k * P:(k + 1) * P],
                                      ident16[:, :])
                mm.then_inc(mm_ready, 1)

            def job_g(ph, r, b, job):
                pe.wait_ge(w_late, 7 * 16)
                ph.wait_bank(pe, job)
                ph.wait_taken(pe, ("N", DK - 1, NH - 1))
                for a in range(TT):
                    mm = product(ph.bank(job)[:, a * E:(a + 1) * E],
                                 [(nfT[:, k, a * P:(a + 1) * P], gate_w[:, k, :]) for k in range(DK)])
                mm.then_inc(mm_ready, 1)

            def job_ct(ph, r, b, job):
                c = job[2]
                if b is None and c == 0:
                    up_products(r, 0, 0, 0, 0)
                pe.wait_ge(comb_ready, r + 1)
                ph.wait_bank(pe, job)
                for a in range(TH):
                    mm = pe.transpose(ph.bank(job)[0:E, a * P:(a + 1) * P], comb[:, c * TH + a, :], ident[:, :])
                mm.then_inc(mm_ready, 1)

            def up_products(bp, hf, it, par, j):
                n = state(bp, hf, it, par) * 2 + j
                wcol = (it * 2 + par) * (DK * 2 * I) + j * P
                for g, taken in ((0, g_ready), (1, l_ready)):
                    pe.wait_ge(taken, n + 1)
                    for k in range(DK):
                        mm = pe.matmul(ps[:, 4 + g, :], w1[:, bass.ds(wcol + (k * 2 * I + g * I), P)],
                                       nfT[:, k, hf * HALF:(hf + 1) * HALF], start=(k == 0), stop=(k == DK - 1))
                    mm.then_inc(p1_ready, 1)

            def loop(b, bp):
                if bp is not None:
                    pe.wait_ge(dve_scaled, 5)

                def transpose_states(w, par, tiles):
                    pe.wait_ge(scan_done, w * CT + CT + SCAN_CREDIT)
                    for a in tiles:
                        pe.wait_ge(hT_used, w * TT + (a + 1))
                        for d in range(CT):
                            mm = pe.transpose(ps[:, a % 4, d * P:(d + 1) * P],
                                              slot(par, d, bp is None)[:, a * P:(a + 1) * P], ident[:, :])
                        mm.then_inc(hT_ready, 1)

                def bias_product(hf):
                    pe.wait_ge(mix_taken, bp * 2 + hf + 1)
                    if b is None and hf == 0:
                        phase_between(B).wait_taken(pe, ("CT", 0, NH - 1))
                    for a in range(TH):
                        tok = slice((hf * TH + a) * P, (hf * TH + a + 1) * P)
                        pe.matmul(ps[:, 6 + a // 2, (a % 2) * D:(a % 2 + 1) * D], rows[32:32 + E, tok],
                                  bias2[32:32 + E, :], start=(a % 2 == 0), stop=True, skip_group_check=True)

                def down_products(s, par, col, tiles=(0, 1)):
                    ex_a = ex_sets[par if b is None else 0][3]
                    for j in tiles:
                        if j == 0:
                            pe.wait_ge(aw_ready, s + 1 + EX_CREDIT)
                        for a in range(TH):
                            mm = pe.matmul(ps[:, 6 + a // 2, (a % 2) * D:(a % 2 + 1) * D],
                                           ex_a[:, j, a * P:(a + 1) * P], w2[:, bass.ds(col + j * D, D)],
                                           start=False, stop=True, skip_group_check=True)
                        if j == 1:
                            mm.then_inc(p2_ready, 1)

                lag = 1 if b is not None else 2

                def body(hf, it, par, first):
                    running = b is not None and not (hf == 0 and first)
                    early = b is None and hf == 0 and first
                    if bp is not None and not early:
                        up_products(bp, hf, it, par, 0)

                    def down(tiles):
                        s = state(bp, hf, it, par)
                        if not isinstance(it, int) or par >= lag:
                            down_products(s - lag, (par - lag) % 2, it * (4 * D) + (par - lag) * 2 * D, tiles)
                        elif hf == 1:
                            down_products(s - lag, (par - lag) % 2, (E + par - lag) * 2 * D, tiles)

                    if b is None:
                        down((0,))
                    if running:
                        transpose_states(state(b, hf, it, par) - 1, 1 - par, range(4))
                    if bp is not None and b is not None and hf == 1 and isinstance(it, int) and par == 1:
                        bias_product(hf)
                    if bp is not None:
                        up_products(bp, hf, it, par, 1)
                        if hf == 0 and first:
                            if b is not None:
                                phase_between(b).wait_taken(pe, steps[-1])
                            bias_product(hf)
                    if running:
                        transpose_states(state(b, hf, it, par) - 1, 1 - par, range(4, TT))
                    if bp is not None:
                        down((0, 1) if b is not None else (1,))
                        if b is None and hf == 1 and isinstance(it, int) and par == 1:
                            bias_product(hf)

                turns(pe, body)
                if b is not None:
                    transpose_states(state(b, 1, ITS - 1, 1), 1, range(TT))
                if bp is not None:
                    for back in range(lag, 0, -1):
                        down_products(state(bp, 1, ITS - 1, 1) + 1 - back, (2 - back) % 2, (E - back) * 2 * D)

            over_rows(pe, phases, loop)


def kernel(**inputs):
    import concourse.bacc as bacc
    import numpy as np
    from concourse.bass_utils import run_bass_kernel_spmd

    v = {name: np.asarray(a) for name, a in inputs.items()}
    attn, cross, ffn = "L0_attn_", "L0_xattn_", "L0_ffn_"
    E, I2, D = v[ffn + "mlp1_weight"].shape
    w1 = v[ffn + "mlp1_weight"].reshape(E, I2 // 2, 2, D).transpose(0, 3, 2, 1).reshape(E, D, I2)
    b1 = v[ffn + "mlp1_bias"].reshape(E, I2 // 256, 128, 2).transpose(2, 0, 3, 1).reshape(128, E * I2 // 128)
    laid = {
        "x": v["x"], "ctxT": v["ctx_1024"].transpose(2, 0, 1).reshape(D, -1),
        "W_in": v[attn + "W_in"], "conv_w": v[attn + "conv_w"], "conv_b": v[attn + "conv_b"],
        "W_x": v[attn + "W_x"], "W_dt": v[attn + "W_dt"], "b_dt": v[attn + "b_dt"],
        "A_log": v[attn + "A_log"], "D_skip": v[attn + "D"], "W_out": v[attn + "W_out"],
        "hW": v[cross + "hW"], "qWT": v[cross + "qW"].T, "cWT": v[cross + "cW"].T, "kWT": v[cross + "kW"].T,
        "vWT": v[cross + "vW"].T, "oWT": v[cross + "oW"].T,
        "hb": v[cross + "hb"], "qb": v[cross + "qb"], "cb": v[cross + "cb"], "kb": v[cross + "kb"],
        "vb": v[cross + "vb"], "ob": v[cross + "ob"],
        "norm_w": v[ffn + "norm_weight"], "gate_wT": v[ffn + "gate_weight"].T,
        "gate_b": v[ffn + "gate_bias"].reshape(1, E), "mlp1_wT": w1, "mlp1_bT": b1,
        "mlp2_wT": v[ffn + "mlp2_weight"].transpose(0, 2, 1), "mlp2_b": v[ffn + "mlp2_bias"],
    }
    laid = {name: np.ascontiguousarray(a) for name, a in laid.items()}
    nc = bacc.Bacc("TRN2", target_bir_lowering=False, num_devices=1)
    t = {name: nc.dram_tensor(f"in_{name}", a.shape, mybir.dt.from_np(a.dtype), kind="ExternalInput").ap()
         for name, a in laid.items()}
    out = nc.dram_tensor("out_x", v["x"].shape, F32, kind="ExternalOutput").ap()
    decoder_layer(nc, t, out)
    r = run_bass_kernel_spmd(nc, [{f"in_{name}": a for name, a in laid.items()}], core_ids=[0])
    return r.results[0]["out_x"]
```
